# Optimizing a Trainium2 kernel written in Bass

```python
import numpy as np
import jax
import jax.numpy as jnp

def _softmax(x, axis=-1):
    return jax.nn.softmax(x, axis=axis)

def _gelu(x):
    return jax.nn.gelu(x, approximate=True)

def _silu(x):
    return jax.nn.silu(x)

def _sigmoid(x):
    return jax.nn.sigmoid(x)

def _layernorm(x, axis=-1, eps=1e-05):
    m = jnp.mean(x, axis=axis, keepdims=True)
    v = jnp.var(x, axis=axis, keepdims=True)
    return (x - m) / jnp.sqrt(v + eps)

def _scatter_add(tgt, idx, src, axis=0):
    return tgt.at[idx].add(src)

def _segment_sum(src, seg, n):
    return jax.ops.segment_sum(src, seg, n)
kernel_name = 'mk_gnn_preln_d4_gnn_r8_bb0fb2'

def setup_inputs(seed: int=0):
    np.random.seed(seed)
    _w = jnp.asarray

    def _rec_inputs():
        import jax
        import jax.numpy as jnp
        _gk = jax.random.key(seed)
        x = -0.000202 + 1 * jax.random.normal(jax.random.fold_in(_gk, 1), (6250, 128), jnp.float32)
        src = jax.random.randint(jax.random.fold_in(_gk, 2), (100000,), 0, 6250, jnp.int32)
        dst = jax.random.randint(jax.random.fold_in(_gk, 3), (100000,), 0, 6250, jnp.int32)
        _o = jnp.argsort(dst, stable=True)
        src = src[_o]
        dst = dst[_o]
        edge_attr_128 = -6.47781e-05 + 0.999943 * jax.random.normal(jax.random.fold_in(_gk, 12), (100000, 128), jnp.float32)
        return (x, src, dst, edge_attr_128)
    x, src, dst, edge_attr_128 = _rec_inputs()

    def _L0_gnn_setup():
        import jax, jax.numpy as jnp
        import numpy as np
        NEG_SLOPE = 0.2
        key = jax.random.key(seed)
        k1, k2, k3, k4, k5, k6 = jax.random.split(key, 6)
        N, E, IN, OUT = (6250, 100000, 128, 128)
        x = jax.random.normal(k1, (N, IN), dtype=jnp.float32)
        edge_index = jax.random.randint(k2, (2, E), 0, N, dtype=jnp.int64)
        W = jax.random.normal(k3, (IN, OUT), dtype=jnp.float32) / np.sqrt(IN)
        att_src = jax.random.normal(k4, (OUT,), dtype=jnp.float32) / np.sqrt(OUT)
        att_dst = jax.random.normal(k5, (OUT,), dtype=jnp.float32) / np.sqrt(OUT)
        bias = jnp.zeros((OUT,), dtype=jnp.float32)
        return {'x': x, 'edge_index': edge_index, 'W': W, 'att_src': att_src, 'att_dst': att_dst, 'bias': bias}
    _L0_gnn_all = _L0_gnn_setup()
    _L0_gnn_in = {k: v for k, v in _L0_gnn_all.items() if k in ('W', 'att_src', 'att_dst', 'bias')}
    del _L0_gnn_all

    def _L1_gnn_setup():
        import jax, jax.numpy as jnp
        import numpy as np
        N, D_IN, D_HID, H, D_OUT, E = (2500, 128, 128, 4, 128, 40000)
        LN_EPS = 1e-05
        key = jax.random.key(seed)
        ks = jax.random.split(key, 10)
        x = jax.random.normal(ks[0], (N, D_IN), dtype=jnp.float32)
        edge_index = jax.random.randint(ks[1], (2, E), 0, N, dtype=jnp.int32)
        Wq = jax.random.normal(ks[2], (H, D_HID, D_IN), dtype=jnp.float32) / np.sqrt(D_IN)
        Wk = jax.random.normal(ks[3], (H, D_HID, D_IN), dtype=jnp.float32) / np.sqrt(D_IN)
        FINAL = D_HID * H
        gamma = jnp.ones((FINAL,), dtype=jnp.float32)
        beta = jnp.zeros((FINAL,), dtype=jnp.float32)
        Wr = jax.random.normal(ks[4], (FINAL, D_IN), dtype=jnp.float32) / np.sqrt(D_IN)
        br = jnp.zeros((FINAL,), dtype=jnp.float32)
        Wo = jax.random.normal(ks[5], (D_OUT, FINAL), dtype=jnp.float32) / np.sqrt(FINAL)
        bo = jnp.zeros((D_OUT,), dtype=jnp.float32)
        return {'x': x, 'edge_index': edge_index, 'Wq': Wq, 'Wk': Wk, 'gamma': gamma, 'beta': beta, 'Wr': Wr, 'br': br, 'Wo': Wo, 'bo': bo}
    _L1_gnn_all = _L1_gnn_setup()
    _L1_gnn_in = {k: v for k, v in _L1_gnn_all.items() if k in ('Wq', 'Wk', 'gamma', 'beta', 'Wr', 'br', 'Wo', 'bo')}
    del _L1_gnn_all

    def _L2_gnn_setup():
        import jax, jax.numpy as jnp
        import numpy as np
        LOG2 = float(np.log(2.0))

        def ssp(x):
            return jax.nn.softplus(x) - LOG2

        def linear(x, W, b):
            return x @ W.T + b
        N, E, H, F = (12500, 200000, 128, 128)
        key = jax.random.key(seed)
        ks = jax.random.split(key, 14)
        s = 1.0 / np.sqrt(H)
        inp = {'h': jax.random.normal(ks[0], (N, H), dtype=jnp.float32), 'e': jax.random.normal(ks[1], (E, F), dtype=jnp.float32), 'W_node': jax.random.uniform(ks[2], (H, H), minval=-s, maxval=s), 'b_node': jax.random.uniform(ks[3], (H,), minval=-s, maxval=s), 'W_e1': jax.random.uniform(ks[4], (H, F), minval=-s, maxval=s), 'b_e1': jax.random.uniform(ks[5], (H,), minval=-s, maxval=s), 'W_e2': jax.random.uniform(ks[6], (H, H), minval=-s, maxval=s), 'b_e2': jax.random.uniform(ks[7], (H,), minval=-s, maxval=s), 'W_fc1': jax.random.uniform(ks[8], (H, H), minval=-s, maxval=s), 'b_fc1': jax.random.uniform(ks[9], (H,), minval=-s, maxval=s), 'W_fc2': jax.random.uniform(ks[10], (H, H), minval=-s, maxval=s), 'b_fc2': jax.random.uniform(ks[11], (H,), minval=-s, maxval=s), 'src': jax.random.randint(ks[12], (E,), 0, N, dtype=jnp.int32), 'dst': jax.random.randint(ks[13], (E,), 0, N, dtype=jnp.int32)}
        return inp
    _L2_gnn_all = _L2_gnn_setup()
    _L2_gnn_in = {k: v for k, v in _L2_gnn_all.items() if k in ('W_node', 'b_node', 'W_e1', 'b_e1', 'W_e2', 'b_e2', 'W_fc1', 'b_fc1', 'W_fc2', 'b_fc2')}
    del _L2_gnn_all

    def _L3_gnn_setup():
        import jax, jax.numpy as jnp
        import numpy as np
        N_NODES = 6250
        N_EDGES = 100000
        D_IN = 128
        D_HID = 256
        EPS = 0.0
        key = jax.random.key(seed)
        k1, k2, k3, k4 = jax.random.split(key, 4)
        x = jax.random.normal(k1, (N_NODES, D_IN), dtype=jnp.float32)
        edge_index = jax.random.randint(k2, (2, N_EDGES), 0, N_NODES, dtype=jnp.int64)
        W1 = jax.random.normal(k3, (D_IN, D_HID), dtype=jnp.float32) * (1.0 / np.sqrt(D_IN))
        b1 = jnp.zeros((D_HID,), dtype=jnp.float32)
        W2 = jax.random.normal(k4, (D_HID, D_IN), dtype=jnp.float32) * (1.0 / np.sqrt(D_HID))
        b2 = jnp.zeros((D_IN,), dtype=jnp.float32)
        return {'x': x, 'edge_index': edge_index, 'W1': W1, 'b1': b1, 'W2': W2, 'b2': b2}
    _L3_gnn_all = _L3_gnn_setup()
    _L3_gnn_in = {k: v for k, v in _L3_gnn_all.items() if k in ('W1', 'b1', 'W2', 'b2')}
    del _L3_gnn_all
    return {'x': x, 'src': src, 'dst': dst, 'edge_attr_128': edge_attr_128, 'L0_gnn_W': _L0_gnn_in['W'], 'L0_gnn_att_src': _L0_gnn_in['att_src'], 'L0_gnn_att_dst': _L0_gnn_in['att_dst'], 'L0_gnn_bias': _L0_gnn_in['bias'], 'L1_gnn_Wq': _L1_gnn_in['Wq'], 'L1_gnn_Wk': _L1_gnn_in['Wk'], 'L1_gnn_gamma': _L1_gnn_in['gamma'], 'L1_gnn_beta': _L1_gnn_in['beta'], 'L1_gnn_Wr': _L1_gnn_in['Wr'], 'L1_gnn_br': _L1_gnn_in['br'], 'L1_gnn_Wo': _L1_gnn_in['Wo'], 'L1_gnn_bo': _L1_gnn_in['bo'], 'L2_gnn_W_node': _L2_gnn_in['W_node'], 'L2_gnn_b_node': _L2_gnn_in['b_node'], 'L2_gnn_W_e1': _L2_gnn_in['W_e1'], 'L2_gnn_b_e1': _L2_gnn_in['b_e1'], 'L2_gnn_W_e2': _L2_gnn_in['W_e2'], 'L2_gnn_b_e2': _L2_gnn_in['b_e2'], 'L2_gnn_W_fc1': _L2_gnn_in['W_fc1'], 'L2_gnn_b_fc1': _L2_gnn_in['b_fc1'], 'L2_gnn_W_fc2': _L2_gnn_in['W_fc2'], 'L2_gnn_b_fc2': _L2_gnn_in['b_fc2'], 'L3_gnn_W1': _L3_gnn_in['W1'], 'L3_gnn_b1': _L3_gnn_in['b1'], 'L3_gnn_W2': _L3_gnn_in['W2'], 'L3_gnn_b2': _L3_gnn_in['b2']}

def reference(x, src, dst, edge_attr_128, L0_gnn_W, L0_gnn_att_src, L0_gnn_att_dst, L0_gnn_bias, L1_gnn_Wq, L1_gnn_Wk, L1_gnn_gamma, L1_gnn_beta, L1_gnn_Wr, L1_gnn_br, L1_gnn_Wo, L1_gnn_bo, L2_gnn_W_node, L2_gnn_b_node, L2_gnn_W_e1, L2_gnn_b_e1, L2_gnn_W_e2, L2_gnn_b_e2, L2_gnn_W_fc1, L2_gnn_b_fc1, L2_gnn_W_fc2, L2_gnn_b_fc2, L3_gnn_W1, L3_gnn_b1, L3_gnn_W2, L3_gnn_b2):
    import jax
    import jax.numpy as jnp

    def _L0_gnn_ref(x, edge_index, W, att_src, att_dst, bias):
        import jax, jax.numpy as jnp
        import numpy as np
        NEG_SLOPE = 0.2
        N = x.shape[0]
        loop = jnp.arange(N, dtype=edge_index.dtype)
        src = jnp.concatenate([edge_index[0], loop])
        dst = jnp.concatenate([edge_index[1], loop])
        h = x @ W
        a_s = h @ att_src
        a_d = h @ att_dst
        e = jax.nn.leaky_relu(a_s[src] + a_d[dst], NEG_SLOPE)
        m = jax.ops.segment_max(e, dst, num_segments=N)
        p = jnp.exp(e - m[dst])
        denom = jax.ops.segment_sum(p, dst, num_segments=N)
        alpha = p / denom[dst]
        out = jax.ops.segment_sum(h[src] * alpha[:, None], dst, num_segments=N)
        return out + bias

    def _L1_gnn_ref(x, edge_index, Wq, Wk, gamma, beta, Wr, br, Wo, bo):
        import jax, jax.numpy as jnp
        import numpy as np
        N, D_IN, D_HID, H, D_OUT, E = (2500, 128, 128, 4, 128, 40000)
        LN_EPS = 1e-05
        n = x.shape[0]
        scale = jnp.sqrt(jnp.asarray(Wq.shape[1], dtype=x.dtype))
        row, col = (edge_index[0], edge_index[1])
        Q = jnp.einsum('nd,hed->hne', x, Wq)
        K = jnp.einsum('nd,hed->hne', x, Wk)
        Qr = Q[:, row]
        logits = (Qr * K[:, col]).sum(-1) / scale
        alpha = jax.nn.softmax(logits, axis=1)
        msg = Qr * alpha[..., None]
        agg = jax.vmap(lambda m: jax.ops.segment_sum(m, col, num_segments=n))(msg)
        heads = agg + x[None]
        h = jnp.transpose(heads, (1, 0, 2)).reshape(n, -1)
        mu = h.mean(-1, keepdims=True)
        var = ((h - mu) ** 2).mean(-1, keepdims=True)
        hn = (h - mu) * jax.lax.rsqrt(var + LN_EPS) * gamma + beta
        hs = hn * jax.nn.sigmoid(hn)
        res = x @ Wr.T + br
        return (hs + res) @ Wo.T + bo

    def _L2_gnn_ref(h, e, W_node, b_node, W_e1, b_e1, W_e2, b_e2, W_fc1, b_fc1, W_fc2, b_fc2, src, dst):
        import jax, jax.numpy as jnp
        import numpy as np
        LOG2 = float(np.log(2.0))

        def ssp(x):
            return jax.nn.softplus(x) - LOG2

        def linear(x, W, b):
            return x @ W.T + b
        N = h.shape[0]
        hn = linear(h, W_node, b_node)
        ef = ssp(linear(e, W_e1, b_e1))
        ef = ssp(linear(ef, W_e2, b_e2))
        m = hn[src] * ef
        agg = jax.ops.segment_sum(m, dst, num_segments=N)
        out = ssp(linear(agg, W_fc1, b_fc1))
        out = linear(out, W_fc2, b_fc2)
        return out

    def _L3_gnn_ref(x, edge_index, W1, b1, W2, b2):
        import jax, jax.numpy as jnp
        import numpy as np
        N_NODES = 6250
        N_EDGES = 100000
        D_IN = 128
        D_HID = 256
        EPS = 0.0
        src = edge_index[0]
        dst = edge_index[1]
        agg = jax.ops.segment_sum(x[src], dst, num_segments=x.shape[0])
        h = (1.0 + EPS) * x + agg
        h = jnp.maximum(h @ W1 + b1, 0.0)
        return h @ W2 + b2
    edge_index = jnp.stack([src, dst])
    h = jnp.maximum(_layernorm(x, axis=-1), 0.0)
    x = x + _L0_gnn_ref(h, edge_index, L0_gnn_W, L0_gnn_att_src, L0_gnn_att_dst, L0_gnn_bias)
    h = jnp.maximum(_layernorm(x, axis=-1), 0.0)
    x = x + _L1_gnn_ref(h, edge_index, L1_gnn_Wq, L1_gnn_Wk, L1_gnn_gamma, L1_gnn_beta, L1_gnn_Wr, L1_gnn_br, L1_gnn_Wo, L1_gnn_bo)
    h = jnp.maximum(_layernorm(x, axis=-1), 0.0)
    x = x + _L2_gnn_ref(h, edge_attr_128, L2_gnn_W_node, L2_gnn_b_node, L2_gnn_W_e1, L2_gnn_b_e1, L2_gnn_W_e2, L2_gnn_b_e2, L2_gnn_W_fc1, L2_gnn_b_fc1, L2_gnn_W_fc2, L2_gnn_b_fc2, src, dst)
    h = jnp.maximum(_layernorm(x, axis=-1), 0.0)
    x = x + _L3_gnn_ref(h, edge_index, L3_gnn_W1, L3_gnn_b1, L3_gnn_W2, L3_gnn_b2)
    return x

_drawn_inputs = setup_inputs


def setup_inputs(seed=0):
    import zlib

    import numpy as np

    out = dict(_drawn_inputs(seed))
    spreads = {'L0_gnn_bias': (0.0, 0.1),
     'L1_gnn_gamma': (1.0, 0.2),
     'L1_gnn_beta': (0.0, 0.31),
     'L1_gnn_br': (0.0, 0.1),
     'L1_gnn_bo': (0.0, 0.1),
     'L3_gnn_b1': (0.0, 2.0),
     'L3_gnn_b2': (0.0, 2.0)}
    factors = {'edge_attr_128': 7.748,
     'L0_gnn_att_dst': 25.575,
     'L1_gnn_Wq': 62.425,
     'L1_gnn_Wk': 56.599,
     'L2_gnn_W_node': 3.709,
     'L2_gnn_b_node': 8.0,
     'L2_gnn_W_e1': 7.8,
     'L2_gnn_b_e1': 39.921,
     'L2_gnn_W_e2': 4.267,
     'L2_gnn_b_e2': 29.24,
     'L2_gnn_W_fc1': 3.135,
     'L2_gnn_b_fc1': 32.456,
     'L2_gnn_b_fc2': 8.0,
     'L3_gnn_W1': 4.335,
     'L3_gnn_W2': 3.058}
    for name, (base, spread) in spreads.items():
        noise = np.random.default_rng([zlib.crc32(name.encode()), seed]).standard_normal(out[name].shape)
        drawn = base * np.exp(spread * noise) if base else spread * noise
        out[name] = jnp.asarray(drawn.astype(out[name].dtype))
    for name, factor in factors.items():
        out[name] = (out[name] * factor).astype(out[name].dtype)
    return out
```

```python
from contextlib import ExitStack

import numpy as np

import concourse.bass as bass
from concourse import mybir

P = 128
C = 8
W_NARROW = 32
W_WIDE = 128
CW = 256
G4 = 4
GN = G4 * P
HEADS = 4
BIG = 1.0e30
START = -1.0e29
EPS = 1e-5
SLOPE = 0.2
LOG2 = float(np.log(2.0))

F32 = mybir.dt.float32
BF16 = mybir.dt.bfloat16
I32 = mybir.dt.int32
ALU = mybir.AluOpType
ACT = mybir.ActivationFunctionType
AX = mybir.AxisListType
ENG = mybir.EngineType
ds = bass.ds


def padded(n_nodes, n_edges):
    nodes = -(-(n_nodes + CW) // GN) * GN
    tiles = -(-n_edges // (P * 2 * C)) * 2 * C
    return nodes, tiles


class Names:
    pass


class Chain:

    def __init__(self, eng, sem, before=0):
        self.eng, self.sem, self.before, self.n = eng, sem, before, 0

    def add(self, ins):
        ins.then_inc(self.sem, 1)
        self.n += 1
        return ins

    def wait(self):
        self.eng.wait_ge(self.sem, self.before + self.n)

    def step(self, ins):
        self.add(ins)
        self.wait()

    def close(self, count):
        self.wait()
        assert self.n == count, (self.n, count)


def over(ap, shape):
    return ap.unsqueeze(2).to_broadcast(shape)


def new_semaphore(nc, m, name):
    semaphore = nc.alloc_semaphore(name)
    m.semaphores.append(semaphore)
    return semaphore


def clear_semaphores(nc, m):
    nc.clear_and_free_semaphores(m.semaphores)
    nc.all_engine_barrier()
    m.semaphores = []


def setup_phase(nc, k, m):
    T, NP, N = k.T, k.NP, k.N
    with ExitStack() as ctx:
        sb = lambda n, s, d: ctx.enter_context(nc.sbuf_tensor(n, s, d))
        sem = lambda n: new_semaphore(nc, m, n)
        dst_i = sb("su_dst", [P, T], I32)
        first_i = sb("su_first", [P, T], I32)
        last_i = sb("su_last", [1, T], I32)
        hi_i = sb("su_hi", [P, T], I32)
        hi_b = sb("su_hib", [P, T], BF16)
        lo_i = sb("su_lo", [P, T], I32)
        span = sb("su_span", [1, 2, T], F32)
        most = sb("su_most", [1, 4], F32)
        loaded = sem("su_loaded")
        hi_ready = sem("su_hi_ready")
        iotas = sem("su_iotas")
        chain = sem("su_chain")
        stored = sem("su_stored")
        pool_chain = sem("su_pool")
        with nc.Block() as block:
            @block.sync
            def _(sp):
                sp.dma_start(dst_i[:], k.dram["dst_tl"]).then_inc(loaded, 16)
                sp.dma_start(first_i[:], k.dram["dst_first"].partition_broadcast(P)).then_inc(loaded, 16)
                sp.dma_start(last_i[:], k.dram["dst_last"].unsqueeze(0)).then_inc(loaded, 16)
                sp.dma_start(hi_i[:], k.dram["src_el_t"]).then_inc(loaded, 16)
                sp.dma_start(lo_i[:], k.dram["src_el"]).then_inc(loaded, 16)
                sp.dma_start(m.src_idx[:], k.dram["src_tl"]).then_inc(loaded, 16)
                sp.wait_ge(hi_ready, 1)
                sp.dma_start(k.dram["hi_dram"].rearrange("(p t) -> p t", p=P), hi_b[:]).then_inc(stored, 16)
                sp.wait_ge(stored, 16)
                sp.wait_ge(loaded, 96)

            @block.gpsimd
            def _(pool):
                ch = Chain(pool, pool_chain)
                ch.add(pool.iota(m.iota_i[:], [[1, P]], base=0, channel_multiplier=0))
                ch.add(pool.iota(m.part_i[:], [[0, 1]], base=0, channel_multiplier=1))
                ch.step(pool.memset(m.ident[:], 0.0))
                ch.step(pool.affine_select(out=m.ident[:], in_=m.ident[:], compare_op=ALU.not_equal, fill=1.0,
                                           base=0, pattern=[[-1, P]], channel_multiplier=1))
                ch.step(pool.memset(m.eps[:], EPS))
                pool.memset(m.ones[:], 1.0).then_inc(iotas, 1)

            @block.vector
            def _(v):
                ch = Chain(v, chain)
                v.wait_ge(loaded, 96)
                ch.step(v.tensor_scalar(hi_i[:], hi_i[:], 7, None, ALU.logical_shift_right))
                v.tensor_copy(hi_b[:], hi_i[:]).then_inc(hi_ready, 1)
                ch.step(v.tensor_scalar(lo_i[:], lo_i[:], P - 1, None, ALU.bitwise_and))
                ch.add(v.tensor_copy(m.src_lo[:], lo_i[:]))
                ch.add(v.tensor_copy(m.dst_f[:], dst_i[:]))
                ch.step(v.tensor_copy(m.base_f[:], first_i[:]))
                ch.step(v.tensor_scalar(m.base_f[:], m.base_f[:], float(N - 1), None, ALU.min))
                ch.add(v.tensor_tensor(m.loc_f[:], m.dst_f[:], m.base_f[:], ALU.subtract))
                ch.add(v.tensor_copy(m.base_i[:], m.base_f[0:1, :]))
                ch.step(v.tensor_copy(span[:, 0, :], last_i[:]))
                ch.step(v.tensor_scalar(span[:, 0, :], span[:, 0, :], float(N - 1), None, ALU.min))
                ch.step(v.tensor_tensor(span[:, 0, :], span[:, 0, :], m.base_f[0:1, :], ALU.subtract))
                ch.step(v.tensor_reduce(most[:, 0:1], span[:, 0, :], AX.X, ALU.max))
                first_of = m.base_f[0:1, :].rearrange("p (c t) -> p c t", t=C)
                ch.step(v.tensor_tensor(span[:, 1, :].rearrange("p (c t) -> p c t", t=C), first_of,
                                        first_of[:, :, 0:1].to_broadcast([1, T // C, C]), ALU.subtract))
                ch.add(v.tensor_copy(m.rel_i[:], span[:, 1, :]))
                ch.step(v.tensor_reduce(most[:, 1:2], span[:, 1, :], AX.X, ALU.max))
                ch.add(v.tensor_scalar(most[:, 2:3], most[:, 0:1], float(W_NARROW - 1), None, ALU.is_le))
                ch.step(v.tensor_scalar(most[:, 3:4], most[:, 1:2], float(CW - W_NARROW), None, ALU.is_le))
                ch.step(v.tensor_tensor(most[:, 0:1], most[:, 2:3], most[:, 3:4], ALU.mult))
                ch.step(v.tensor_copy(m.narrow_i[:], most[:, 0:1]))
                v.wait_ge(pool_chain, 2)
                ch.add(v.tensor_copy(m.iota_f[:], m.iota_i[:]))
                ch.add(v.tensor_copy(m.iota_w[:], m.iota_i[:]))
                ch.add(v.tensor_copy(m.part_f[:], m.part_i[:]))
                ch.wait()
                v.wait_ge(iotas, 1)


def mean_and_var(v, ch, stats, mv, count):
    mean, var = mv[:, :, 0], mv[:, :, 1]
    ch.step(v.tensor_tensor(var, stats[:, :, 1], stats[:, :, 4], ALU.subtract))
    ch.step(v.scalar_tensor_tensor(var, var, count / 4.0, var, ALU.mult, ALU.mult))
    ch.step(v.tensor_tensor(var, var, stats[:, :, 2], ALU.add))
    ch.step(v.tensor_tensor(var, var, stats[:, :, 5], ALU.add))
    ch.add(v.tensor_tensor(mean, stats[:, :, 1], stats[:, :, 4], ALU.add))
    ch.wait()
    ch.add(v.tensor_scalar(mean, mean, 0.5, None, ALU.mult))
    ch.step(v.tensor_scalar(var, var, 1.0 / count, None, ALU.mult))


def norm_phase(nc, k, m, name, table=None):
    NB, NG = k.NB, k.NG
    with ExitStack() as ctx:
        sb = lambda n, s, d: ctx.enter_context(nc.sbuf_tensor(name + n, s, d))
        sem = lambda n: new_semaphore(nc, m, name + n)
        stats = sb("stats", [P, NB, 6], F32)
        mv = sb("mv", [P, NB, 2], F32)
        rstd = sb("rstd", [P, NB], F32)
        shift = sb("shift", [P, NB], F32)
        h = [sb(f"h{b}", [P, 2, P], F32) for b in range(2)]
        t_ps = [ctx.enter_context(nc.psum_tensor(f"{name}t_ps{b}", [P, 512], F32)) for b in range(2)]
        chain, var_ready, std_ready, shift_ready = sem("chain"), sem("var_ready"), sem("std_ready"), sem("shift_ready")
        h_ready, h_read, t_ready, t_free = sem("h_ready"), sem("h_read"), sem("t_ready"), sem("t_free")
        stored = [sem(f"stored{b}") for b in range(2)]
        with nc.Block() as block:
            @block.vector
            def _(v):
                with v.Fori(0, NG) as g:
                    for b in range(G4):
                        v.bn_stats(stats[:, ds(g * G4 + b, 1), :], m.x[:, ds(g * G4 + b, 1), :]).then_inc(chain, 1)
                ch = Chain(v, chain, NG * G4)
                ch.wait()
                mean_and_var(v, ch, stats[:], mv[:], P)
                v.sem_inc(var_ready, 1)
                v.wait_ge(std_ready, 1)
                ch.step(v.reciprocal(rstd[:], rstd[:]))
                v.scalar_tensor_tensor(shift[:], mv[:, :, 0], -1.0, rstd[:], ALU.mult, ALU.mult).then_inc(shift_ready, 1)
                with v.Fori(0, NG) as g:
                    for b in range(2):
                        v.wait_ge(t_ready, g * 2 + b + 1)
                        v.tensor_copy(m.hT[:, ds(g * GN + b * 2 * P, 2 * P)], t_ps[b][:, 0:2 * P]).then_inc(t_free, 1)

            @block.scalar
            def _(act):
                act.wait_ge(var_ready, 1)
                act.activation(rstd[:], mv[:, :, 1], ACT.Sqrt, bias=m.eps[:]).then_inc(std_ready, 1)
                act.wait_ge(shift_ready, 1)
                act.sem_inc(h_read, 2)
                if table is not None:
                    for b in range(2):
                        act.sem_inc(stored[b], 16)
                with act.Fori(0, NG) as g:
                    for b in range(2):
                        act.wait_ge(h_read, g * 2 + b + 1)
                        if table is not None:
                            act.wait_ge(stored[b], g * 16 + 16)
                        for q in range(2):
                            block_no = g * G4 + b * 2 + q
                            act.activation(h[b][:, q, :], m.x[:, ds(block_no, 1), :].rearrange("p a d -> p (a d)"),
                                           ACT.Relu, bias=shift[:, ds(block_no, 1)],
                                           scale=rstd[:, ds(block_no, 1)]).then_inc(h_ready, 1)

            @block.tensor
            def _(pe):
                pe.sem_inc(t_free, 2)
                with pe.Fori(0, NG) as g:
                    for b in range(2):
                        pe.wait_ge(h_ready, g * 4 + 2 * b + 2)
                        pe.wait_ge(t_free, g * 2 + b + 1)
                        pe.transpose(t_ps[b][:, 0:P], h[b][:, 0, :], m.ident[:])
                        pe.transpose(t_ps[b][:, P:2 * P], h[b][:, 1, :], m.ident[:]).then_inc(t_ready, 1)
                        pe.wait_ge(t_ready, g * 2 + b + 1)
                        pe.sem_inc(h_read, 1)

            @block.sync
            def _(sp):
                if table is None:
                    return
                with sp.Fori(0, NG) as g:
                    for b in range(2):
                        sp.wait_ge(h_ready, g * 4 + 2 * b + 2)
                        sp.dma_start(table.rearrange("(n p) d -> p n d", p=P)[:, ds(g * G4 + b * 2, 2), :],
                                     h[b][:]).then_inc(stored[b], 16)
                for b in range(2):
                    sp.wait_ge(stored[b], 16 * (NG + 1))


def attention_tables_phase(nc, k, m, ad):
    NG, NB = k.NG, k.NB
    with ExitStack() as ctx:
        sb = lambda n, s, d: ctx.enter_context(nc.sbuf_tensor("at_" + n, s, d))
        sem = lambda n: new_semaphore(nc, m, "at_" + n)
        ps = lambda n: ctx.enter_context(nc.psum_tensor("at_" + n, [P, 512], F32))
        wT = sb("wT", [P, P], F32)
        att = sb("att", [P, 2], F32)
        row = sb("row", [1, k.NP], F32)
        a = sb("a", [NB, P], F32)
        part = sb("part", [NB, P], F32)
        w_ps, s_ps, d_ps = ps("w_ps"), [ps(f"s_ps{b}") for b in range(1)], ps("d_ps")
        loaded, w_ready, rep_ready, rows_ready = sem("loaded"), sem("w_ready"), sem("rep_ready"), sem("rows_ready")
        copied, moved, chain = sem("copied"), sem("moved"), sem("chain")
        with nc.Block() as block:
            @block.sync
            def _(sp):
                sp.dma_start(wT[:], k.dram["W0T"]).then_inc(loaded, 16)
                sp.dma_start(att[:, 0:1], k.dram["att_src"].unsqueeze(1)).then_inc(loaded, 16)
                sp.dma_start(att[:, 1:2], k.dram["att_dst"].unsqueeze(1)).then_inc(loaded, 16)
                sp.wait_ge(copied, 2 * NG + 2)
                sp.dma_start(k.dram["as_dram"].unsqueeze(0), row[:]).then_inc(moved, 16)
                sp.wait_ge(moved, 16)
                sp.dma_start(a[:], k.dram["as_dram"].rearrange("(b n) -> b n", n=P)).then_inc(moved, 16)
                sp.wait_ge(moved, 32)

            @block.tensor
            def _(pe):
                pe.wait_ge(loaded, 48)
                pe.matmul(w_ps[:, 0:2], wT[:], att[:], start=True, stop=True).then_inc(w_ready, 1)
                pe.wait_ge(rep_ready, 2)
                pe.sem_inc(copied, 2)
                with pe.Fori(0, NG) as g:
                    pe.wait_ge(copied, 2 * g + 2)
                    pe.matmul(s_ps[0][:], m.ws_rep[:], m.hT[:, ds(g * GN, GN)], start=True, stop=True)
                    pe.matmul(d_ps[:], m.wd_rep[:], m.hT[:, ds(g * GN, GN)], start=True,
                              stop=True).then_inc(rows_ready, 1)

            @block.vector
            def _(v):
                v.wait_ge(w_ready, 1)
                v.tensor_scalar(m.ws_rep[:], m.ones[:], w_ps[:, 0:1], None, ALU.mult).then_inc(rep_ready, 1)
                v.tensor_scalar(m.wd_rep[:], m.ones[:], w_ps[:, 1:2], None, ALU.mult).then_inc(rep_ready, 1)
                with v.Fori(0, NG) as g:
                    v.wait_ge(rows_ready, g + 1)
                    v.tensor_copy(row[:, ds(g * GN, GN)], s_ps[0][0:1, :]).then_inc(copied, 1)
                    v.tensor_copy(ad[:, ds(g * GN, GN)], d_ps[:]).then_inc(copied, 1)
                v.wait_ge(moved, 32)
                ch = Chain(v, chain)
                ch.step(v.tensor_copy(m.as_part[:, 0, :], a[:]))
                ch.step(v.tensor_tensor(a[:], a[:], m.as_part[:, 0, :], ALU.subtract))
                ch.step(v.tensor_copy(m.as_part[:, 1, :], a[:]))
                ch.step(v.tensor_tensor(a[:], a[:], m.as_part[:, 1, :], ALU.subtract))
                ch.step(v.tensor_copy(m.as_part[:, 2, :], a[:]))


def lookup_phase(nc, k, m, s_el):
    NB, T = k.NB, k.T
    L = 8
    with ExitStack() as ctx:
        sb = lambda n, s, d: ctx.enter_context(nc.sbuf_tensor("lu_" + n, s, d))
        sem = lambda n: new_semaphore(nc, m, "lu_" + n)
        hi = [sb(f"hi{b}", [NB, L * P], BF16) for b in range(2)]
        onehot = [sb(f"onehot{b}", [NB, L * P], BF16) for b in range(2)]
        picked = [sb(f"picked{b}", [P, L], F32) for b in range(2)]
        masked = sb("masked", [P, L, P], F32)
        lo = [sb(f"lo{b}", [P, L], F32) for b in range(2)]
        block_ps = [ctx.enter_context(nc.psum_tensor(f"lu_ps{b}", [P, L * P], F32)) for b in range(2)]
        hi_ready, hi_free = [sem(f"hi_ready{b}") for b in range(2)], sem("hi_free")
        onehot_ready, onehot_free, block_ready, block_free = (sem(n) for n in ("oh_ready", "oh_free", "b_ready", "b_free"))
        picks, kept, lo_ready = sem("picks"), sem("kept"), sem("lo_ready")
        hi_rows = k.dram["hi_dram"].partition_broadcast(NB)
        steps = T // L
        with nc.Block() as block:
            @block.sync
            def _(sp):
                with sp.Fori(0, steps // 2) as i:
                    for b in range(2):
                        sp.wait_ge(hi_free, 2 * i + b + 1)
                        sp.dma_start(hi[b][:], hi_rows[:, ds((2 * i + b) * L * P, L * P)]).then_inc(hi_ready[b], 16)

            @block.vector
            def _(v):
                v.sem_inc(hi_free, 2)
                def make(i, b):
                    v.wait_ge(hi_ready[b], 16 * i + 16)
                    v.wait_ge(onehot_free, 2 * i + b + 1)
                    v.tensor_scalar(onehot[b][:], hi[b][:], m.part_f[0:NB, :], None, ALU.is_equal).then_inc(onehot_ready, 1)
                    v.wait_ge(onehot_ready, 2 * i + b + 1)
                    v.sem_inc(hi_free, 1)

                def pick(i, b):
                    c = 2 * i + b
                    v.tensor_copy(lo[b][:], m.src_lo[:, ds(c * L, L)]).then_inc(lo_ready, 1)
                    v.wait_ge(block_ready, c + 1)
                    v.wait_ge(lo_ready, c + 1)
                    for q in range(L):
                        v.scalar_tensor_tensor(masked[:, q, :], m.iota_f[:], lo[b][:, q:q + 1],
                                               block_ps[b][:, q * P:(q + 1) * P], ALU.is_equal, ALU.mult,
                                               accum_out=picked[b][:, q:q + 1]).then_inc(picks, 1)
                    v.wait_ge(picks, L * c + L)
                    v.tensor_copy(s_el[:, ds(c * L, L)], picked[b][:]).then_inc(kept, 1)
                    v.sem_inc(block_free, 1)
                    v.wait_ge(kept, c + 1)

                make(0, 0)
                with v.Fori(0, steps // 2 - 1) as i:
                    make(i, 1)
                    pick(i, 0)
                    make(i + 1, 0)
                    pick(i, 1)
                make(steps // 2 - 1, 1)
                pick(steps // 2 - 1, 0)
                pick(steps // 2 - 1, 1)

            @block.tensor
            def _(pe):
                pe.sem_inc(onehot_free, 2)
                pe.sem_inc(block_free, 2)
                with pe.Fori(0, steps // 2) as i:
                    for b in range(2):
                        c = 2 * i + b
                        pe.wait_ge(onehot_ready, c + 1)
                        pe.wait_ge(block_free, c + 1)
                        for q in range(L):
                            for part in range(3):
                                ins = pe.matmul(block_ps[b][:, q * P:(q + 1) * P], onehot[b][:, q * P:(q + 1) * P],
                                                m.as_part[:, part, :], start=(part == 0), stop=(part == 2))
                        ins.then_inc(block_ready, 1)
                        pe.wait_ge(block_ready, c + 1)
                        pe.sem_inc(onehot_free, 1)


def segment_max_phase(nc, k, m, s_el):
    T = k.T
    TB = -(-T // P)
    with ExitStack() as ctx:
        sb = lambda n, s, d: ctx.enter_context(nc.sbuf_tensor("sg_" + n, s, d))
        sem = lambda n: new_semaphore(nc, m, "sg_" + n)
        here_i = sb("here_i", [P, T], I32)
        other_i = sb("other_i", [P, 2, T], I32)
        here = sb("here", [P, T], F32)
        other = sb("other", [P, 2, T], F32)
        bars = sb("bars", [P, 2, T], F32)
        run = sb("run", [P, T], F32)
        ends = sb("ends", [P, T], F32)
        most = sb("most", [P, T], F32)
        col = sb("col", [P, 2], F32)
        line = sb("line", [1, 3, P + 1], F32)
        carry = sb("carry", [P, 1], F32)
        rows = [sb(f"rows{n}", [P, P], F32) for n in range(2)]
        line_ps = ctx.enter_context(nc.psum_tensor("sg_line_ps", [P, 512], F32))
        t_ps = [ctx.enter_context(nc.psum_tensor(f"sg_t_ps{b}", [P, 512], F32)) for b in range(2)]
        loaded, chain, cols_ready, lines_ready = sem("loaded"), sem("chain"), sem("cols_ready"), sem("lines_ready")
        carry_out, carry_in, scanned, stored = sem("carry_out"), sem("carry_in"), sem("scanned"), sem("stored")
        row_loaded = [sem(f"row_loaded{b}") for b in range(2)]
        turned, taken = sem("turned"), sem("taken")
        moves = [(n, tb) for n in range(3) for tb in range(TB)]
        with nc.Block() as block:
            @block.sync
            def _(sp):
                sp.dma_start(here_i[:], k.dram["dst_el"]).then_inc(loaded, 16)
                sp.dma_start(other_i[:, 0, :], k.dram["dst_before"]).then_inc(loaded, 16)
                sp.dma_start(other_i[:, 1, :], k.dram["dst_after"]).then_inc(loaded, 16)
                sp.wait_ge(scanned, 1)
                for n, t in enumerate((s_el, most, ends)):
                    sp.dma_start(k.dram["el_dram"][n].rearrange("(p t) -> p t", p=P), t[:]).then_inc(stored, 16)
                sp.wait_ge(stored, 48)
                for i, (n, tb) in enumerate(moves):
                    nt = min(P, T - tb * P)
                    if i >= 2:
                        sp.wait_ge(turned, i - 1)
                    sp.dma_start(rows[i % 2][0:nt, :], k.dram["el_dram"][n].rearrange("(t p) -> t p", p=P)[tb * P:tb * P + nt, :]
                                 ).then_inc(row_loaded[i % 2], 16)

            @block.tensor
            def _(pe):
                for n in range(2):
                    pe.wait_ge(cols_ready, n + 1)
                    pe.matmul(line_ps[0:1, 0:P], col[:, 0:1], m.ident[:], start=True, stop=True)
                    pe.matmul(line_ps[0:1, P:2 * P], col[:, 1:2], m.ident[:], start=True, stop=True
                              ).then_inc(lines_ready, 1)
                    pe.wait_ge(carry_out, n + 1)
                    c0 = 0 if n == 0 else 1
                    pe.matmul(line_ps[:, 2 * P:2 * P + 1], line[:, 2, c0:c0 + P], m.ones[0:1, 0:1], start=True, stop=True
                              ).then_inc(carry_in, 1)
                for i, (n, tb) in enumerate(moves):
                    nt = min(P, T - tb * P)
                    pe.wait_ge(row_loaded[i % 2], 16 * (i // 2 + 1))
                    if i >= 2:
                        pe.wait_ge(taken, i - 1)
                    pe.transpose(t_ps[i % 2][:, 0:nt], rows[i % 2][0:nt, :], m.ident[0:nt, 0:nt]).then_inc(turned, 1)

            @block.vector
            def _(v):
                ch = Chain(v, chain)
                v.wait_ge(loaded, 48)
                ch.add(v.tensor_copy(here[:], here_i[:]))
                ch.step(v.tensor_copy(other[:], other_i[:]))
                for n in range(2):
                    ch.step(v.tensor_tensor(other[:, n, :], other[:, n, :], here[:], ALU.not_equal))
                    ch.step(v.tensor_scalar(bars[:, n, :], other[:, n, :], -BIG, None, ALU.mult))
                for n in range(2):
                    back = slice(None, None, -1) if n else slice(None)
                    data = (s_el, run)[n]
                    out = (run, most)[n]
                    ch.step(v.tensor_tensor_scan(out[:, back], bars[:, n, back], data[:, back], -BIG, ALU.add, ALU.max))
                    edge = 0 if n else T - 1
                    ch.add(v.tensor_copy(col[:, 0:1], out[:, edge:edge + 1]))
                    ch.add(v.tensor_reduce(col[:, 1:2], bars[:, n, :], AX.X, ALU.min))
                    ch.wait()
                    v.sem_inc(cols_ready, 1)
                    v.wait_ge(lines_ready, n + 1)
                    ch.add(v.memset(line[:, 2, :], -BIG))
                    ch.step(v.tensor_copy(line[:, 0:2, 0:P], line_ps[0:1, 0:2 * P].rearrange("p (a b) -> p a b", a=2)))
                    to = line[:, 2, P - 1::-1] if n else line[:, 2, 1:P + 1]
                    ch.step(v.tensor_tensor_scan(to, line[:, 1, P - 1::-1] if n else line[:, 1, 0:P],
                                                 line[:, 0, P - 1::-1] if n else line[:, 0, 0:P], -BIG, ALU.add, ALU.max))
                    v.sem_inc(carry_out, 1)
                    v.wait_ge(carry_in, n + 1)
                    ch.step(v.tensor_copy(carry[:], line_ps[:, 2 * P:2 * P + 1]))
                    ch.step(v.tensor_tensor_scan(out[:, back], bars[:, n, back], data[:, back], carry[:], ALU.add, ALU.max))
                ch.step(v.tensor_tensor(ends[:], most[:], other[:, 1, :], ALU.mult))
                v.sem_inc(scanned, 1)
                for i, (n, tb) in enumerate(moves):
                    nt = min(P, T - tb * P)
                    v.wait_ge(turned, i + 1)
                    v.tensor_copy(m.tl[:, n, tb * P:tb * P + nt], t_ps[i % 2][:, 0:nt]).then_inc(taken, 1)
                v.wait_ge(taken, len(moves))
def over_chunks(eng, k, wide, body):
    half = k.NC // 2
    if not wide:
        with eng.Fori(0, half) as i:
            for b in range(2):
                body(2 * i + b, 2 * i + b, None, i, b)
    else:
        with eng.Fori(0, k.NW) as w:
            with eng.Fori(0, half) as i:
                for b in range(2):
                    body(w * k.NC + 2 * i + b, 2 * i + b, w, w * half + i, b)


def over_chunks_lagged(eng, k, wide, first, second, per_window=None):
    half = k.NC // 2

    def run(w, n0, i0):
        at = lambda i, b: (n0 + 2 * i + b, 2 * i + b, w, i0 + i, b)
        first(*at(0, 0))
        with eng.Fori(0, half - 1) as i:
            first(*at(i, 1))
            second(*at(i, 0))
            first(*at(i + 1, 0))
            second(*at(i, 1))
        first(*at(half - 1, 1))
        second(*at(half - 1, 0))
        second(*at(half - 1, 1))

    if not wide:
        run(None, 0, 0)
    else:
        with eng.Fori(0, k.NW) as w:
            run(w, w * k.NC, w * half)
            per_window(w)


def both_paths(eng, m, path):
    narrow = eng.value_load(m.narrow_i[:], min_val=0, max_val=1)
    with eng.If(narrow != 0):
        path(False)
    with eng.Else():
        path(True)


def bases_of(eng, nc, k, table, chunk, w, most=None):
    if w is not None:
        return [w * W_WIDE] * C
    _, values = nc.values_load_multi_w_load_instructions(
        table[0:1, ds(chunk * C, C)], engines=(eng.engine,), min_val=0, max_val=k.N - 1 if most is None else most,
        skip_runtime_bounds_check_because="setup_phase bounds the bases, and takes this path only where the others fit")
    return values


def gather_program(pool, k, m, s, table, wide):
    def chunk_rows(n, chunk, w, i, b):
        pool.wait_ge(s.rows_free, n + 1)
        pool.tensor_copy(s.idx[b][:], m.src_idx[:, ds(chunk * C, C)]).then_inc(s.idx_ready, 1)
        pool.wait_ge(s.idx_ready, n + 1)
        pool.sem_inc(s.idx_seen, 1)
        for t in range(C):
            pool.indirect_dma_start(s.rows[b][:, t, :], None, table,
                                    bass.IndirectOffsetOnAxis(ap=s.idx[b][:, t:t + 1], axis=0)
                                    ).then_inc(s.gathered[b], 16)
    over_chunks(pool, k, wide, chunk_rows)


def edge_resources(nc, m, ctx, name):
    sb = lambda n, s, d: ctx.enter_context(nc.sbuf_tensor(name + n, s, d))
    sem = lambda n: new_semaphore(nc, m, name + n)
    s = Names()
    s.idx = [sb(f"idx{b}", [P, C], I32) for b in range(2)]
    s.rows = [sb(f"rows{b}", [P, C, P], F32) for b in range(2)]
    s.onehot = [sb(f"onehot{b}", [P, C * W_WIDE], F32) for b in range(2)]
    s.rows_free, s.idx_ready, s.idx_seen = sem("rows_free"), sem("idx_ready"), sem("idx_seen")
    s.gathered = [sem(f"gathered{b}") for b in range(2)]
    s.agg_ready, s.agg_free, s.added = sem("agg_ready"), sem("agg_free"), sem("added")
    s.chain = sem("chain")
    return s, sb, sem


def onehot_of(v, m, s, chunk, w, b):
    W = W_NARROW if w is None else W_WIDE
    view = s.onehot[b][:, 0:C * W].rearrange("p (t w) -> p t w", w=W)
    nodes = (m.iota_f if w is None else m.iota_w)[:, 0:W]
    where = (m.loc_f if w is None else m.dst_f)[:, ds(chunk * C, C)]
    return view, v.tensor_tensor(view, nodes.unsqueeze(1).to_broadcast([P, C, W]),
                                 where.unsqueeze(2).to_broadcast([P, C, W]), ALU.is_equal)


def next_window(v, m, chain, w):
    v.tensor_scalar(m.iota_w[:], m.iota_w[:], float(W_WIDE), None, ALU.add).then_inc(chain, 1)
    v.wait_ge(chain, w + 1)


def attention_edges(nc, k, m, acc, ad):
    BANKS = 4
    STEPS = C + 7
    with ExitStack() as ctx:
        s, sb, sem = edge_resources(nc, m, ctx, "e0_")
        masked_all = sb("masked", [P, C * W_WIDE], F32)
        ade = sb("ade", [P, C], F32)
        uv = sb("uv", [P, 2, C], F32)
        diff = sb("diff", [P, C], F32)
        pl = [sb(f"pl{b}", [P, C, 2], F32) for b in range(2)]
        weights = [sb(f"weights{b}", [P, C * 2 * W_WIDE], F32) for b in range(2)]
        agg = [ctx.enter_context(nc.psum_tensor(f"e0_agg{n}", [P, 512], F32)) for n in range(BANKS)]
        diff_ready, p_ready, weights_ready, start = sem("diff_ready"), sem("p_ready"), sem("weights_ready"), sem("start")
        windows = sem("windows")

        def shape(wide):
            W = W_WIDE if wide else W_NARROW
            return W, 512 // (4 * W), C * 4 * W // 512

        with nc.Block() as block:
            @block.gpsimd
            def _(pool):
                both_paths(pool, m, lambda wide: gather_program(pool, k, m, s, k.table[0], wide))

            @block.scalar
            def _(act):
                def p_of(n, chunk, w, i, b):
                    act.wait_ge(diff_ready, n + 1)
                    act.activation(pl[b][:, :, 0], diff[:], ACT.Exp).then_inc(p_ready, 1)
                both_paths(act, m, lambda wide: over_chunks(act, k, wide, p_of))

            @block.vector
            def _(v):
                v.memset(acc[:], 0.0).then_inc(start, 1)
                v.wait_ge(start, 1)
                v.sem_inc(s.rows_free, 2)

                def path(wide):
                    W, G, per = shape(wide)
                    v.sem_inc(s.agg_free, min(BANKS, 2 * per))

                    def weigh(n, chunk, w, i, b):
                        ch = Chain(v, s.chain, n * STEPS)
                        onehot, ins = onehot_of(v, m, s, chunk, w, b)
                        ch.step(ins)
                        masked = masked_all[:, 0:C * W].rearrange("p (t w) -> p t w", w=W)
                        for t, base in enumerate(bases_of(v, nc, k, m.base_i, chunk, w)):
                            ch.add(v.tensor_tensor(masked[:, t, :], onehot[:, t, :], ad[:, ds(base, W)], ALU.mult))
                        ch.wait()
                        ch.step(v.tensor_reduce(ade[:], masked, AX.X, ALU.add))
                        ch.step(v.tensor_tensor(uv[:], m.tl[:, 0:2, ds(chunk * C, C)],
                                                ade[:].unsqueeze(1).to_broadcast([P, 2, C]), ALU.add))
                        ch.step(v.scalar_tensor_tensor(uv[:], uv[:], SLOPE, uv[:], ALU.mult, ALU.max))
                        v.tensor_tensor(diff[:], uv[:, 0, :], uv[:, 1, :], ALU.subtract).then_inc(diff_ready, 1)
                        ch.add(v.tensor_copy(pl[b][:, :, 1], m.tl[:, 2, ds(chunk * C, C)]))
                        v.wait_ge(p_ready, n + 1)
                        ch.wait()
                        both = weights[b][:, 0:C * 2 * W].rearrange("p (t kw) -> p t kw", kw=2 * W)
                        for kind in range(2):
                            ch.add(v.tensor_tensor(both[:, :, kind * W:(kind + 1) * W], onehot,
                                                   pl[b][:, :, kind:kind + 1].to_broadcast([P, C, W]), ALU.mult))
                        ch.close(STEPS)
                        v.sem_inc(weights_ready, 1)

                    def add(n, chunk, w, i, b):
                        bases = bases_of(v, nc, k, m.base_i, chunk, w)
                        for g in range(per):
                            v.wait_ge(s.agg_ready, n * per + g + 1)
                            for q in range(G):
                                t = g * G + q
                                window = acc[:, :, ds(bases[t], W)]
                                got = agg[(b * per + g) % BANKS][:, q * 4 * W:q * 4 * W + 3 * W]
                                v.tensor_tensor(window, window, got.rearrange("p (a w) -> p a w", w=W),
                                                ALU.add).then_inc(s.added, 1)
                                v.wait_ge(s.added, n * C + t + 1)
                            v.sem_inc(s.agg_free, 1)
                        v.sem_inc(s.rows_free, 1)

                    over_chunks_lagged(v, k, wide, weigh, add, lambda w: next_window(v, m, windows, w))
                both_paths(v, m, path)

            @block.tensor
            def _(pe):
                def path(wide):
                    W, G, per = shape(wide)

                    def sums(n, chunk, w, i, b):
                        pe.wait_ge(s.gathered[b], (i + 1) * 16 * C)
                        pe.wait_ge(weights_ready, n + 1)
                        both = weights[b][:, 0:C * 2 * W].rearrange("p (t kw) -> p t kw", kw=2 * W)
                        for g in range(per):
                            pe.wait_ge(s.agg_free, n * per + g + 1)
                            to = agg[(b * per + g) % BANKS]
                            for q in range(G):
                                t, at = g * G + q, q * 4 * W
                                pe.matmul(to[:, at:at + W], s.rows[b][:, t, :], both[:, t, 0:W], start=True, stop=True)
                                ins = pe.matmul(to[:, at + W:at + 3 * W], m.ones[:], both[:, t, :], start=True, stop=True)
                            ins.then_inc(s.agg_ready, 1)
                    over_chunks(pe, k, wide, sums)
                both_paths(pe, m, path)


def reset_windows(v, m, chain):
    v.tensor_copy(m.iota_w[:], m.iota_f[:]).then_inc(chain, 1)
    v.wait_ge(chain, 1)


def sum_edges(nc, k, m, name, acc, table):
    BANKS = 4
    with ExitStack() as ctx:
        s, sb, sem = edge_resources(nc, m, ctx, name)
        agg = [ctx.enter_context(nc.psum_tensor(f"{name}agg{n}", [P, 512], F32)) for n in range(BANKS)]
        onehot_ready, start, windows = sem("onehot_ready"), sem("start"), sem("windows")

        def shape(wide):
            W = W_WIDE if wide else W_NARROW
            G = min(C, 512 // W)
            return W, G, C // G

        with nc.Block() as block:
            @block.gpsimd
            def _(pool):
                both_paths(pool, m, lambda wide: gather_program(pool, k, m, s, table, wide))

            @block.vector
            def _(v):
                reset_windows(v, m, start)
                v.memset(acc[:], 0.0).then_inc(start, 1)
                v.wait_ge(start, 2)
                v.sem_inc(s.rows_free, 2)

                def path(wide):
                    W, G, per = shape(wide)
                    v.sem_inc(s.agg_free, min(BANKS, 2 * per))

                    def make(n, chunk, w, i, b):
                        onehot_of(v, m, s, chunk, w, b)[1].then_inc(onehot_ready, 1)

                    def add(n, chunk, w, i, b):
                        bases = bases_of(v, nc, k, m.base_i, chunk, w)
                        for g in range(per):
                            v.wait_ge(s.agg_ready, n * per + g + 1)
                            for q in range(G):
                                t = g * G + q
                                window = acc[:, ds(bases[t], W)]
                                v.tensor_tensor(window, window, agg[(b * per + g) % BANKS][:, q * W:(q + 1) * W],
                                                ALU.add).then_inc(s.added, 1)
                                v.wait_ge(s.added, n * C + t + 1)
                            v.sem_inc(s.agg_free, 1)
                        v.sem_inc(s.rows_free, 1)

                    over_chunks_lagged(v, k, wide, make, add, lambda w: next_window(v, m, windows, w))
                both_paths(v, m, path)

            @block.tensor
            def _(pe):
                def path(wide):
                    W, G, per = shape(wide)

                    def sums(n, chunk, w, i, b):
                        pe.wait_ge(s.gathered[b], (i + 1) * 16 * C)
                        pe.wait_ge(onehot_ready, n + 1)
                        for g in range(per):
                            pe.wait_ge(s.agg_free, n * per + g + 1)
                            to = agg[(b * per + g) % BANKS]
                            for q in range(G):
                                t = g * G + q
                                ins = pe.matmul(to[:, q * W:(q + 1) * W], s.rows[b][:, t, :],
                                                s.onehot[b][:, t * W:(t + 1) * W], start=True, stop=True)
                            ins.then_inc(s.agg_ready, 1)
                    over_chunks(pe, k, wide, sums)
                both_paths(pe, m, path)


def filter_edges(nc, k, m, acc):
    BANKS = 4
    E = C * P
    with ExitStack() as ctx:
        s, sb, sem = edge_resources(nc, m, ctx, "e2_")
        w1 = sb("w1", [P, P], F32)
        w2 = sb("w2", [P, P], F32)
        b1 = sb("b1", [P, 1], F32)
        b2 = sb("b2", [1, P], F32)
        edge = [sb(f"edge{b}", [P, E], F32) for b in range(2)]
        low1, low2 = sb("low1", [P, E], F32), sb("low2", [P, E], F32)
        top1, top2 = sb("top1", [P, E], F32), sb("top2", [P, E], F32)
        filt1 = [sb(f"filt1_{b}", [P, E], F32) for b in range(2)]
        message = sb("message", [P, E], F32)
        z1 = ctx.enter_context(nc.psum_tensor("e2_z1", [P, E], F32))
        z2 = ctx.enter_context(nc.psum_tensor("e2_z2", [P, E], F32))
        agg = [ctx.enter_context(nc.psum_tensor(f"e2_agg{n}", [P, 512], F32)) for n in range(BANKS)]
        consts, edge_ready, start, windows = sem("consts"), [sem(f"edge_ready{b}") for b in range(2)], sem("start"), sem("windows")
        z1_ready, z2_ready, z1_free, z2_free = sem("z1_ready"), sem("z2_ready"), sem("z1_free"), sem("z2_free")
        low1_ready, low2_ready, top1_ready, low1_free, low2_free = (sem(n) for n in ("low1_ready", "low2_ready", "top1_ready", "low1_free", "low2_free"))
        filt1_ready, message_ready = sem("filt1_ready"), sem("message_ready")
        low_chain = [sem("low1_chain"), sem("low2_chain")]

        def shape(wide):
            W = W_WIDE if wide else W_NARROW
            G = min(C, 512 // W)
            return W, G, C // G

        with nc.Block() as block:
            @block.sync
            def _(sp):
                for t, d in ((w1, k.dram["We1T"]), (w2, k.dram["We2T"]), (b1, k.dram["b_e1"].unsqueeze(1)), (b2, k.dram["b_e2"].unsqueeze(0))):
                    sp.dma_start(t[:], d).then_inc(consts, 16)

                def load(n, chunk, w, i, b):
                    sp.wait_ge(z1_ready, n + 1)
                    sp.dma_start(edge[b][:], k.dram["edge_T"][:, ds(chunk * E, E)]).then_inc(edge_ready[b], 16)
                both_paths(sp, m, lambda wide: over_chunks(sp, k, wide, load))
                sp.wait_ge(consts, 64)

            @block.gpsimd
            def _(pool):
                both_paths(pool, m, lambda wide: gather_program(pool, k, m, s, k.table[2], wide))

            @block.tensor
            def _(pe):
                pe.wait_ge(consts, 64)
                pe.sem_inc(z1_ready, 2)

                def path(wide):
                    W, G, per = shape(wide)

                    def first(n, chunk, w, i, b):
                        pe.wait_ge(edge_ready[b], 16 * (i + 1))
                        pe.wait_ge(z1_free, n + 1)
                        for half in range(2):
                            ins = pe.matmul(z1[:, half * 512:(half + 1) * 512], w1[:], edge[b][:, half * 512:(half + 1) * 512],
                                            start=True, stop=True)
                        ins.then_inc(z1_ready, 1)

                    def second(n, chunk, w, i, b):
                        pe.wait_ge(z2_free, n + 1)
                        pe.wait_ge(filt1_ready, n + 1)
                        for t in range(C):
                            to = z2[:, t * P:(t + 1) * P]
                            pe.matmul(to, m.ones[0:1, :], b2[:], start=True, stop=False)
                            ins = pe.matmul(to, filt1[b][:, t * P:(t + 1) * P], w2[:], start=False, stop=True)
                        ins.then_inc(z2_ready, 1)
                        pe.wait_ge(message_ready, n + 1)
                        for g in range(per):
                            pe.wait_ge(s.agg_free, n * per + g + 1)
                            to = agg[(b * per + g) % BANKS]
                            for q in range(G):
                                t = g * G + q
                                ins = pe.matmul(to[:, q * W:(q + 1) * W], message[:, t * P:(t + 1) * P],
                                                s.onehot[b][:, t * W:(t + 1) * W], start=True, stop=True)
                            ins.then_inc(s.agg_ready, 1)
                    over_chunks_lagged(pe, k, wide, first, second, lambda w: None)
                both_paths(pe, m, path)

            @block.scalar
            def _(act):
                act.wait_ge(consts, 64)

                def low_part(z, low, bias, ready, n, chain):
                    ch = Chain(act, chain, n * 2)
                    ch.step(act.activation(low[:], z[:], ACT.Abs, bias=bias))
                    ch.step(act.activation(low[:], low[:], ACT.Exp, scale=-1.0))
                    act.activation(low[:], low[:], ACT.Ln, bias=1.0).then_inc(ready, 1)

                def first(n, chunk, w, i, b):
                    act.wait_ge(z1_ready, n + 3)
                    act.wait_ge(low1_free, n + 1)
                    low_part(z1, low1, b1[:], low1_ready, n, low_chain[0])

                def second(n, chunk, w, i, b):
                    act.wait_ge(z2_ready, n + 1)
                    act.wait_ge(low2_free, n + 1)
                    low_part(z2, low2, 0.0, low2_ready, n, low_chain[1])
                both_paths(act, m, lambda wide: over_chunks_lagged(act, k, wide, first, second, lambda w: None))

            @block.vector
            def _(v):
                v.wait_ge(consts, 64)
                reset_windows(v, m, start)
                v.memset(acc[:], 0.0).then_inc(start, 1)
                v.wait_ge(start, 2)
                for free, count in ((s.rows_free, 2), (z1_free, 1), (z2_free, 1), (low1_free, 1), (low2_free, 1)):
                    v.sem_inc(free, count)

                def path(wide):
                    W, G, per = shape(wide)
                    v.sem_inc(s.agg_free, min(BANKS, 2 * per))

                    def first(n, chunk, w, i, b):
                        v.wait_ge(low_chain[0], 2 * n + 1)
                        v.tensor_scalar(top1[:], z1[:], b1[:], 0.0, ALU.add, ALU.max).then_inc(top1_ready, 1)
                        v.wait_ge(low1_ready, n + 1)
                        v.wait_ge(top1_ready, n + 1)
                        v.sem_inc(z1_free, 1)
                        v.scalar_tensor_tensor(filt1[b][:], low1[:], -LOG2, top1[:], ALU.add, ALU.add).then_inc(filt1_ready, 1)
                        v.wait_ge(filt1_ready, n + 1)
                        v.sem_inc(low1_free, 1)

                    def second(n, chunk, w, i, b):
                        ch = Chain(v, s.chain, n * 4)
                        ch.add(onehot_of(v, m, s, chunk, w, b)[1])
                        v.wait_ge(low_chain[1], 2 * n + 1)
                        ch.add(v.tensor_scalar(top2[:], z2[:], 0.0, None, ALU.max))
                        v.wait_ge(low2_ready, n + 1)
                        ch.wait()
                        v.sem_inc(z2_free, 1)
                        ch.step(v.tensor_tensor(top2[:], low2[:], top2[:], ALU.add))
                        v.sem_inc(low2_free, 1)
                        v.wait_ge(s.gathered[b], (i + 1) * 16 * C)
                        ch.step(v.scalar_tensor_tensor(message[:], top2[:], -LOG2, s.rows[b][:].rearrange("p t d -> p (t d)"),
                                                       ALU.add, ALU.mult))
                        ch.close(4)
                        v.sem_inc(message_ready, 1)
                        v.sem_inc(s.rows_free, 1)
                        bases = bases_of(v, nc, k, m.base_i, chunk, w)
                        for g in range(per):
                            v.wait_ge(s.agg_ready, n * per + g + 1)
                            for q in range(G):
                                t = g * G + q
                                window = acc[:, ds(bases[t], W)]
                                v.tensor_tensor(window, window, agg[(b * per + g) % BANKS][:, q * W:(q + 1) * W],
                                                ALU.add).then_inc(s.added, 1)
                                v.wait_ge(s.added, n * C + t + 1)
                            v.sem_inc(s.agg_free, 1)
                    over_chunks_lagged(v, k, wide, first, second, lambda w: next_window(v, m, windows, w))
                both_paths(v, m, path)


def softmax_edges(nc, k, m, acc, shift_row, top, den):
    T_BANKS, X_BANKS, AGG_BANKS = 2, 2, 2
    LOGITS, CHAIN = 3, 12
    with ExitStack() as ctx:
        s, sb, sem = edge_resources(nc, m, ctx, "e1_")
        ps = lambda n: ctx.enter_context(nc.psum_tensor("e1_" + n, [P, 512], F32))
        key = [sb(f"key{b}", [P, HEADS, CW], F32) for b in range(2)]
        rows_T = sb("rows_T", [P, C, P], F32)
        masked = [sb(f"masked{n}", [P, 512], F32) for n in range(2)]
        weights = [sb(f"weights{n}", [P, 512], F32) for n in range(4)]
        logit = sb("logit", [P, C, HEADS], F32)
        member = sb("member", [P, C], F32)
        p = sb("p", [P, C, HEADS], F32)
        p_sum = sb("p_sum", [P, HEADS], F32)
        col_max = sb("col_max", [P, HEADS], F32)
        new_max = sb("new_max", [HEADS, 1], F32)
        diag = sb("diag", [HEADS, HEADS], F32)
        top_all = [sb(f"top_all{b}", [P, HEADS], F32) for b in range(2)]
        fade = [sb(f"fade{b}", [P, HEADS], F32) for b in range(2)]
        t_ps = [ps(f"t{n}") for n in range(T_BANKS)]
        x_ps = [ps(f"x{n}") for n in range(X_BANKS)]
        agg = [ps(f"agg{n}") for n in range(AGG_BANKS)]
        max_ps = ps("max")
        key_ready, key_free = [sem(f"key_ready{b}") for b in range(2)], sem("key_free")
        turned, t_free, rows_T_ready, rows_T_free = sem("turned"), sem("t_free"), sem("rows_T_ready"), sem("rows_T_free")
        x_ready, x_free, logits_chain = sem("x_ready"), sem("x_free"), sem("logits_chain")
        col_ready, col_turned, diag_ready, top_ready = sem("col_ready"), sem("col_turned"), sem("diag_ready"), sem("top_ready")
        shifted, p_ready, weights_ready, weights_chain = sem("shifted"), sem("p_ready"), sem("weights_ready"), sem("weights_chain")
        start, windows, faded = sem("start"), sem("windows"), sem("faded")

        def shape(wide):
            W = W_WIDE if wide else W_NARROW
            return W, 512 // (HEADS * W), C * HEADS * W // 512

        def walk(eng, wide, first, end, per_window=None):
            half = k.NC // 2
            if not wide:
                first(0, 0, None, 0, 0, False)
                with eng.Fori(0, half - 1) as i:
                    first(2 * i + 1, 2 * i + 1, None, i, 1, True)
                    first(2 * i + 2, 2 * i + 2, None, i + 1, 0, True)
                first(k.NC - 1, k.NC - 1, None, half - 1, 1, True)
                end(k.NC - 1, k.NC - 1, None, half - 1, 1)
            else:
                with eng.Fori(0, k.NW) as w:
                    with eng.Fori(0, half) as i:
                        for b in range(2):
                            at = (w * k.NC + 2 * i + b, 2 * i + b, w, w * half + i, b)
                            first(*at, False)
                            end(*at)
                    if per_window:
                        per_window(w)

        with nc.Block() as block:
            @block.sync
            def _(sp):
                def load(n, chunk, w, i, b):
                    sp.wait_ge(key_free, n + 1)
                    if w is None:
                        base = sp.value_load(m.base_i[0:1, ds(chunk * C, 1)], min_val=0, max_val=k.N - 1)
                        sp.dma_start(key[b][:], k.dram["key_dram"][:, :, ds(base, CW)]).then_inc(key_ready[b], 16)
                    else:
                        sp.dma_start(key[b][:, :, 0:W_WIDE], k.dram["key_dram"][:, :, ds(w * W_WIDE, W_WIDE)]).then_inc(key_ready[b], 16)
                both_paths(sp, m, lambda wide: over_chunks(sp, k, wide, load))

            @block.gpsimd
            def _(pool):
                both_paths(pool, m, lambda wide: gather_program(pool, k, m, s, k.table[1], wide))

            @block.scalar
            def _(act):
                def chunk_work(n, chunk, w, i, b):
                    act.wait_ge(rows_T_free, n + 1)
                    for half in range(2):
                        act.wait_ge(turned, 2 * n + half + 1)
                        act.activation(rows_T[:, half * 4:half * 4 + 4, :].rearrange("p t d -> p (t d)"), t_ps[half][:],
                                       ACT.Copy).then_inc(rows_T_ready, 1)
                    act.wait_ge(shifted, n + 1)
                    act.activation(p[:], p[:], ACT.Exp).then_inc(p_ready, 1)
                    act.activation(fade[b][:], fade[b][:], ACT.Exp).then_inc(p_ready, 1)
                both_paths(act, m, lambda wide: over_chunks(act, k, wide, chunk_work))

            @block.tensor
            def _(pe):
                def path(wide):
                    W, G, per = shape(wide)

                    def sums(n, chunk, w, i, b):
                        for g in range(per):
                            pe.wait_ge(weights_ready, n * per + g + 1)
                            pe.wait_ge(s.agg_free, n * per + g + 1)
                            to = agg[g % 2]
                            for q in range(G):
                                ins = pe.matmul(to[:, q * HEADS * W:(q + 1) * HEADS * W], s.rows[b][:, g * G + q, :],
                                                weights[(g + 2 * b) % 4][:, q * HEADS * W:(q + 1) * HEADS * W],
                                                start=True, stop=True)
                            ins.then_inc(s.agg_ready, 1)

                    def chunk_work(n, chunk, w, i, b, lagged):
                        pe.wait_ge(s.gathered[b], (i + 1) * 16 * C)
                        for half in range(2):
                            pe.wait_ge(rows_T_free, n + 1)
                            for q in range(4):
                                ins = pe.transpose(t_ps[half][:, q * P:(q + 1) * P], s.rows[b][:, half * 4 + q, :], m.ident[:])
                            ins.then_inc(turned, 1)
                        if lagged:
                            sums(n - 1, None, w, None, 1 - b)
                        pe.wait_ge(key_ready[b], 16 * (i + 1))
                        rel = bases_of(pe, nc, k, m.rel_i, chunk, w, CW - W_NARROW) if w is None else [0] * C
                        for g in range(per):
                            pe.wait_ge(rows_T_ready, 2 * n + (g * G) // 4 + 1)
                            pe.wait_ge(x_free, n * per + g + 1)
                            for q in range(G):
                                t = g * G + q
                                ins = pe.matmul(x_ps[g % 2][:, q * HEADS * W:(q + 1) * HEADS * W], rows_T[:, t, :],
                                                key[b][:, :, ds(rel[t], W)], start=True, stop=True)
                            ins.then_inc(x_ready, 1)
                        pe.wait_ge(col_ready, n + 1)
                        pe.transpose(max_ps[0:HEADS, 0:P], col_max[:], m.ident[:]).then_inc(col_turned, 1)
                        pe.wait_ge(diag_ready, n + 1)
                        pe.matmul(max_ps[:, P:P + HEADS], m.ones[0:HEADS, :], diag[:], start=True, stop=True).then_inc(top_ready, 1)
                    walk(pe, wide, chunk_work, sums)
                both_paths(pe, m, path)

            @block.vector
            def _(v):
                reset_windows(v, m, start)
                for t, value in ((acc, 0.0), (shift_row, START), (top, START), (den, 0.0), (top_all[1], START)):
                    v.memset(t[:], value).then_inc(start, 1)
                v.wait_ge(start, 6)
                for free, count in ((s.rows_free, 2), (key_free, 2), (rows_T_free, 1), (x_free, 2), (s.agg_free, 2)):
                    v.sem_inc(free, count)

                def path(wide):
                    W, G, per = shape(wide)

                    def add(n, chunk, w, i, b):
                        bases = bases_of(v, nc, k, m.base_i, chunk, w)
                        window = acc[:, :, ds(bases[0], W)]
                        v.tensor_tensor(window, window, over(fade[b][:], [P, HEADS, W]), ALU.mult).then_inc(s.added, 1)
                        v.wait_ge(s.added, n * (C + 1) + 1)
                        for g in range(per):
                            if wide:
                                build(n, g, b)
                            v.wait_ge(s.agg_ready, n * per + g + 1)
                            for q in range(G):
                                t = g * G + q
                                window = acc[:, :, ds(bases[t], W)]
                                got = agg[g % 2][:, q * HEADS * W:(q + 1) * HEADS * W].rearrange("p (h w) -> p h w", w=W)
                                v.tensor_tensor(window, window, got, ALU.add).then_inc(s.added, 1)
                                v.wait_ge(s.added, n * (C + 1) + t + 2)
                            v.sem_inc(s.agg_free, 1)
                        v.sem_inc(s.rows_free, 1)

                    def build(n, g, b):
                        onehot = s.onehot[b][:, 0:C * W].rearrange("p (t w) -> p t w", w=W)
                        out = weights[(g + 2 * b) % 4][:].rearrange("p (t h w) -> p t h w", h=HEADS, w=W)
                        t = slice(g * G, (g + 1) * G)
                        v.tensor_tensor(out, onehot[:, t, :].unsqueeze(2).to_broadcast([P, G, HEADS, W]),
                                        p[:, t, :].unsqueeze(3).to_broadcast([P, G, HEADS, W]), ALU.mult).then_inc(weights_chain, 1)
                        v.wait_ge(weights_chain, n * per + g + 1)
                        v.sem_inc(weights_ready, 1)

                    def chunk_work(n, chunk, w, i, b, lagged):
                        ch = Chain(v, logits_chain, n * (LOGITS + 2 * per))
                        onehot, ins = onehot_of(v, m, s, chunk, w, b)
                        ch.step(ins)
                        ch.step(v.tensor_reduce(member[:], onehot, AX.X, ALU.add))
                        ch.add(v.tensor_scalar(member[:], member[:], -1.0, BIG, ALU.add, ALU.mult))
                        for g in range(per):
                            v.wait_ge(x_ready, n * per + g + 1)
                            t = slice(g * G, (g + 1) * G)
                            part = masked[g % 2][:].rearrange("p (t h w) -> p t h w", h=HEADS, w=W)
                            ch.step(v.tensor_tensor(part, x_ps[g % 2][:].rearrange("p (t h w) -> p t h w", h=HEADS, w=W),
                                                    onehot[:, t, :].unsqueeze(2).to_broadcast([P, G, HEADS, W]), ALU.mult))
                            v.sem_inc(x_free, 1)
                            ch.add(v.tensor_reduce(logit[:, t, :], part, AX.X, ALU.add))
                        ch.close(LOGITS + 2 * per)
                        v.sem_inc(rows_T_free, 1)
                        v.sem_inc(key_free, 1)
                        ch = Chain(v, s.chain, n * CHAIN)
                        ch.step(v.tensor_tensor(logit[:], logit[:], over(member[:], [P, C, HEADS]), ALU.add))
                        ch.step(v.tensor_reduce(col_max[:], logit[:].rearrange("p t h -> p h t"), AX.X, ALU.max))
                        v.sem_inc(col_ready, 1)
                        if lagged:
                            add(n - 1, chunk - 1, w, None, 1 - b)
                        v.wait_ge(col_turned, n + 1)
                        ch.step(v.tensor_reduce(new_max[:], max_ps[0:HEADS, 0:P], AX.X, ALU.max))
                        ch.step(v.tensor_tensor(top[:], top[:], new_max[:], ALU.max))
                        ch.step(v.tensor_scalar(diag[:], m.ident[0:HEADS, 0:HEADS], top[:], None, ALU.mult))
                        v.sem_inc(diag_ready, 1)
                        if wide:
                            span = shift_row[:, ds(w * W_WIDE, W_WIDE)]
                        else:
                            base = v.value_load(m.base_i[0:1, ds(chunk * C, 1)], min_val=0, max_val=k.N - 1)
                            span = shift_row[:, ds(base, CW)]
                        size = W_WIDE if wide else CW
                        ch.add(v.tensor_scalar(span, m.ones[0:HEADS, 0:1].to_broadcast([HEADS, size]), top[:], None, ALU.mult))
                        v.wait_ge(top_ready, n + 1)
                        ch.step(v.tensor_copy(top_all[b][:], max_ps[:, P:P + HEADS]))
                        ch.add(v.tensor_tensor(fade[b][:], top_all[1 - b][:], top_all[b][:], ALU.subtract))
                        ch.step(v.tensor_tensor(p[:], logit[:], top_all[b][:].unsqueeze(1).to_broadcast([P, C, HEADS]), ALU.subtract))
                        v.sem_inc(shifted, 1)
                        v.wait_ge(p_ready, 2 * n + 2)
                        if not wide:
                            for g in range(per):
                                build(n, g, b)
                        ch.add(v.tensor_reduce(p_sum[:], p[:].rearrange("p t h -> p h t"), AX.X, ALU.add))
                        ch.step(v.tensor_tensor(den[:], den[:], fade[b][:], ALU.mult))
                        ch.step(v.tensor_tensor(den[:], den[:], p_sum[:], ALU.add))
                        ch.close(CHAIN)
                    walk(v, wide, chunk_work, add, lambda w: next_window(v, m, windows, w))
                both_paths(v, m, path)
class Node:

    def __init__(self, nc, ctx, k, m, name):
        self.nc, self.ctx, self.k, self.m, self.name = nc, ctx, k, m, name

    def sb(self, n, shape, dt=F32):
        return self.ctx.enter_context(self.nc.sbuf_tensor(self.name + n, shape, dt))

    def ps(self, n):
        return self.ctx.enter_context(self.nc.psum_tensor(self.name + n, [P, 512], F32))

    def sem(self, n):
        return new_semaphore(self.nc, self.m, self.name + n)


def load_nodes(nc, k, m, name, x_from, hT_from=None):
    with ExitStack() as ctx:
        loaded = new_semaphore(nc, m, name + "loaded")
        with nc.Block() as block:
            @block.sync
            def _(sp):
                sp.dma_start(m.x[:], x_from.rearrange("(n p) d -> p n d", p=P)).then_inc(loaded, 16)
                if hT_from is not None:
                    sp.dma_start(m.hT[:], hT_from).then_inc(loaded, 16)
                sp.wait_ge(loaded, 32 if hT_from is not None else 16)


def keep_nodes(nc, k, m, name, x_to, hT_to=None):
    with ExitStack() as ctx:
        kept = new_semaphore(nc, m, name + "kept")
        with nc.Block() as block:
            @block.sync
            def _(sp):
                sp.dma_start(x_to.rearrange("(n p) d -> p n d", p=P), m.x[:]).then_inc(kept, 16)
                if hT_to is not None:
                    sp.dma_start(hT_to, m.hT[:]).then_inc(kept, 16)
                sp.wait_ge(kept, 32 if hT_to is not None else 16)


def add_to_x(v, m, g, y, bias, ch):
    x = m.x[:, ds(g * G4, G4), :]
    ch.step(v.tensor_tensor(x, x, y[:].rearrange("p (b d) -> p b d", b=G4), ALU.add))
    ch.step(v.tensor_tensor(x, x, bias[:].unsqueeze(1).to_broadcast([P, G4, P]), ALU.add))


def attention_output(nc, k, m, acc, ad):
    STEPS = 16
    with ExitStack() as ctx:
        a = Node(nc, ctx, k, m, "o0_")
        w, bias = a.sb("w", [P, P]), a.sb("bias", [P, P])
        e = a.sb("e", [P, 2, GN])
        top, whole, mixed = a.sb("top", [P, GN]), a.sb("whole", [P, GN]), a.sb("mixed", [P, GN])
        own_ps, y_ps = a.ps("own"), a.ps("y")
        loaded, own_ready, own_free, chain = a.sem("loaded"), a.sem("own_ready"), a.sem("own_free"), a.sem("chain")
        shifted, factors, mixed_ready, y_ready = a.sem("shifted"), a.sem("factors"), a.sem("mixed_ready"), a.sem("y_ready")
        with nc.Block() as block:
            @block.sync
            def _(sp):
                sp.dma_start(w[:], k.dram["W0"]).then_inc(loaded, 16)
                sp.dma_start(bias[:], k.dram["bias0"].partition_broadcast(P)).then_inc(loaded, 16)
                sp.wait_ge(loaded, 32)

            @block.tensor
            def _(pe):
                pe.wait_ge(loaded, 32)
                with pe.Fori(0, k.NG) as g:
                    pe.wait_ge(own_free, g + 1)
                    pe.matmul(own_ps[:], m.ws_rep[:], m.hT[:, ds(g * GN, GN)], start=True, stop=True).then_inc(own_ready, 1)
                    pe.wait_ge(mixed_ready, g + 1)
                    for b in range(G4):
                        ins = pe.matmul(y_ps[:, b * P:(b + 1) * P], mixed[:, b * P:(b + 1) * P], w[:], start=True, stop=True)
                    ins.then_inc(y_ready, 1)

            @block.scalar
            def _(act):
                with act.Fori(0, k.NG) as g:
                    act.wait_ge(shifted, g + 1)
                    act.activation(e[:], e[:], ACT.Exp).then_inc(factors, 1)

            @block.vector
            def _(v):
                v.wait_ge(loaded, 32)
                v.sem_inc(own_free, 1)
                with v.Fori(0, k.NG) as g:
                    ch = Chain(v, chain, g * STEPS)
                    at = ds(g * GN, GN)
                    v.wait_ge(own_ready, g + 1)
                    ch.add(v.tensor_tensor(e[:, 1, :], own_ps[:], ad[:, at], ALU.add))
                    ch.step(v.tensor_scalar(e[:, 0, :], acc[:, 1, at], 0.0, -BIG, ALU.is_equal, ALU.mult))
                    v.sem_inc(own_free, 1)
                    ch.step(v.tensor_tensor(e[:, 0, :], e[:, 0, :], acc[:, 2, at], ALU.add))
                    ch.step(v.tensor_tensor(e[:, 0, :], e[:, 0, :], ad[:, at], ALU.add))
                    ch.step(v.scalar_tensor_tensor(e[:], e[:], SLOPE, e[:], ALU.mult, ALU.max))
                    ch.step(v.tensor_tensor(top[:], e[:, 0, :], e[:, 1, :], ALU.max))
                    ch.step(v.tensor_tensor(e[:], e[:], top[:].unsqueeze(1).to_broadcast([P, 2, GN]), ALU.subtract))
                    v.sem_inc(shifted, 1)
                    v.wait_ge(factors, g + 1)
                    ch.add(v.tensor_tensor(mixed[:], acc[:, 0, at], e[:, 0, :], ALU.mult))
                    ch.add(v.tensor_tensor(top[:], m.hT[:, at], e[:, 1, :], ALU.mult))
                    ch.step(v.tensor_tensor(whole[:], acc[:, 1, at], e[:, 0, :], ALU.mult))
                    ch.add(v.tensor_tensor(mixed[:], mixed[:], top[:], ALU.add))
                    ch.step(v.tensor_tensor(whole[:], whole[:], e[:, 1, :], ALU.add))
                    ch.step(v.reciprocal(whole[:], whole[:]))
                    ch.step(v.tensor_tensor(mixed[:], mixed[:], whole[:], ALU.mult))
                    v.sem_inc(mixed_ready, 1)
                    v.wait_ge(y_ready, g + 1)
                    add_to_x(v, m, g, y_ps, bias, ch)
                    ch.close(STEPS)


def key_phase(nc, k, m):
    SCALE = float(P) ** -0.5
    with ExitStack() as ctx:
        a = Node(nc, ctx, k, m, "key_")
        wq, wk, pair = a.sb("wq", [P, HEADS, P]), a.sb("wk", [P, HEADS, P]), a.sb("pair", [P, HEADS, P])
        out = a.sb("out", [P, HEADS, GN])
        pair_ps = a.ps("pair_ps")
        key_ps = [a.ps(f"key_ps{h}") for h in range(HEADS)]
        loaded, pair_ready, pair_kept = a.sem("loaded"), a.sem("pair_ready"), a.sem("pair_kept")
        key_ready, taken, stored = a.sem("key_ready"), a.sem("taken"), a.sem("stored")
        with nc.Block() as block:
            @block.sync
            def _(sp):
                sp.dma_start(wq[:], k.dram["Wq"]).then_inc(loaded, 16)
                sp.dma_start(wk[:], k.dram["Wk"]).then_inc(loaded, 16)
                sp.sem_inc(stored, 16)
                with sp.Fori(0, k.NG) as g:
                    sp.wait_ge(taken, HEADS * (g + 1) + HEADS)
                    sp.dma_start(k.dram["key_dram"][:, :, ds(g * GN, GN)], out[:]).then_inc(stored, 16)
                sp.wait_ge(stored, 16 * (k.NG + 1))

            @block.tensor
            def _(pe):
                pe.wait_ge(loaded, 32)
                for h in range(HEADS):
                    ins = pe.matmul(pair_ps[:, h * P:(h + 1) * P], wk[:, h, :], wq[:, h, :], start=True, stop=True)
                ins.then_inc(pair_ready, 1)
                pe.wait_ge(pair_kept, 1)
                pe.sem_inc(taken, HEADS)
                with pe.Fori(0, k.NG) as g:
                    pe.wait_ge(taken, HEADS * (g + 1))
                    for h in range(HEADS):
                        pe.matmul(key_ps[h][:], pair[:, h, :], m.hT[:, ds(g * GN, GN)], start=True, stop=True
                                  ).then_inc(key_ready, 1)

            @block.vector
            def _(v):
                v.wait_ge(pair_ready, 1)
                v.tensor_scalar(pair[:].rearrange("p h d -> p (h d)"), pair_ps[:], SCALE, None, ALU.mult).then_inc(pair_kept, 1)
                with v.Fori(0, k.NG) as g:
                    v.wait_ge(stored, 16 * (g + 1))
                    for h in range(2):
                        v.wait_ge(key_ready, HEADS * g + h + 1)
                        v.tensor_copy(out[:, h, :], key_ps[h][:]).then_inc(taken, 1)

            @block.scalar
            def _(act):
                with act.Fori(0, k.NG) as g:
                    act.wait_ge(stored, 16 * (g + 1))
                    for h in range(2, 4):
                        act.wait_ge(key_ready, HEADS * g + h + 1)
                        act.activation(out[:, h, :], key_ps[h][:], ACT.Copy).then_inc(taken, 1)


def factor_phase(nc, k, m, shift_row, top, den, factor):
    with ExitStack() as ctx:
        a = Node(nc, ctx, k, m, "fa_")
        negative, inverse = a.sb("negative", [HEADS, 1]), a.sb("inverse", [P, HEADS])
        f_ps, den_ps = a.ps("f_ps"), a.ps("den_ps")
        den_ready, top_ready, row_ready, cols_ready, taken, chain = (
            a.sem(n) for n in ("den_ready", "top_ready", "row_ready", "cols_ready", "taken", "chain"))
        static = a.sb("static", [HEADS, GN])
        with nc.Block() as block:
            @block.tensor
            def _(pe):
                pe.matmul(den_ps[:, 0:HEADS], m.ones[:], den[:], start=True, stop=True).then_inc(den_ready, 1)
                with pe.Fori(0, k.NG) as g:
                    pe.wait_ge(row_ready, g + 1)
                    for b in range(G4):
                        ins = pe.matmul(f_ps[:, b * HEADS:(b + 1) * HEADS], static[:, b * P:(b + 1) * P],
                                        m.ident[0:HEADS, 0:HEADS], start=True, stop=True)
                    ins.then_inc(cols_ready, 1)

            @block.scalar
            def _(act):
                act.wait_ge(top_ready, 1)
                act.sem_inc(taken, 1)
                with act.Fori(0, k.NG) as g:
                    act.wait_ge(taken, g + 1)
                    act.activation(static[:], shift_row[:, ds(g * GN, GN)], ACT.Exp, bias=negative[:]).then_inc(row_ready, 1)

            @block.vector
            def _(v):
                v.tensor_scalar(negative[:], top[:], -1.0, None, ALU.mult).then_inc(top_ready, 1)
                v.wait_ge(den_ready, 1)
                v.reciprocal(inverse[:], den_ps[:, 0:HEADS]).then_inc(chain, 1)
                v.wait_ge(chain, 1)
                with v.Fori(0, k.NG) as g:
                    v.wait_ge(cols_ready, g + 1)
                    v.tensor_tensor(factor[:, ds(g * G4, G4), :], f_ps[:, 0:G4 * HEADS].rearrange("p (b h) -> p b h", h=HEADS),
                                    inverse[:].unsqueeze(1).to_broadcast([P, G4, HEADS]), ALU.mult).then_inc(taken, 1)


def softmax_output(nc, k, m, acc, factor):
    F = HEADS * P
    STEPS = 21
    with ExitStack() as ctx:
        a = Node(nc, ctx, k, m, "o1_")
        wq, wr, wo = a.sb("wq", [P, HEADS, P]), a.sb("wr", [P, F]), a.sb("wo", [P, HEADS, P])
        bo, gamma, beta, br = a.sb("bo", [P, P]), a.sb("gamma", [P, F]), a.sb("beta", [P, F]), a.sb("br", [P, F])
        sums, h_T, h_rows = a.sb("sums", [P, HEADS, P]), a.sb("h_T", [P, P]), a.sb("h_rows", [P, P])
        heads, gate, joined_T = a.sb("heads", [P, F]), a.sb("gate", [P, F]), a.sb("joined_T", [P, F])
        fac = a.sb("fac", [P, HEADS])
        stats, mv, rstd = a.sb("stats", [P, 1, 6]), a.sb("mv", [P, 1, 2]), a.sb("rstd", [P, 1])
        heads_ps, h_ps, res_ps, t_ps, y_ps = (a.ps(n) for n in ("heads_ps", "h_ps", "res_ps", "t_ps", "y_ps"))
        loaded, copied, sums_ready, chain, act_chain = (a.sem(n) for n in ("loaded", "copied", "sums_ready", "chain", "act_chain"))
        var_ready, shift_ready, gate_ready, affine, joined_ready, turned, joined_T_ready, y_ready, done = (
            a.sem(n) for n in ("var_ready", "shift_ready", "gate_ready", "affine", "joined_ready", "turned", "joined_T_ready",
                               "y_ready", "done"))
        parts = ((wq, k.dram["WqT"]), (wr, k.dram["WrT"]), (wo, k.dram["WoT"]), (bo, k.dram["bo"].partition_broadcast(P)), (gamma, k.dram["gamma"].partition_broadcast(P)),
                 (beta, k.dram["beta"].partition_broadcast(P)), (br, k.dram["br"].partition_broadcast(P)))
        with nc.Block() as block:
            @block.sync
            def _(sp):
                for t, d in parts:
                    sp.dma_start(t[:], d).then_inc(loaded, 16)
                sp.wait_ge(loaded, 16 * len(parts))

            @block.scalar
            def _(act):
                act.wait_ge(loaded, 16 * len(parts))
                with act.Fori(0, k.NB) as n:
                    act.wait_ge(done, n + 1)
                    act.activation(sums[:], acc[:, :, ds(n * P, P)], ACT.Copy).then_inc(copied, 1)
                    act.activation(h_T[:], m.hT[:, ds(n * P, P)], ACT.Copy).then_inc(copied, 1)
                    act.wait_ge(sums_ready, n + 1)
                    act.activation(h_rows[:], h_ps[:, 0:P], ACT.Copy).then_inc(copied, 1)
                    ch = Chain(act, act_chain, n * 4)
                    act.wait_ge(var_ready, n + 1)
                    ch.step(act.activation(rstd[:], mv[:, :, 1], ACT.Ln, bias=m.eps[:]))
                    ch.step(act.activation(rstd[:], rstd[:], ACT.Exp, scale=-0.5))
                    act.sem_inc(shift_ready, 1)
                    act.wait_ge(affine, n + 1)
                    ch.step(act.activation(gate[:], heads[:], ACT.Exp, scale=-1.0))
                    ch.step(act.activation(gate[:], gate[:], ACT.Ln, bias=1.0))
                    act.activation(gate[:], gate[:], ACT.Exp, scale=-1.0).then_inc(gate_ready, 1)
                    act.wait_ge(turned, n + 1)
                    act.activation(joined_T[:], t_ps[:], ACT.Copy).then_inc(joined_T_ready, 1)

            @block.tensor
            def _(pe):
                pe.wait_ge(loaded, 16 * len(parts))
                with pe.Fori(0, k.NB) as n:
                    pe.wait_ge(copied, 3 * n + 2)
                    pe.wait_ge(done, n + 1)
                    for h in range(HEADS):
                        pe.matmul(heads_ps[:, h * P:(h + 1) * P], sums[:, h, :], wq[:, h, :], start=True, stop=True)
                    pe.transpose(h_ps[:, 0:P], h_T[:], m.ident[:])
                    pe.matmul(res_ps[:], h_T[:], wr[:], start=True, stop=True).then_inc(sums_ready, 1)
                    pe.wait_ge(joined_ready, n + 1)
                    for h in range(HEADS):
                        ins = pe.transpose(t_ps[:, h * P:(h + 1) * P], gate[:, h * P:(h + 1) * P], m.ident[:])
                    ins.then_inc(turned, 1)
                    pe.wait_ge(joined_T_ready, n + 1)
                    for h in range(HEADS):
                        ins = pe.matmul(y_ps[:, 0:P], joined_T[:, h * P:(h + 1) * P], wo[:, h, :],
                                        start=(h == 0), stop=(h == HEADS - 1))
                    ins.then_inc(y_ready, 1)

            @block.vector
            def _(v):
                v.wait_ge(loaded, 16 * len(parts))
                v.sem_inc(done, 1)
                with v.Fori(0, k.NB) as n:
                    ch = Chain(v, chain, n * STEPS)
                    ch.step(v.tensor_copy(fac[:], factor[:, ds(n, 1), :].rearrange("p a h -> p (a h)")))
                    v.wait_ge(sums_ready, n + 1)
                    v.wait_ge(copied, 3 * n + 3)
                    for h in range(HEADS):
                        ch.add(v.scalar_tensor_tensor(heads[:, h * P:(h + 1) * P], heads_ps[:, h * P:(h + 1) * P], fac[:, h:h + 1],
                                                      h_rows[:], ALU.mult, ALU.add))
                    ch.wait()
                    ch.step(v.bn_stats(stats[:, 0, :], heads[:]))
                    mean_and_var(v, ch, stats[:], mv[:], F)
                    v.sem_inc(var_ready, 1)
                    v.wait_ge(shift_ready, n + 1)
                    ch.step(v.tensor_scalar(heads[:], heads[:], mv[:, 0, 0:1], rstd[:], ALU.subtract, ALU.mult))
                    ch.step(v.tensor_tensor(heads[:], heads[:], gamma[:], ALU.mult))
                    ch.step(v.tensor_tensor(heads[:], heads[:], beta[:], ALU.add))
                    v.sem_inc(affine, 1)
                    v.wait_ge(gate_ready, n + 1)
                    ch.step(v.tensor_tensor(gate[:], gate[:], heads[:], ALU.mult))
                    ch.step(v.tensor_tensor(gate[:], gate[:], res_ps[:], ALU.add))
                    ch.step(v.tensor_tensor(gate[:], gate[:], br[:], ALU.add))
                    v.sem_inc(joined_ready, 1)
                    v.wait_ge(y_ready, n + 1)
                    x = m.x[:, ds(n, 1), :].rearrange("p a d -> p (a d)")
                    ch.step(v.tensor_tensor(x, x, y_ps[:, 0:P], ALU.add))
                    ch.step(v.tensor_tensor(x, x, bo[:], ALU.add))
                    ch.close(STEPS)
                    v.sem_inc(done, 1)


def product_phase(nc, k, m):
    with ExitStack() as ctx:
        a = Node(nc, ctx, k, m, "pr_")
        w, bias = a.sb("w", [P, P]), a.sb("bias", [P, P])
        h_T, out, y_ps = a.sb("h_T", [P, GN]), a.sb("out", [P, G4, P]), a.ps("y")
        loaded, copied, y_ready, y_free, out_ready, stored = (
            a.sem(n) for n in ("loaded", "copied", "y_ready", "y_free", "out_ready", "stored"))
        with nc.Block() as block:
            @block.sync
            def _(sp):
                sp.dma_start(w[:], k.dram["WnT"]).then_inc(loaded, 16)
                sp.dma_start(bias[:], k.dram["b_node"].partition_broadcast(P)).then_inc(loaded, 16)
                sp.sem_inc(stored, 16)
                with sp.Fori(0, k.NG) as g:
                    sp.wait_ge(out_ready, g + 1)
                    sp.dma_start(k.table[2].rearrange("(n p) d -> p n d", p=P)[:, ds(g * G4, G4), :], out[:]).then_inc(stored, 16)
                sp.wait_ge(stored, 16 * (k.NG + 1))

            @block.scalar
            def _(act):
                act.sem_inc(y_ready, 1)
                with act.Fori(0, k.NG) as g:
                    act.wait_ge(y_ready, g + 1)
                    act.activation(h_T[:], m.hT[:, ds(g * GN, GN)], ACT.Copy).then_inc(copied, 1)

            @block.tensor
            def _(pe):
                pe.wait_ge(loaded, 32)
                pe.sem_inc(y_free, 1)
                with pe.Fori(0, k.NG) as g:
                    pe.wait_ge(copied, g + 1)
                    pe.wait_ge(y_free, g + 1)
                    for b in range(G4):
                        ins = pe.matmul(y_ps[:, b * P:(b + 1) * P], h_T[:, b * P:(b + 1) * P], w[:], start=True, stop=True)
                    ins.then_inc(y_ready, 1)

            @block.vector
            def _(v):
                v.wait_ge(loaded, 32)
                with v.Fori(0, k.NG) as g:
                    v.wait_ge(y_ready, g + 2)
                    v.wait_ge(stored, 16 * (g + 1))
                    v.tensor_tensor(out[:], y_ps[:].rearrange("p (b d) -> p b d", b=G4),
                                    bias[:].unsqueeze(1).to_broadcast([P, G4, P]), ALU.add).then_inc(out_ready, 1)
                    v.wait_ge(out_ready, g + 1)
                    v.sem_inc(y_free, 1)


def filter_output(nc, k, m, acc):
    STEPS = 5
    with ExitStack() as ctx:
        a = Node(nc, ctx, k, m, "o2_")
        w1, w2, b1, bias = a.sb("w1", [P, P]), a.sb("w2", [P, P]), a.sb("b1", [P, 1]), a.sb("bias", [P, P])
        low, top = a.sb("low", [P, GN]), a.sb("top", [P, GN])
        z_ps, y_ps = a.ps("z"), a.ps("y")
        loaded, z_ready, z_free, low_ready, chain, act_chain, mid_ready, y_ready = (
            a.sem(n) for n in ("loaded", "z_ready", "z_free", "low_ready", "chain", "act_chain", "mid_ready", "y_ready"))
        with nc.Block() as block:
            @block.sync
            def _(sp):
                for t, d in ((w1, k.dram["Wf1T"]), (w2, k.dram["Wf2T"]), (b1, k.dram["b_fc1"].unsqueeze(1)), (bias, k.dram["b_fc2"].partition_broadcast(P))):
                    sp.dma_start(t[:], d).then_inc(loaded, 16)
                sp.wait_ge(loaded, 64)

            @block.tensor
            def _(pe):
                pe.wait_ge(loaded, 64)
                with pe.Fori(0, k.NG) as g:
                    pe.wait_ge(z_free, g + 1)
                    pe.matmul(z_ps[:], w1[:], acc[:, ds(g * GN, GN)], start=True, stop=True).then_inc(z_ready, 1)
                    pe.wait_ge(mid_ready, g + 1)
                    for b in range(G4):
                        ins = pe.matmul(y_ps[:, b * P:(b + 1) * P], low[:, b * P:(b + 1) * P], w2[:], start=True, stop=True)
                    ins.then_inc(y_ready, 1)

            @block.scalar
            def _(act):
                act.wait_ge(loaded, 64)
                act.sem_inc(y_ready, 1)
                with act.Fori(0, k.NG) as g:
                    ch = Chain(act, act_chain, g * 2)
                    act.wait_ge(z_ready, g + 1)
                    act.wait_ge(y_ready, g + 1)
                    ch.step(act.activation(low[:], z_ps[:], ACT.Abs, bias=b1[:]))
                    ch.step(act.activation(low[:], low[:], ACT.Exp, scale=-1.0))
                    act.activation(low[:], low[:], ACT.Ln, bias=1.0).then_inc(low_ready, 1)

            @block.vector
            def _(v):
                v.wait_ge(loaded, 64)
                v.sem_inc(z_free, 1)
                with v.Fori(0, k.NG) as g:
                    ch = Chain(v, chain, g * 4)
                    v.wait_ge(act_chain, 2 * g + 1)
                    ch.add(v.tensor_scalar(top[:], z_ps[:], b1[:], 0.0, ALU.add, ALU.max))
                    v.wait_ge(low_ready, g + 1)
                    ch.wait()
                    v.sem_inc(z_free, 1)
                    ch.step(v.scalar_tensor_tensor(low[:], low[:], -LOG2, top[:], ALU.add, ALU.add))
                    v.sem_inc(mid_ready, 1)
                    v.wait_ge(y_ready, g + 2)
                    add_to_x(v, m, g, y_ps, bias, ch)
                    ch.close(4)


def perceptron_output(nc, k, m, acc):
    with ExitStack() as ctx:
        a = Node(nc, ctx, k, m, "o3_")
        w1, w2, b1, bias = a.sb("w1", [P, 2 * P]), a.sb("w2", [P, 2, P]), a.sb("b1", [P, 2]), a.sb("bias", [P, P])
        mid = a.sb("mid", [P, 2, GN])
        z_ps, y_ps = [a.ps(f"z{n}") for n in range(2)], a.ps("y")
        loaded, sum_ready, z_ready, mid_ready, chain, y_ready = (
            a.sem(n) for n in ("loaded", "sum_ready", "z_ready", "mid_ready", "chain", "y_ready"))
        with nc.Block() as block:
            @block.sync
            def _(sp):
                for t, d in ((w1, k.dram["W1"]), (w2, k.dram["W2"]), (b1, k.dram["b1"]), (bias, k.dram["b2"].partition_broadcast(P))):
                    sp.dma_start(t[:], d).then_inc(loaded, 16)
                sp.wait_ge(loaded, 64)

            @block.tensor
            def _(pe):
                pe.wait_ge(loaded, 64)
                pe.sem_inc(mid_ready, 2)
                with pe.Fori(0, k.NG) as g:
                    pe.wait_ge(sum_ready, g + 1)
                    pe.wait_ge(mid_ready, 2 * g + 2)
                    for n in range(2):
                        pe.matmul(z_ps[n][:], w1[:, n * P:(n + 1) * P], acc[:, ds(g * GN, GN)], start=True, stop=True
                                  ).then_inc(z_ready, 1)
                    pe.wait_ge(mid_ready, 2 * g + 4)
                    for b in range(G4):
                        for n in range(2):
                            ins = pe.matmul(y_ps[:, b * P:(b + 1) * P], mid[:, n, b * P:(b + 1) * P], w2[:, n, :],
                                            start=(n == 0), stop=(n == 1))
                    ins.then_inc(y_ready, 1)

            @block.scalar
            def _(act):
                act.wait_ge(loaded, 64)
                act.sem_inc(y_ready, 1)
                with act.Fori(0, k.NG) as g:
                    act.wait_ge(y_ready, g + 1)
                    for n in range(2):
                        act.wait_ge(z_ready, 2 * g + n + 1)
                        act.activation(mid[:, n, :], z_ps[n][:], ACT.Relu, bias=b1[:, n:n + 1]).then_inc(mid_ready, 1)

            @block.vector
            def _(v):
                v.wait_ge(loaded, 64)
                with v.Fori(0, k.NG) as g:
                    ch = Chain(v, chain, g * 2)
                    at = ds(g * GN, GN)
                    v.tensor_tensor(acc[:, at], acc[:, at], m.hT[:, at], ALU.add).then_inc(sum_ready, 1)
                    v.wait_ge(y_ready, g + 2)
                    add_to_x(v, m, g, y_ps, bias, ch)
                    ch.close(2)
def build(nc, k):
    k.NC, k.NB, k.NG, k.NW = k.T // C, k.NP // P, k.NP // GN, k.NP // W_WIDE
    m = Names()
    m.semaphores = []

    def sbuf(ctx, name, shape, dt=F32):
        return ctx.enter_context(nc.sbuf_tensor("m_" + name, shape, dt))

    def nodes(ctx, layer):
        m.x = sbuf(ctx, f"x_{layer}", [P, k.NB, P])
        m.hT = sbuf(ctx, f"hT_{layer}", [P, k.NP])

    with ExitStack() as whole:
        m.src_idx = sbuf(whole, "src_idx", [P, k.T], I32)
        m.dst_f = sbuf(whole, "dst_f", [P, k.T])
        m.loc_f = sbuf(whole, "loc_f", [P, k.T])
        m.base_i = sbuf(whole, "base_i", [1, k.T], I32)
        m.rel_i = sbuf(whole, "rel_i", [1, k.T], I32)
        m.narrow_i = sbuf(whole, "narrow_i", [1, 1], I32)
        m.iota_i = sbuf(whole, "iota_i", [P, P], I32)
        m.iota_f = sbuf(whole, "iota_f", [P, P])
        m.iota_w = sbuf(whole, "iota_w", [P, P])
        m.part_i = sbuf(whole, "part_i", [P, 1], I32)
        m.part_f = sbuf(whole, "part_f", [P, 1])
        m.ident = sbuf(whole, "ident", [P, P])
        m.ones = sbuf(whole, "ones", [P, P])
        m.eps = sbuf(whole, "eps", [P, 1])
        with ExitStack() as layer:
            m.tl = sbuf(layer, "tl", [P, 3, k.T])
            m.ws_rep, m.wd_rep = sbuf(layer, "ws_rep", [P, P]), sbuf(layer, "wd_rep", [P, P])
            ad = sbuf(layer, "ad", [P, k.NP])
            with ExitStack() as first:
                m.src_lo, m.as_part = sbuf(first, "src_lo", [P, k.T]), sbuf(first, "as_part", [k.NB, 3, P], BF16)
                with ExitStack() as su:
                    m.base_f = sbuf(su, "base_f", [P, k.T])
                    setup_phase(nc, k, m)
                with ExitStack() as ctx:
                    nodes(ctx, 0)
                    load_nodes(nc, k, m, "l0_", k.dram["x_in"])
                    norm_phase(nc, k, m, "n0_", k.table[0])
                    attention_tables_phase(nc, k, m, ad)
                    keep_nodes(nc, k, m, "k0_", k.dram["x_dram"], k.dram["hT_dram"])
                s_el = sbuf(first, "s_el", [P, k.T])
                lookup_phase(nc, k, m, s_el)
                segment_max_phase(nc, k, m, s_el)
            clear_semaphores(nc, m)
            acc = sbuf(layer, "acc0", [P, 3, k.NP])
            attention_edges(nc, k, m, acc, ad)
            with ExitStack() as ctx:
                nodes(ctx, 1)
                load_nodes(nc, k, m, "l1_", k.dram["x_dram"], k.dram["hT_dram"])
                attention_output(nc, k, m, acc, ad)
                norm_phase(nc, k, m, "n1_", k.table[1])
                key_phase(nc, k, m)
                keep_nodes(nc, k, m, "k1_", k.dram["x_dram"], k.dram["hT_dram"])
        clear_semaphores(nc, m)
        with ExitStack() as layer:
            acc = sbuf(layer, "acc1", [P, HEADS, k.NP])
            factor = sbuf(layer, "factor", [P, k.NB, HEADS])
            with ExitStack() as ctx:
                top = sbuf(ctx, "top", [HEADS, 1])
                den = sbuf(ctx, "den", [P, HEADS])
                shift_row = sbuf(ctx, "shift_row", [HEADS, k.NP])
                softmax_edges(nc, k, m, acc, shift_row, top, den)
                factor_phase(nc, k, m, shift_row, top, den, factor)
            with ExitStack() as ctx:
                nodes(ctx, 2)
                load_nodes(nc, k, m, "l2_", k.dram["x_dram"], k.dram["hT_dram"])
                softmax_output(nc, k, m, acc, factor)
                norm_phase(nc, k, m, "n2_")
                product_phase(nc, k, m)
                keep_nodes(nc, k, m, "k2_", k.dram["x_dram"])
        clear_semaphores(nc, m)
        with ExitStack() as layer:
            acc = sbuf(layer, "acc2", [P, k.NP])
            filter_edges(nc, k, m, acc)
            with ExitStack() as ctx:
                nodes(ctx, 3)
                load_nodes(nc, k, m, "l3_", k.dram["x_dram"])
                filter_output(nc, k, m, acc)
                norm_phase(nc, k, m, "n3_", k.table[3])
                keep_nodes(nc, k, m, "k3_", k.dram["x_dram"], k.dram["hT_dram"])
        clear_semaphores(nc, m)
        with ExitStack() as layer:
            acc = sbuf(layer, "acc3", [P, k.NP])
            sum_edges(nc, k, m, "e3_", acc, k.table[3])
            with ExitStack() as ctx:
                nodes(ctx, 4)
                load_nodes(nc, k, m, "l4_", k.dram["x_dram"], k.dram["hT_dram"])
                perceptron_output(nc, k, m, acc)
                keep_nodes(nc, k, m, "k4_", k.dram["out"])
        clear_semaphores(nc, m)


def kernel(**inputs):
    from concourse import bacc
    from concourse.bass_utils import run_bass_kernel_spmd

    a = {name: np.asarray(value) for name, value in inputs.items()}
    N, E = a["x"].shape[0], a["src"].shape[0]
    NP, T = padded(N, E)
    EP = T * P
    x = np.zeros((NP, P), np.float32)
    x[:N] = a["x"]
    src = np.zeros(EP, np.int32)
    src[:E] = a["src"]
    dst = np.full(EP, NP, np.int32)
    dst[:E] = a["dst"]
    edge = np.zeros((P, EP), np.float32)
    edge[:, :E] = a["edge_attr_128"].T
    heads = lambda w: w.reshape(HEADS, P, P)
    arrays = {
        "x_in": x, "src_tl": src.reshape(T, P).T, "dst_tl": dst.reshape(T, P).T,
        "dst_first": dst.reshape(T, P)[:, 0], "dst_last": dst.reshape(T, P)[:, -1],
        "src_el": src.reshape(P, T), "src_el_t": src.reshape(P, T).T.reshape(P, T), "dst_el": dst.reshape(P, T),
        "dst_before": np.concatenate([np.full(1, -1, np.int32), dst[:-1]]).reshape(P, T),
        "dst_after": np.concatenate([dst[1:], np.full(1, NP + 1, np.int32)]).reshape(P, T),
        "edge_T": edge,
        "W0": a["L0_gnn_W"], "W0T": a["L0_gnn_W"].T, "att_src": a["L0_gnn_att_src"], "att_dst": a["L0_gnn_att_dst"],
        "bias0": a["L0_gnn_bias"],
        "Wq": a["L1_gnn_Wq"].transpose(1, 0, 2), "Wk": a["L1_gnn_Wk"].transpose(1, 0, 2),
        "WqT": a["L1_gnn_Wq"].transpose(2, 0, 1), "gamma": a["L1_gnn_gamma"], "beta": a["L1_gnn_beta"],
        "WrT": a["L1_gnn_Wr"].T, "br": a["L1_gnn_br"],
        "WoT": a["L1_gnn_Wo"].T.reshape(HEADS, P, P).transpose(1, 0, 2), "bo": a["L1_gnn_bo"],
        "WnT": a["L2_gnn_W_node"].T, "b_node": a["L2_gnn_b_node"], "We1T": a["L2_gnn_W_e1"].T, "b_e1": a["L2_gnn_b_e1"],
        "We2T": a["L2_gnn_W_e2"].T, "b_e2": a["L2_gnn_b_e2"], "Wf1T": a["L2_gnn_W_fc1"].T, "b_fc1": a["L2_gnn_b_fc1"],
        "Wf2T": a["L2_gnn_W_fc2"].T, "b_fc2": a["L2_gnn_b_fc2"],
        "W1": a["L3_gnn_W1"], "b1": a["L3_gnn_b1"].reshape(2, P).T, "W2": a["L3_gnn_W2"].reshape(2, P, P).transpose(1, 0, 2),
        "b2": a["L3_gnn_b2"],
    }
    arrays = {name: np.ascontiguousarray(value) for name, value in arrays.items()}
    nc = bacc.Bacc("TRN2", target_bir_lowering=False, num_devices=1)
    k = Names()
    k.N, k.NP, k.T = N, NP, T
    k.dram = {name: nc.dram_tensor(name, value.shape, mybir.dt.from_np(value.dtype), kind="ExternalInput").ap()
              for name, value in arrays.items()}
    k.dram["out"] = nc.dram_tensor("out", (NP, P), F32, kind="ExternalOutput").ap()
    scratch = {"x_dram": ((NP, P), F32), "hT_dram": ((P, NP), F32), "key_dram": ((P, HEADS, NP), F32), "as_dram": ((NP,), F32),
               "el_dram": ((3, EP), F32), "hi_dram": ((EP,), BF16)}
    for name, (shape, dt) in scratch.items():
        k.dram[name] = nc.dram_tensor(name, shape, dt).ap()
    k.table = [nc.dram_tensor(f"table{n}", (NP, P), F32).ap() for n in range(4)]
    build(nc, k)
    result = run_bass_kernel_spmd(nc, [arrays], core_ids=[0])
    return result.results[0]["out"][:N]
```

```python
from contextlib import ExitStack

import numpy as np

import concourse.bass as bass
from concourse import mybir

P = 128
C = 8
RING = 4
W_NARROW = 16
W_WIDE = 128
CW = 128
G4 = 4
GN = G4 * P
HEADS = 4
BIG = 1.0e30
START = -1.0e29
EPS = 1e-5
SLOPE = 0.2
LOG2 = float(np.log(2.0))

F32 = mybir.dt.float32
BF16 = mybir.dt.bfloat16
I32 = mybir.dt.int32
ALU = mybir.AluOpType
ACT = mybir.ActivationFunctionType
AX = mybir.AxisListType
ENG = mybir.EngineType
ds = bass.ds


def padded(n_nodes, n_edges):
    nodes = -(-(n_nodes + CW) // GN) * GN
    tiles = -(-n_edges // (P * 2 * C)) * 2 * C
    return nodes, tiles


class Names:
    pass


class Chain:

    def __init__(self, eng, sem, before=0):
        self.eng, self.sem, self.before, self.n = eng, sem, before, 0

    def add(self, ins):
        ins.then_inc(self.sem, 1)
        self.n += 1
        return ins

    def wait(self):
        self.eng.wait_ge(self.sem, self.before + self.n)

    def step(self, ins):
        self.add(ins)
        self.wait()

    def close(self, count):
        self.wait()
        assert self.n == count, (self.n, count)


def over(ap, shape):
    return ap.unsqueeze(2).to_broadcast(shape)


def new_semaphore(nc, m, name):
    semaphore = nc.alloc_semaphore(name)
    m.semaphores.append(semaphore)
    return semaphore


def clear_semaphores(nc, m):
    nc.clear_and_free_semaphores(m.semaphores)
    nc.all_engine_barrier()
    m.semaphores = []


def setup_phase(nc, k, m):
    T, NP, N = k.T, k.NP, k.N
    with ExitStack() as ctx:
        sb = lambda n, s, d: ctx.enter_context(nc.sbuf_tensor(n, s, d))
        sem = lambda n: new_semaphore(nc, m, n)
        dst_i = sb("su_dst", [P, T], I32)
        first_i = sb("su_first", [P, T], I32)
        last_i = sb("su_last", [1, T], I32)
        hi_i = sb("su_hi", [P, T], I32)
        hi_b = sb("su_hib", [P, T], BF16)
        lo_i = sb("su_lo", [P, T], I32)
        span = sb("su_span", [1, 2, T], F32)
        most = sb("su_most", [1, 4], F32)
        loaded = sem("su_loaded")
        hi_ready = sem("su_hi_ready")
        iotas = sem("su_iotas")
        chain = sem("su_chain")
        stored = sem("su_stored")
        pool_chain = sem("su_pool")
        with nc.Block() as block:
            @block.sync
            def _(sp):
                sp.dma_start(dst_i[:], k.dram["dst_tl"]).then_inc(loaded, 16)
                sp.dma_start(first_i[:], k.dram["dst_first"].partition_broadcast(P)).then_inc(loaded, 16)
                sp.dma_start(last_i[:], k.dram["dst_last"].unsqueeze(0)).then_inc(loaded, 16)
                sp.dma_start(hi_i[:], k.dram["src_el_t"]).then_inc(loaded, 16)
                sp.dma_start(lo_i[:], k.dram["src_el"]).then_inc(loaded, 16)
                sp.dma_start(m.src_idx[:], k.dram["src_tl"]).then_inc(loaded, 16)
                sp.wait_ge(hi_ready, 1)
                sp.dma_start(k.dram["hi_dram"].rearrange("(p t) -> p t", p=P), hi_b[:]).then_inc(stored, 16)
                sp.wait_ge(stored, 16)
                sp.wait_ge(loaded, 96)

            @block.gpsimd
            def _(pool):
                ch = Chain(pool, pool_chain)
                ch.add(pool.iota(m.iota_i[:], [[1, P]], base=0, channel_multiplier=0))
                ch.add(pool.iota(m.part_i[:], [[0, 1]], base=0, channel_multiplier=1))
                ch.step(pool.memset(m.ident[:], 0.0))
                ch.step(pool.affine_select(out=m.ident[:], in_=m.ident[:], compare_op=ALU.not_equal, fill=1.0,
                                           base=0, pattern=[[-1, P]], channel_multiplier=1))
                ch.step(pool.memset(m.eps[:], EPS))
                pool.memset(m.ones[:], 1.0).then_inc(iotas, 1)

            @block.vector
            def _(v):
                ch = Chain(v, chain)
                v.wait_ge(loaded, 96)
                ch.step(v.tensor_scalar(hi_i[:], hi_i[:], 7, None, ALU.logical_shift_right))
                v.tensor_copy(hi_b[:], hi_i[:]).then_inc(hi_ready, 1)
                ch.step(v.tensor_scalar(lo_i[:], lo_i[:], P - 1, None, ALU.bitwise_and))
                ch.add(v.tensor_copy(m.src_lo[:], lo_i[:]))
                ch.add(v.tensor_copy(m.dst_f[:], dst_i[:]))
                ch.step(v.tensor_copy(m.base_f[:], first_i[:]))
                ch.step(v.tensor_scalar(m.base_f[:], m.base_f[:], float(N - 1), None, ALU.min))
                ch.add(v.tensor_tensor(m.loc_f[:], m.dst_f[:], m.base_f[:], ALU.subtract))
                ch.add(v.tensor_copy(m.base_i[:], m.base_f[0:1, :]))
                ch.step(v.tensor_copy(span[:, 0, :], last_i[:]))
                ch.step(v.tensor_scalar(span[:, 0, :], span[:, 0, :], float(N - 1), None, ALU.min))
                ch.step(v.tensor_tensor(span[:, 0, :], span[:, 0, :], m.base_f[0:1, :], ALU.subtract))
                ch.step(v.tensor_reduce(most[:, 0:1], span[:, 0, :], AX.X, ALU.max))
                first_of = m.base_f[0:1, :].rearrange("p (c t) -> p c t", t=C)
                ch.step(v.tensor_tensor(span[:, 1, :].rearrange("p (c t) -> p c t", t=C), first_of,
                                        first_of[:, :, 0:1].to_broadcast([1, T // C, C]), ALU.subtract))
                ch.add(v.tensor_copy(m.rel_i[:], span[:, 1, :]))
                ch.step(v.tensor_reduce(most[:, 1:2], span[:, 1, :], AX.X, ALU.max))
                ch.add(v.tensor_scalar(most[:, 2:3], most[:, 0:1], float(W_NARROW - 1), None, ALU.is_le))
                ch.step(v.tensor_scalar(most[:, 3:4], most[:, 1:2], float(CW - W_NARROW), None, ALU.is_le))
                ch.step(v.tensor_tensor(most[:, 0:1], most[:, 2:3], most[:, 3:4], ALU.mult))
                ch.step(v.tensor_copy(m.narrow_i[:], most[:, 0:1]))
                v.wait_ge(pool_chain, 2)
                ch.add(v.tensor_copy(m.iota_f[:], m.iota_i[:]))
                ch.add(v.tensor_copy(m.iota_w[:], m.iota_i[:]))
                ch.add(v.tensor_copy(m.part_f[:], m.part_i[:]))
                ch.wait()
                v.wait_ge(iotas, 1)


def mean_and_var(v, ch, stats, mv, count):
    mean, var = mv[:, :, 0], mv[:, :, 1]
    ch.step(v.tensor_tensor(var, stats[:, :, 1], stats[:, :, 4], ALU.subtract))
    ch.step(v.scalar_tensor_tensor(var, var, count / 4.0, var, ALU.mult, ALU.mult))
    ch.step(v.tensor_tensor(var, var, stats[:, :, 2], ALU.add))
    ch.step(v.tensor_tensor(var, var, stats[:, :, 5], ALU.add))
    ch.add(v.tensor_tensor(mean, stats[:, :, 1], stats[:, :, 4], ALU.add))
    ch.wait()
    ch.add(v.tensor_scalar(mean, mean, 0.5, None, ALU.mult))
    ch.step(v.tensor_scalar(var, var, 1.0 / count, None, ALU.mult))


def norm_phase(nc, k, m, name, table=None):
    NB, NG = k.NB, k.NG
    with ExitStack() as ctx:
        sb = lambda n, s, d: ctx.enter_context(nc.sbuf_tensor(name + n, s, d))
        sem = lambda n: new_semaphore(nc, m, name + n)
        stats = sb("stats", [P, NB, 6], F32)
        mv = sb("mv", [P, NB, 2], F32)
        rstd = sb("rstd", [P, NB], F32)
        shift = sb("shift", [P, NB], F32)
        h = [sb(f"h{b}", [P, 2, P], F32) for b in range(2)]
        t_ps = [ctx.enter_context(nc.psum_tensor(f"{name}t_ps{b}", [P, 512], F32)) for b in range(2)]
        chain, var_ready, std_ready, shift_ready = sem("chain"), sem("var_ready"), sem("std_ready"), sem("shift_ready")
        h_ready, h_read, t_ready, t_free = sem("h_ready"), sem("h_read"), sem("t_ready"), sem("t_free")
        stored = [sem(f"stored{b}") for b in range(2)]
        with nc.Block() as block:
            @block.vector
            def _(v):
                with v.Fori(0, NG) as g:
                    for b in range(G4):
                        v.bn_stats(stats[:, ds(g * G4 + b, 1), :], m.x[:, ds(g * G4 + b, 1), :]).then_inc(chain, 1)
                ch = Chain(v, chain, NG * G4)
                ch.wait()
                mean_and_var(v, ch, stats[:], mv[:], P)
                v.sem_inc(var_ready, 1)
                v.wait_ge(std_ready, 1)
                ch.step(v.reciprocal(rstd[:], rstd[:]))
                v.scalar_tensor_tensor(shift[:], mv[:, :, 0], -1.0, rstd[:], ALU.mult, ALU.mult).then_inc(shift_ready, 1)
                with v.Fori(0, NG) as g:
                    for b in range(2):
                        v.wait_ge(t_ready, g * 2 + b + 1)
                        v.tensor_copy(m.hT[:, ds(g * GN + b * 2 * P, 2 * P)], t_ps[b][:, 0:2 * P]).then_inc(t_free, 1)

            @block.scalar
            def _(act):
                act.wait_ge(var_ready, 1)
                act.activation(rstd[:], mv[:, :, 1], ACT.Sqrt, bias=m.eps[:]).then_inc(std_ready, 1)
                act.wait_ge(shift_ready, 1)
                act.sem_inc(h_read, 2)
                if table is not None:
                    for b in range(2):
                        act.sem_inc(stored[b], 16)
                with act.Fori(0, NG) as g:
                    for b in range(2):
                        act.wait_ge(h_read, g * 2 + b + 1)
                        if table is not None:
                            act.wait_ge(stored[b], g * 16 + 16)
                        for q in range(2):
                            block_no = g * G4 + b * 2 + q
                            act.activation(h[b][:, q, :], m.x[:, ds(block_no, 1), :].rearrange("p a d -> p (a d)"),
                                           ACT.Relu, bias=shift[:, ds(block_no, 1)],
                                           scale=rstd[:, ds(block_no, 1)]).then_inc(h_ready, 1)

            @block.tensor
            def _(pe):
                pe.sem_inc(t_free, 2)
                with pe.Fori(0, NG) as g:
                    for b in range(2):
                        pe.wait_ge(h_ready, g * 4 + 2 * b + 2)
                        pe.wait_ge(t_free, g * 2 + b + 1)
                        pe.transpose(t_ps[b][:, 0:P], h[b][:, 0, :], m.ident[:])
                        pe.transpose(t_ps[b][:, P:2 * P], h[b][:, 1, :], m.ident[:]).then_inc(t_ready, 1)
                        pe.wait_ge(t_ready, g * 2 + b + 1)
                        pe.sem_inc(h_read, 1)

            @block.sync
            def _(sp):
                if table is None:
                    return
                with sp.Fori(0, NG) as g:
                    for b in range(2):
                        sp.wait_ge(h_ready, g * 4 + 2 * b + 2)
                        sp.dma_start(table.rearrange("(n p) d -> p n d", p=P)[:, ds(g * G4 + b * 2, 2), :],
                                     h[b][:]).then_inc(stored[b], 16)
                for b in range(2):
                    sp.wait_ge(stored[b], 16 * (NG + 1))


def attention_tables_phase(nc, k, m, ad):
    NG, NB = k.NG, k.NB
    with ExitStack() as ctx:
        sb = lambda n, s, d: ctx.enter_context(nc.sbuf_tensor("at_" + n, s, d))
        sem = lambda n: new_semaphore(nc, m, "at_" + n)
        ps = lambda n: ctx.enter_context(nc.psum_tensor("at_" + n, [P, 512], F32))
        wT = sb("wT", [P, P], F32)
        att = sb("att", [P, 2], F32)
        row = sb("row", [1, k.NP], F32)
        a = sb("a", [NB, P], F32)
        part = sb("part", [NB, P], F32)
        w_ps, s_ps, d_ps = ps("w_ps"), [ps(f"s_ps{b}") for b in range(1)], ps("d_ps")
        loaded, w_ready, rep_ready, rows_ready = sem("loaded"), sem("w_ready"), sem("rep_ready"), sem("rows_ready")
        copied, moved, chain = sem("copied"), sem("moved"), sem("chain")
        with nc.Block() as block:
            @block.sync
            def _(sp):
                sp.dma_start(wT[:], k.dram["W0T"]).then_inc(loaded, 16)
                sp.dma_start(att[:, 0:1], k.dram["att_src"].unsqueeze(1)).then_inc(loaded, 16)
                sp.dma_start(att[:, 1:2], k.dram["att_dst"].unsqueeze(1)).then_inc(loaded, 16)
                sp.wait_ge(copied, 2 * NG + 2)
                sp.dma_start(k.dram["as_dram"].unsqueeze(0), row[:]).then_inc(moved, 16)
                sp.wait_ge(moved, 16)
                sp.dma_start(a[:], k.dram["as_dram"].rearrange("(b n) -> b n", n=P)).then_inc(moved, 16)
                sp.wait_ge(moved, 32)

            @block.tensor
            def _(pe):
                pe.wait_ge(loaded, 48)
                pe.matmul(w_ps[:, 0:2], wT[:], att[:], start=True, stop=True).then_inc(w_ready, 1)
                pe.wait_ge(rep_ready, 2)
                pe.sem_inc(copied, 2)
                with pe.Fori(0, NG) as g:
                    pe.wait_ge(copied, 2 * g + 2)
                    pe.matmul(s_ps[0][:], m.ws_rep[:], m.hT[:, ds(g * GN, GN)], start=True, stop=True)
                    pe.matmul(d_ps[:], m.wd_rep[:], m.hT[:, ds(g * GN, GN)], start=True,
                              stop=True).then_inc(rows_ready, 1)

            @block.vector
            def _(v):
                v.wait_ge(w_ready, 1)
                v.tensor_scalar(m.ws_rep[:], m.ones[:], w_ps[:, 0:1], None, ALU.mult).then_inc(rep_ready, 1)
                v.tensor_scalar(m.wd_rep[:], m.ones[:], w_ps[:, 1:2], None, ALU.mult).then_inc(rep_ready, 1)
                with v.Fori(0, NG) as g:
                    v.wait_ge(rows_ready, g + 1)
                    v.tensor_copy(row[:, ds(g * GN, GN)], s_ps[0][0:1, :]).then_inc(copied, 1)
                    v.tensor_copy(ad[:, ds(g * GN, GN)], d_ps[:]).then_inc(copied, 1)
                v.wait_ge(moved, 32)
                ch = Chain(v, chain)
                ch.step(v.tensor_copy(m.as_part[:, 0, :], a[:]))
                ch.step(v.tensor_tensor(a[:], a[:], m.as_part[:, 0, :], ALU.subtract))
                ch.step(v.tensor_copy(m.as_part[:, 1, :], a[:]))
                ch.step(v.tensor_tensor(a[:], a[:], m.as_part[:, 1, :], ALU.subtract))
                ch.step(v.tensor_copy(m.as_part[:, 2, :], a[:]))


def lookup_phase(nc, k, m, s_el):
    NB, T = k.NB, k.T
    L = 8
    with ExitStack() as ctx:
        sb = lambda n, s, d: ctx.enter_context(nc.sbuf_tensor("lu_" + n, s, d))
        sem = lambda n: new_semaphore(nc, m, "lu_" + n)
        hi = [sb(f"hi{b}", [NB, L * P], BF16) for b in range(2)]
        onehot = [sb(f"onehot{b}", [NB, L * P], BF16) for b in range(2)]
        picked = [sb(f"picked{b}", [P, L], F32) for b in range(2)]
        masked = sb("masked", [P, L, P], F32)
        lo = [sb(f"lo{b}", [P, L], F32) for b in range(2)]
        block_ps = [ctx.enter_context(nc.psum_tensor(f"lu_ps{b}", [P, L * P], F32)) for b in range(2)]
        hi_ready, hi_free = [sem(f"hi_ready{b}") for b in range(2)], sem("hi_free")
        onehot_ready, onehot_free, block_ready, block_free = (sem(n) for n in ("oh_ready", "oh_free", "b_ready", "b_free"))
        picks, kept, lo_ready = sem("picks"), sem("kept"), sem("lo_ready")
        hi_rows = k.dram["hi_dram"].partition_broadcast(NB)
        steps = T // L
        with nc.Block() as block:
            @block.sync
            def _(sp):
                with sp.Fori(0, steps // 2) as i:
                    for b in range(2):
                        sp.wait_ge(hi_free, 2 * i + b + 1)
                        sp.dma_start(hi[b][:], hi_rows[:, ds((2 * i + b) * L * P, L * P)]).then_inc(hi_ready[b], 16)

            @block.vector
            def _(v):
                v.sem_inc(hi_free, 2)
                def make(i, b):
                    v.wait_ge(hi_ready[b], 16 * i + 16)
                    v.wait_ge(onehot_free, 2 * i + b + 1)
                    v.tensor_scalar(onehot[b][:], hi[b][:], m.part_f[0:NB, :], None, ALU.is_equal).then_inc(onehot_ready, 1)
                    v.wait_ge(onehot_ready, 2 * i + b + 1)
                    v.sem_inc(hi_free, 1)

                def pick(i, b):
                    c = 2 * i + b
                    v.tensor_copy(lo[b][:], m.src_lo[:, ds(c * L, L)]).then_inc(lo_ready, 1)
                    v.wait_ge(block_ready, c + 1)
                    v.wait_ge(lo_ready, c + 1)
                    for q in range(L):
                        v.scalar_tensor_tensor(masked[:, q, :], m.iota_f[:], lo[b][:, q:q + 1],
                                               block_ps[b][:, q * P:(q + 1) * P], ALU.is_equal, ALU.mult,
                                               accum_out=picked[b][:, q:q + 1]).then_inc(picks, 1)
                    v.wait_ge(picks, L * c + L)
                    v.tensor_copy(s_el[:, ds(c * L, L)], picked[b][:]).then_inc(kept, 1)
                    v.sem_inc(block_free, 1)
                    v.wait_ge(kept, c + 1)

                make(0, 0)
                with v.Fori(0, steps // 2 - 1) as i:
                    make(i, 1)
                    pick(i, 0)
                    make(i + 1, 0)
                    pick(i, 1)
                make(steps // 2 - 1, 1)
                pick(steps // 2 - 1, 0)
                pick(steps // 2 - 1, 1)

            @block.tensor
            def _(pe):
                pe.sem_inc(onehot_free, 2)
                pe.sem_inc(block_free, 2)
                with pe.Fori(0, steps // 2) as i:
                    for b in range(2):
                        c = 2 * i + b
                        pe.wait_ge(onehot_ready, c + 1)
                        pe.wait_ge(block_free, c + 1)
                        for q in range(L):
                            for part in range(3):
                                ins = pe.matmul(block_ps[b][:, q * P:(q + 1) * P], onehot[b][:, q * P:(q + 1) * P],
                                                m.as_part[:, part, :], start=(part == 0), stop=(part == 2))
                        ins.then_inc(block_ready, 1)
                        pe.wait_ge(block_ready, c + 1)
                        pe.sem_inc(onehot_free, 1)


def segment_max_phase(nc, k, m, s_el):
    T = k.T
    TB = -(-T // P)
    with ExitStack() as ctx:
        sb = lambda n, s, d: ctx.enter_context(nc.sbuf_tensor("sg_" + n, s, d))
        sem = lambda n: new_semaphore(nc, m, "sg_" + n)
        here_i = sb("here_i", [P, T], I32)
        other_i = sb("other_i", [P, 2, T], I32)
        here = sb("here", [P, T], F32)
        other = sb("other", [P, 2, T], F32)
        bars = sb("bars", [P, 2, T], F32)
        run = sb("run", [P, T], F32)
        ends = sb("ends", [P, T], F32)
        most = sb("most", [P, T], F32)
        col = sb("col", [P, 2], F32)
        line = sb("line", [1, 3, P + 1], F32)
        carry = sb("carry", [P, 1], F32)
        rows = [sb(f"rows{n}", [P, P], F32) for n in range(2)]
        line_ps = ctx.enter_context(nc.psum_tensor("sg_line_ps", [P, 512], F32))
        t_ps = [ctx.enter_context(nc.psum_tensor(f"sg_t_ps{b}", [P, 512], F32)) for b in range(2)]
        loaded, chain, cols_ready, lines_ready = sem("loaded"), sem("chain"), sem("cols_ready"), sem("lines_ready")
        carry_out, carry_in, scanned, stored = sem("carry_out"), sem("carry_in"), sem("scanned"), sem("stored")
        row_loaded = [sem(f"row_loaded{b}") for b in range(2)]
        turned, taken = sem("turned"), sem("taken")
        moves = [(n, tb) for n in range(3) for tb in range(TB)]
        with nc.Block() as block:
            @block.sync
            def _(sp):
                sp.dma_start(here_i[:], k.dram["dst_el"]).then_inc(loaded, 16)
                sp.dma_start(other_i[:, 0, :], k.dram["dst_before"]).then_inc(loaded, 16)
                sp.dma_start(other_i[:, 1, :], k.dram["dst_after"]).then_inc(loaded, 16)
                sp.wait_ge(scanned, 1)
                for n, t in enumerate((s_el, most, ends)):
                    sp.dma_start(k.dram["el_dram"][n].rearrange("(p t) -> p t", p=P), t[:]).then_inc(stored, 16)
                sp.wait_ge(stored, 48)
                for i, (n, tb) in enumerate(moves):
                    nt = min(P, T - tb * P)
                    if i >= 2:
                        sp.wait_ge(turned, i - 1)
                    sp.dma_start(rows[i % 2][0:nt, :], k.dram["el_dram"][n].rearrange("(t p) -> t p", p=P)[tb * P:tb * P + nt, :]
                                 ).then_inc(row_loaded[i % 2], 16)

            @block.tensor
            def _(pe):
                for n in range(2):
                    pe.wait_ge(cols_ready, n + 1)
                    pe.matmul(line_ps[0:1, 0:P], col[:, 0:1], m.ident[:], start=True, stop=True)
                    pe.matmul(line_ps[0:1, P:2 * P], col[:, 1:2], m.ident[:], start=True, stop=True
                              ).then_inc(lines_ready, 1)
                    pe.wait_ge(carry_out, n + 1)
                    c0 = 0 if n == 0 else 1
                    pe.matmul(line_ps[:, 2 * P:2 * P + 1], line[:, 2, c0:c0 + P], m.ones[0:1, 0:1], start=True, stop=True
                              ).then_inc(carry_in, 1)
                for i, (n, tb) in enumerate(moves):
                    nt = min(P, T - tb * P)
                    pe.wait_ge(row_loaded[i % 2], 16 * (i // 2 + 1))
                    if i >= 2:
                        pe.wait_ge(taken, i - 1)
                    pe.transpose(t_ps[i % 2][:, 0:nt], rows[i % 2][0:nt, :], m.ident[0:nt, 0:nt]).then_inc(turned, 1)

            @block.vector
            def _(v):
                ch = Chain(v, chain)
                v.wait_ge(loaded, 48)
                ch.add(v.tensor_copy(here[:], here_i[:]))
                ch.step(v.tensor_copy(other[:], other_i[:]))
                for n in range(2):
                    ch.step(v.tensor_tensor(other[:, n, :], other[:, n, :], here[:], ALU.not_equal))
                    ch.step(v.tensor_scalar(bars[:, n, :], other[:, n, :], -BIG, None, ALU.mult))
                for n in range(2):
                    back = slice(None, None, -1) if n else slice(None)
                    data = (s_el, run)[n]
                    out = (run, most)[n]
                    ch.step(v.tensor_tensor_scan(out[:, back], bars[:, n, back], data[:, back], -BIG, ALU.add, ALU.max))
                    edge = 0 if n else T - 1
                    ch.add(v.tensor_copy(col[:, 0:1], out[:, edge:edge + 1]))
                    ch.add(v.tensor_reduce(col[:, 1:2], bars[:, n, :], AX.X, ALU.min))
                    ch.wait()
                    v.sem_inc(cols_ready, 1)
                    v.wait_ge(lines_ready, n + 1)
                    ch.add(v.memset(line[:, 2, :], -BIG))
                    ch.step(v.tensor_copy(line[:, 0:2, 0:P], line_ps[0:1, 0:2 * P].rearrange("p (a b) -> p a b", a=2)))
                    to = line[:, 2, P - 1::-1] if n else line[:, 2, 1:P + 1]
                    ch.step(v.tensor_tensor_scan(to, line[:, 1, P - 1::-1] if n else line[:, 1, 0:P],
                                                 line[:, 0, P - 1::-1] if n else line[:, 0, 0:P], -BIG, ALU.add, ALU.max))
                    v.sem_inc(carry_out, 1)
                    v.wait_ge(carry_in, n + 1)
                    ch.step(v.tensor_copy(carry[:], line_ps[:, 2 * P:2 * P + 1]))
                    ch.step(v.tensor_tensor_scan(out[:, back], bars[:, n, back], data[:, back], carry[:], ALU.add, ALU.max))
                ch.step(v.tensor_tensor(ends[:], most[:], other[:, 1, :], ALU.mult))
                v.sem_inc(scanned, 1)
                for i, (n, tb) in enumerate(moves):
                    nt = min(P, T - tb * P)
                    v.wait_ge(turned, i + 1)
                    v.tensor_copy(m.tl[:, n, tb * P:tb * P + nt], t_ps[i % 2][:, 0:nt]).then_inc(taken, 1)
                v.wait_ge(taken, len(moves))
class At:

    def __init__(self, k, w, i, j):
        turn = i + j // RING
        self.w, self.r, self.b = w, j % RING, j % 2
        self.chunk = turn * RING + self.r
        self.n, self.turn, self.pair = self.chunk, turn, turn * (RING // 2) + self.r // 2
        if w is not None:
            self.n = w * k.NC + self.chunk
            self.turn = w * ((k.NC - self.r + RING - 1) // RING) + turn
            self.pair = w * (k.NC // 2) + self.pair


def steps(eng, k, w, count, body):
    full = count // RING
    with eng.Fori(0, full) as i:
        for j in range(RING):
            body(lambda d, i=i, j=j: At(k, w, i, j + d))
    for j in range(count % RING):
        body(lambda d, j=j: At(k, w, full, j + d))


def over_chunks(eng, k, wide, body):
    if not wide:
        steps(eng, k, None, k.NC, lambda at: body(at(0)))
    else:
        with eng.Fori(0, k.NW) as w:
            steps(eng, k, w, k.NC, lambda at: body(at(0)))


def over_chunks_lagged(eng, k, wide, first, second, per_window=None):
    def both(at):
        first(at(1))
        second(at(0))

    def run(w):
        first(At(k, w, 0, 0))
        steps(eng, k, w, k.NC - 1, both)
        second(At(k, w, 0, k.NC - 1))

    if not wide:
        run(None)
    else:
        with eng.Fori(0, k.NW) as w:
            run(w)
            per_window(w)


def both_paths(eng, m, path):
    narrow = eng.value_load(m.narrow_i[:], min_val=0, max_val=1)
    with eng.If(narrow != 0):
        path(False)
    with eng.Else():
        path(True)


def bases_of(eng, nc, k, table, chunk, w, most=None):
    if w is not None:
        return [w * W_WIDE] * C
    _, values = nc.values_load_multi_w_load_instructions(
        table[0:1, ds(chunk * C, C)], engines=(eng.engine,), min_val=0, max_val=k.N - 1 if most is None else most,
        skip_runtime_bounds_check_because="setup_phase bounds the bases, and takes this path only where the others fit")
    return values


def gather_program(pool, k, m, s, table, wide):
    def chunk_rows(at):
        n, chunk, w, b = at.n, at.chunk, at.w, at.b
        pool.wait_ge(s.rows_free[at.r], at.turn + 1)
        pool.sem_inc(s.idx_seen, 1)
        pool.tensor_copy(s.idx[at.r][:], m.src_idx[:, ds(chunk * C, C)]).then_inc(s.idx_ready, 1)
        pool.wait_ge(s.idx_ready, n + 1)
        pool.sem_inc(s.idx_seen, 1)
        for t in range(C):
            pool.indirect_dma_start(s.rows[at.r][:, t, :], None, table,
                                    bass.IndirectOffsetOnAxis(ap=s.idx[at.r][:, t:t + 1], axis=0)
                                    ).then_inc(s.gathered[at.r], 16)
    over_chunks(pool, k, wide, chunk_rows)


def edge_resources(nc, m, ctx, name):
    sb = lambda n, s, d: ctx.enter_context(nc.sbuf_tensor(name + n, s, d))
    sem = lambda n: new_semaphore(nc, m, name + n)
    s = Names()
    s.idx = [sb(f"idx{b}", [P, C], I32) for b in range(RING)]
    s.rows = [sb(f"rows{b}", [P, C, P], F32) for b in range(RING)]
    s.onehot = [sb(f"onehot{b}", [P, C * W_WIDE], F32) for b in range(2)]
    s.rows_free = [sem(f"rows_free{b}") for b in range(RING)]
    s.gathered = [sem(f"gathered{b}") for b in range(RING)]
    s.idx_ready, s.idx_seen = sem("idx_ready"), sem("idx_seen")
    s.agg_ready, s.agg_free, s.added = sem("agg_ready"), sem("agg_free"), sem("added")
    s.chain = sem("chain")
    return s, sb, sem


def onehot_of(v, m, s, chunk, w, b):
    W = W_NARROW if w is None else W_WIDE
    view = s.onehot[b][:, 0:C * W].rearrange("p (t w) -> p t w", w=W)
    nodes = (m.iota_f if w is None else m.iota_w)[:, 0:W]
    where = (m.loc_f if w is None else m.dst_f)[:, ds(chunk * C, C)]
    return view, v.tensor_tensor(view, nodes.unsqueeze(1).to_broadcast([P, C, W]),
                                 where.unsqueeze(2).to_broadcast([P, C, W]), ALU.is_equal)


def next_window(v, m, chain, w):
    v.tensor_scalar(m.iota_w[:], m.iota_w[:], float(W_WIDE), None, ALU.add).then_inc(chain, 1)
    v.wait_ge(chain, w + 1)


def attention_edges(nc, k, m, acc, ad):
    BANKS = 4
    STEPS = C + 7
    with ExitStack() as ctx:
        s, sb, sem = edge_resources(nc, m, ctx, "e0_")
        masked_all = sb("masked", [P, C * W_WIDE], F32)
        ade = sb("ade", [P, C], F32)
        uv = sb("uv", [P, 2, C], F32)
        diff = sb("diff", [P, C], F32)
        pl = [sb(f"pl{b}", [P, C, 2], F32) for b in range(2)]
        weights = [sb(f"weights{b}", [P, C * 2 * W_WIDE], F32) for b in range(2)]
        agg = [ctx.enter_context(nc.psum_tensor(f"e0_agg{n}", [P, 512], F32)) for n in range(BANKS)]
        diff_ready, p_ready, weights_ready, start = sem("diff_ready"), sem("p_ready"), sem("weights_ready"), sem("start")
        windows = sem("windows")

        def shape(wide):
            W = W_WIDE if wide else W_NARROW
            return W, 512 // (4 * W), C * 4 * W // 512

        with nc.Block() as block:
            @block.gpsimd
            def _(pool):
                both_paths(pool, m, lambda wide: gather_program(pool, k, m, s, k.table[0], wide))

            @block.scalar
            def _(act):
                def p_of(at):
                    n, chunk, w, b = at.n, at.chunk, at.w, at.b
                    act.wait_ge(diff_ready, n + 1)
                    act.activation(pl[b][:, :, 0], diff[:], ACT.Exp).then_inc(p_ready, 1)
                both_paths(act, m, lambda wide: over_chunks(act, k, wide, p_of))

            @block.vector
            def _(v):
                v.memset(acc[:], 0.0).then_inc(start, 1)
                v.wait_ge(start, 1)
                for free in s.rows_free:
                    v.sem_inc(free, 1)

                def path(wide):
                    W, G, per = shape(wide)
                    v.sem_inc(s.agg_free, min(BANKS, 2 * per))

                    def weigh(at):
                        n, chunk, w, b = at.n, at.chunk, at.w, at.b
                        ch = Chain(v, s.chain, n * STEPS)
                        onehot, ins = onehot_of(v, m, s, chunk, w, b)
                        ch.step(ins)
                        masked = masked_all[:, 0:C * W].rearrange("p (t w) -> p t w", w=W)
                        for t, base in enumerate(bases_of(v, nc, k, m.base_i, chunk, w)):
                            ch.add(v.tensor_tensor(masked[:, t, :], onehot[:, t, :], ad[:, ds(base, W)], ALU.mult))
                        ch.wait()
                        ch.step(v.tensor_reduce(ade[:], masked, AX.X, ALU.add))
                        ch.step(v.tensor_tensor(uv[:], m.tl[:, 0:2, ds(chunk * C, C)],
                                                ade[:].unsqueeze(1).to_broadcast([P, 2, C]), ALU.add))
                        ch.step(v.scalar_tensor_tensor(uv[:], uv[:], SLOPE, uv[:], ALU.mult, ALU.max))
                        v.tensor_tensor(diff[:], uv[:, 0, :], uv[:, 1, :], ALU.subtract).then_inc(diff_ready, 1)
                        ch.add(v.tensor_copy(pl[b][:, :, 1], m.tl[:, 2, ds(chunk * C, C)]))
                        v.wait_ge(p_ready, n + 1)
                        ch.wait()
                        both = weights[b][:, 0:C * 2 * W].rearrange("p (t kw) -> p t kw", kw=2 * W)
                        for kind in range(2):
                            ch.add(v.tensor_tensor(both[:, :, kind * W:(kind + 1) * W], onehot,
                                                   pl[b][:, :, kind:kind + 1].to_broadcast([P, C, W]), ALU.mult))
                        ch.close(STEPS)
                        v.sem_inc(weights_ready, 1)

                    def add(at):
                        n, chunk, w, b = at.n, at.chunk, at.w, at.b
                        bases = bases_of(v, nc, k, m.base_i, chunk, w)
                        for g in range(per):
                            v.wait_ge(s.agg_ready, n * per + g + 1)
                            for q in range(G):
                                t = g * G + q
                                window = acc[:, :, ds(bases[t], W)]
                                got = agg[(b * per + g) % BANKS][:, q * 4 * W:q * 4 * W + 3 * W]
                                v.tensor_tensor(window, window, got.rearrange("p (a w) -> p a w", w=W),
                                                ALU.add).then_inc(s.added, 1)
                                v.wait_ge(s.added, n * C + t + 1)
                            v.sem_inc(s.agg_free, 1)
                        v.sem_inc(s.rows_free[at.r], 1)

                    over_chunks_lagged(v, k, wide, weigh, add, lambda w: next_window(v, m, windows, w))
                both_paths(v, m, path)

            @block.tensor
            def _(pe):
                def path(wide):
                    W, G, per = shape(wide)

                    def sums(at):
                        n, chunk, w, b = at.n, at.chunk, at.w, at.b
                        pe.wait_ge(s.gathered[at.r], (at.turn + 1) * 16 * C)
                        pe.wait_ge(weights_ready, n + 1)
                        both = weights[b][:, 0:C * 2 * W].rearrange("p (t kw) -> p t kw", kw=2 * W)
                        for g in range(per):
                            pe.wait_ge(s.agg_free, n * per + g + 1)
                            to = agg[(b * per + g) % BANKS]
                            for q in range(G):
                                t, col = g * G + q, q * 4 * W
                                pe.matmul(to[:, col:col + W], s.rows[at.r][:, t, :], both[:, t, 0:W], start=True, stop=True)
                                ins = pe.matmul(to[:, col + W:col + 3 * W], m.ones[:], both[:, t, :], start=True, stop=True)
                            ins.then_inc(s.agg_ready, 1)
                    over_chunks(pe, k, wide, sums)
                both_paths(pe, m, path)


def reset_windows(v, m, chain):
    v.tensor_copy(m.iota_w[:], m.iota_f[:]).then_inc(chain, 1)
    v.wait_ge(chain, 1)


def sum_edges(nc, k, m, name, acc, table):
    BANKS = 4
    with ExitStack() as ctx:
        s, sb, sem = edge_resources(nc, m, ctx, name)
        agg = [ctx.enter_context(nc.psum_tensor(f"{name}agg{n}", [P, 512], F32)) for n in range(BANKS)]
        onehot_ready, start, windows = sem("onehot_ready"), sem("start"), sem("windows")

        def shape(wide):
            W = W_WIDE if wide else W_NARROW
            G = min(C, 512 // W)
            return W, G, C // G

        with nc.Block() as block:
            @block.gpsimd
            def _(pool):
                both_paths(pool, m, lambda wide: gather_program(pool, k, m, s, table, wide))

            @block.vector
            def _(v):
                reset_windows(v, m, start)
                v.memset(acc[:], 0.0).then_inc(start, 1)
                v.wait_ge(start, 2)
                for free in s.rows_free:
                    v.sem_inc(free, 1)

                def path(wide):
                    W, G, per = shape(wide)
                    v.sem_inc(s.agg_free, min(BANKS, 2 * per))

                    def make(at):
                        n, chunk, w, b = at.n, at.chunk, at.w, at.b
                        onehot_of(v, m, s, chunk, w, b)[1].then_inc(onehot_ready, 1)

                    def add(at):
                        n, chunk, w, b = at.n, at.chunk, at.w, at.b
                        bases = bases_of(v, nc, k, m.base_i, chunk, w)
                        for g in range(per):
                            v.wait_ge(s.agg_ready, n * per + g + 1)
                            for q in range(G):
                                t = g * G + q
                                window = acc[:, ds(bases[t], W)]
                                v.tensor_tensor(window, window, agg[(b * per + g) % BANKS][:, q * W:(q + 1) * W],
                                                ALU.add).then_inc(s.added, 1)
                                v.wait_ge(s.added, n * C + t + 1)
                            v.sem_inc(s.agg_free, 1)
                        v.sem_inc(s.rows_free[at.r], 1)

                    over_chunks_lagged(v, k, wide, make, add, lambda w: next_window(v, m, windows, w))
                both_paths(v, m, path)

            @block.tensor
            def _(pe):
                def path(wide):
                    W, G, per = shape(wide)

                    def sums(at):
                        n, chunk, w, b = at.n, at.chunk, at.w, at.b
                        pe.wait_ge(s.gathered[at.r], (at.turn + 1) * 16 * C)
                        pe.wait_ge(onehot_ready, n + 1)
                        for g in range(per):
                            pe.wait_ge(s.agg_free, n * per + g + 1)
                            to = agg[(b * per + g) % BANKS]
                            for q in range(G):
                                t = g * G + q
                                ins = pe.matmul(to[:, q * W:(q + 1) * W], s.rows[at.r][:, t, :],
                                                s.onehot[b][:, t * W:(t + 1) * W], start=True, stop=True)
                            ins.then_inc(s.agg_ready, 1)
                    over_chunks(pe, k, wide, sums)
                both_paths(pe, m, path)


def filter_edges(nc, k, m, acc):
    BANKS = 4
    E = C * P
    with ExitStack() as ctx:
        s, sb, sem = edge_resources(nc, m, ctx, "e2_")
        w1 = sb("w1", [P, P], F32)
        w2 = sb("w2", [P, P], F32)
        b1 = sb("b1", [P, 1], F32)
        b2 = sb("b2", [1, P], F32)
        edge = [sb(f"edge{b}", [P, E], F32) for b in range(2)]
        low1, low2 = sb("low1", [P, E], F32), sb("low2", [P, E], F32)
        top1, top2 = sb("top1", [P, E], F32), sb("top2", [P, E], F32)
        filt1 = [sb(f"filt1_{b}", [P, E], F32) for b in range(2)]
        message = sb("message", [P, E], F32)
        z1 = ctx.enter_context(nc.psum_tensor("e2_z1", [P, E], F32))
        z2 = ctx.enter_context(nc.psum_tensor("e2_z2", [P, E], F32))
        agg = [ctx.enter_context(nc.psum_tensor(f"e2_agg{n}", [P, 512], F32)) for n in range(BANKS)]
        consts, edge_ready, start, windows = sem("consts"), [sem(f"edge_ready{b}") for b in range(2)], sem("start"), sem("windows")
        z1_ready, z2_ready, z1_free, z2_free = sem("z1_ready"), sem("z2_ready"), sem("z1_free"), sem("z2_free")
        low1_ready, low2_ready, top1_ready, low1_free, low2_free = (sem(n) for n in ("low1_ready", "low2_ready", "top1_ready", "low1_free", "low2_free"))
        filt1_ready, message_ready = sem("filt1_ready"), sem("message_ready")
        low_chain = [sem("low1_chain"), sem("low2_chain")]

        def shape(wide):
            W = W_WIDE if wide else W_NARROW
            G = min(C, 512 // W)
            return W, G, C // G

        with nc.Block() as block:
            @block.sync
            def _(sp):
                for t, d in ((w1, k.dram["We1T"]), (w2, k.dram["We2T"]), (b1, k.dram["b_e1"].unsqueeze(1)), (b2, k.dram["b_e2"].unsqueeze(0))):
                    sp.dma_start(t[:], d).then_inc(consts, 16)

                def load(at):
                    n, chunk, w, b = at.n, at.chunk, at.w, at.b
                    sp.wait_ge(z1_ready, n + 1)
                    sp.dma_start(edge[b][:], k.dram["edge_T"][:, ds(chunk * E, E)]).then_inc(edge_ready[b], 16)
                both_paths(sp, m, lambda wide: over_chunks(sp, k, wide, load))
                sp.wait_ge(consts, 64)

            @block.gpsimd
            def _(pool):
                both_paths(pool, m, lambda wide: gather_program(pool, k, m, s, k.table[2], wide))

            @block.tensor
            def _(pe):
                pe.wait_ge(consts, 64)
                pe.sem_inc(z1_ready, 2)

                def path(wide):
                    W, G, per = shape(wide)

                    def first(at):
                        n, chunk, w, b = at.n, at.chunk, at.w, at.b
                        pe.wait_ge(edge_ready[b], 16 * (at.pair + 1))
                        pe.wait_ge(z1_free, n + 1)
                        for half in range(2):
                            ins = pe.matmul(z1[:, half * 512:(half + 1) * 512], w1[:], edge[b][:, half * 512:(half + 1) * 512],
                                            start=True, stop=True)
                        ins.then_inc(z1_ready, 1)

                    def second(at):
                        n, chunk, w, b = at.n, at.chunk, at.w, at.b
                        pe.wait_ge(z2_free, n + 1)
                        pe.wait_ge(filt1_ready, n + 1)
                        for t in range(C):
                            to = z2[:, t * P:(t + 1) * P]
                            pe.matmul(to, m.ones[0:1, :], b2[:], start=True, stop=False)
                            ins = pe.matmul(to, filt1[b][:, t * P:(t + 1) * P], w2[:], start=False, stop=True)
                        ins.then_inc(z2_ready, 1)
                        pe.wait_ge(message_ready, n + 1)
                        for g in range(per):
                            pe.wait_ge(s.agg_free, n * per + g + 1)
                            to = agg[(b * per + g) % BANKS]
                            for q in range(G):
                                t = g * G + q
                                ins = pe.matmul(to[:, q * W:(q + 1) * W], message[:, t * P:(t + 1) * P],
                                                s.onehot[b][:, t * W:(t + 1) * W], start=True, stop=True)
                            ins.then_inc(s.agg_ready, 1)
                    over_chunks_lagged(pe, k, wide, first, second, lambda w: None)
                both_paths(pe, m, path)

            @block.scalar
            def _(act):
                act.preload_act_table_set("natural_log_exp_and_others")
                act.wait_ge(consts, 64)

                def low_part(z, low, bias, ready, n, chain):
                    ch = Chain(act, chain, n * 2)
                    ch.step(act.activation(low[:], z[:], ACT.Abs, bias=bias))
                    ch.step(act.activation(low[:], low[:], ACT.Exp, scale=-1.0))
                    act.activation(low[:], low[:], ACT.Ln, bias=1.0).then_inc(ready, 1)

                def first(at):
                    n, chunk, w, b = at.n, at.chunk, at.w, at.b
                    act.wait_ge(z1_ready, n + 3)
                    act.wait_ge(low1_free, n + 1)
                    low_part(z1, low1, b1[:], low1_ready, n, low_chain[0])

                def second(at):
                    n, chunk, w, b = at.n, at.chunk, at.w, at.b
                    act.wait_ge(z2_ready, n + 1)
                    act.wait_ge(low2_free, n + 1)
                    low_part(z2, low2, 0.0, low2_ready, n, low_chain[1])
                both_paths(act, m, lambda wide: over_chunks_lagged(act, k, wide, first, second, lambda w: None))

            @block.vector
            def _(v):
                v.wait_ge(consts, 64)
                reset_windows(v, m, start)
                v.memset(acc[:], 0.0).then_inc(start, 1)
                v.wait_ge(start, 2)
                for free, count in (*((free, 1) for free in s.rows_free), (z1_free, 1), (z2_free, 1), (low1_free, 1), (low2_free, 1)):
                    v.sem_inc(free, count)

                def path(wide):
                    W, G, per = shape(wide)
                    v.sem_inc(s.agg_free, min(BANKS, 2 * per))

                    def first(at):
                        n, chunk, w, b = at.n, at.chunk, at.w, at.b
                        v.wait_ge(low_chain[0], 2 * n + 1)
                        v.tensor_scalar(top1[:], z1[:], b1[:], 0.0, ALU.add, ALU.max).then_inc(top1_ready, 1)
                        v.wait_ge(low1_ready, n + 1)
                        v.wait_ge(top1_ready, n + 1)
                        v.sem_inc(z1_free, 1)
                        v.scalar_tensor_tensor(filt1[b][:], low1[:], -LOG2, top1[:], ALU.add, ALU.add).then_inc(filt1_ready, 1)
                        v.wait_ge(filt1_ready, n + 1)
                        v.sem_inc(low1_free, 1)

                    def second(at):
                        n, chunk, w, b = at.n, at.chunk, at.w, at.b
                        ch = Chain(v, s.chain, n * 4)
                        ch.add(onehot_of(v, m, s, chunk, w, b)[1])
                        v.wait_ge(low_chain[1], 2 * n + 1)
                        ch.add(v.tensor_scalar(top2[:], z2[:], 0.0, None, ALU.max))
                        v.wait_ge(low2_ready, n + 1)
                        ch.wait()
                        v.sem_inc(z2_free, 1)
                        ch.step(v.tensor_tensor(top2[:], low2[:], top2[:], ALU.add))
                        v.sem_inc(low2_free, 1)
                        v.wait_ge(s.gathered[at.r], (at.turn + 1) * 16 * C)
                        ch.step(v.scalar_tensor_tensor(message[:], top2[:], -LOG2, s.rows[at.r][:].rearrange("p t d -> p (t d)"),
                                                       ALU.add, ALU.mult))
                        ch.close(4)
                        v.sem_inc(message_ready, 1)
                        v.sem_inc(s.rows_free[at.r], 1)
                        bases = bases_of(v, nc, k, m.base_i, chunk, w)
                        for g in range(per):
                            v.wait_ge(s.agg_ready, n * per + g + 1)
                            for q in range(G):
                                t = g * G + q
                                window = acc[:, ds(bases[t], W)]
                                v.tensor_tensor(window, window, agg[(b * per + g) % BANKS][:, q * W:(q + 1) * W],
                                                ALU.add).then_inc(s.added, 1)
                                v.wait_ge(s.added, n * C + t + 1)
                            v.sem_inc(s.agg_free, 1)
                    over_chunks_lagged(v, k, wide, first, second, lambda w: next_window(v, m, windows, w))
                both_paths(v, m, path)


def softmax_edges(nc, k, m, acc, shift_row, top, den):
    SHIFTS = 9
    with ExitStack() as ctx:
        s, sb, sem = edge_resources(nc, m, ctx, "e1_")
        ps = lambda n: ctx.enter_context(nc.psum_tensor("e1_" + n, [P, 512], F32))
        key = [sb(f"key{b}", [P, HEADS, CW], F32) for b in range(2)]
        rows_T = sb("rows_T", [P, C, P], F32)
        masked = [sb(f"masked{b}", [P, 512], F32) for b in range(2)]
        weights = [sb(f"weights{b}", [P, 512], F32) for b in range(2)]
        logit = sb("logit", [P, C, HEADS], F32)
        member = sb("member", [P, C], F32)
        p = sb("p", [P, C, HEADS], F32)
        p_sum = sb("p_sum", [P, HEADS], F32)
        col_max = sb("col_max", [P, HEADS], F32)
        new_max = sb("new_max", [HEADS, 1], F32)
        diag = sb("diag", [HEADS, HEADS], F32)
        top_all = [sb(f"top_all{b}", [P, HEADS], F32) for b in range(2)]
        fade = [sb(f"fade{b}", [P, HEADS], F32) for b in range(2)]
        t_ps = [ps(f"t{n}") for n in range(2)]
        x_ps = [ps(f"x{n}") for n in range(2)]
        agg = [ps(f"agg{n}") for n in range(2)]
        max_ps = ps("max")
        key_ready, key_free = [sem(f"key_ready{b}") for b in range(2)], sem("key_free")
        turned, rows_T_ready, rows_T_free = sem("turned"), sem("rows_T_ready"), sem("rows_T_free")
        x_ready, x_free, logits_chain = sem("x_ready"), sem("x_free"), sem("logits_chain")
        col_ready, col_turned, diag_ready, top_ready = sem("col_ready"), sem("col_turned"), sem("diag_ready"), sem("top_ready")
        shifted, p_ready, weights_ready, weights_chain = sem("shifted"), sem("p_ready"), sem("weights_ready"), sem("weights_chain")
        start, windows = sem("start"), sem("windows")

        def shape(wide):
            W = W_WIDE if wide else W_NARROW
            return W, 512 // (HEADS * W), C * HEADS * W // 512

        def walk(eng, begin, work, finish):
            begin(At(k, None, 0, 0))
            work(At(k, None, 0, 0), None, At(k, None, 0, 1))
            steps(eng, k, None, k.NC - 2, lambda at: work(at(1), at(0), at(2)))
            work(At(k, None, 0, k.NC - 1), At(k, None, 0, k.NC - 2), None)
            finish(At(k, None, 0, k.NC - 1))

        with nc.Block() as block:
            @block.sync
            def _(sp):
                def load(at):
                    n, chunk, w, b = at.n, at.chunk, at.w, at.b
                    sp.wait_ge(key_free, n + 1)
                    if w is None:
                        base = sp.value_load(m.base_i[0:1, ds(chunk * C, 1)], min_val=0, max_val=k.N - 1)
                        sp.dma_start(key[b][:], k.dram["key_dram"][:, :, ds(base, CW)]).then_inc(key_ready[b], 16)
                    else:
                        sp.dma_start(key[b][:, :, 0:W_WIDE], k.dram["key_dram"][:, :, ds(w * W_WIDE, W_WIDE)]).then_inc(key_ready[b], 16)
                both_paths(sp, m, lambda wide: over_chunks(sp, k, wide, load))

            @block.gpsimd
            def _(pool):
                both_paths(pool, m, lambda wide: gather_program(pool, k, m, s, k.table[1], wide))

            @block.scalar
            def _(act):
                def take_rows(at):
                    act.wait_ge(rows_T_free, at.n + 1)
                    for half in range(2):
                        act.wait_ge(turned, 2 * at.n + half + 1)
                        act.activation(rows_T[:, half * 4:half * 4 + 4, :].rearrange("p t d -> p (t d)"), t_ps[half][:],
                                       ACT.Copy).then_inc(rows_T_ready, 1)

                def exponents(at):
                    act.wait_ge(shifted, at.n + 1)
                    act.activation(p[:], p[:], ACT.Exp).then_inc(p_ready, 1)
                    act.activation(fade[at.b][:], fade[at.b][:], ACT.Exp).then_inc(p_ready, 1)

                def work(now, last, following):
                    if following:
                        take_rows(following)
                    exponents(now)

                def both(at):
                    take_rows(at)
                    exponents(at)
                both_paths(act, m, lambda wide: over_chunks(act, k, wide, both) if wide
                           else walk(act, take_rows, work, lambda at: None))

            @block.tensor
            def _(pe):
                def path(wide):
                    W, G, per = shape(wide)

                    def turn_rows(at):
                        pe.wait_ge(s.gathered[at.r], (at.turn + 1) * 16 * C)
                        pe.wait_ge(rows_T_free, at.n + 1)
                        for half in range(2):
                            for q in range(4):
                                ins = pe.transpose(t_ps[half][:, q * P:(q + 1) * P], s.rows[at.r][:, half * 4 + q, :], m.ident[:])
                            ins.then_inc(turned, 1)

                    def products(at):
                        pe.wait_ge(key_ready[at.b], 16 * (at.pair + 1))
                        rel = bases_of(pe, nc, k, m.rel_i, at.chunk, at.w, CW - W_NARROW) if at.w is None else [0] * C
                        for g in range(per):
                            pe.wait_ge(x_free, at.n * per + g + 1)
                            to = x_ps[(at.b * per + g) % 2]
                            for q in range(G):
                                t = g * G + q
                                if t % 4 == 0 or q == 0:
                                    pe.wait_ge(rows_T_ready, 2 * at.n + t // 4 + 1)
                                ins = pe.matmul(to[:, q * HEADS * W:(q + 1) * HEADS * W], rows_T[:, t, :],
                                                key[at.b][:, :, ds(rel[t], W)], start=True, stop=True)
                            ins.then_inc(x_ready, 1)

                    def turn_maximum(at):
                        pe.wait_ge(col_ready, at.n + 1)
                        pe.transpose(max_ps[0:HEADS, 0:P], col_max[:], m.ident[:]).then_inc(col_turned, 1)

                    def spread_maximum(at):
                        pe.wait_ge(diag_ready, at.n + 1)
                        pe.matmul(max_ps[:, P:P + HEADS], m.ones[0:HEADS, :], diag[:], start=True, stop=True).then_inc(top_ready, 1)

                    def sums(at):
                        for g in range(per):
                            pe.wait_ge(weights_ready, at.n * per + g + 1)
                            pe.wait_ge(s.agg_free, at.n * per + g + 1)
                            of = (at.b * per + g) % 2
                            for q in range(G):
                                cols = slice(q * HEADS * W, (q + 1) * HEADS * W)
                                ins = pe.matmul(agg[of][:, cols], s.rows[at.r][:, g * G + q, :], weights[of][:, cols],
                                                start=True, stop=True)
                            ins.then_inc(s.agg_ready, 1)

                    def begin(at):
                        turn_rows(at)
                        products(at)

                    def work(now, last, following):
                        if following:
                            turn_rows(following)
                        turn_maximum(now)
                        if following:
                            products(following)
                        spread_maximum(now)
                        sums(now)

                    def one(at):
                        begin(at)
                        work(at, None, None)

                    if wide:
                        over_chunks(pe, k, wide, one)
                    else:
                        walk(pe, begin, work, lambda at: None)
                both_paths(pe, m, path)

            @block.vector
            def _(v):
                reset_windows(v, m, start)
                for t, value in ((acc, 0.0), (shift_row, START), (top, START), (den, 0.0), (top_all[1], START)):
                    v.memset(t[:], value).then_inc(start, 1)
                v.wait_ge(start, 6)
                for free in s.rows_free:
                    v.sem_inc(free, 1)
                for free, count in ((key_free, 2), (rows_T_free, 1), (x_free, 2), (s.agg_free, 2)):
                    v.sem_inc(free, count)

                def path(wide):
                    W, G, per = shape(wide)
                    LOGITS = 2 + 2 * per + 2 + wide

                    def make(at):
                        ch = Chain(v, logits_chain, at.n * LOGITS)
                        onehot, ins = onehot_of(v, m, s, at.chunk, at.w, at.b)
                        if wide:
                            ch.step(ins)
                            ch.step(v.tensor_reduce(member[:], onehot, AX.X, ALU.add))
                            ch.step(v.tensor_scalar(member[:], member[:], -1.0, BIG, ALU.add, ALU.mult))
                        else:
                            ch.add(ins)
                            ch.step(v.tensor_scalar(member[:], m.loc_f[:, ds(at.chunk * C, C)], float(W), -BIG, ALU.is_ge, ALU.mult))

                    def logits(at):
                        ch = Chain(v, logits_chain, at.n * LOGITS + 2 + wide)
                        onehot = s.onehot[at.b][:, 0:C * W].rearrange("p (t w) -> p t w", w=W)
                        for g in range(per):
                            v.wait_ge(x_ready, at.n * per + g + 1)
                            if g == per - 1:
                                v.sem_inc(rows_T_free, 1)
                                v.sem_inc(key_free, 1)
                            t, of = slice(g * G, (g + 1) * G), (at.b * per + g) % 2
                            part = masked[of][:].rearrange("p (t h w) -> p t h w", h=HEADS, w=W)
                            ch.step(v.tensor_tensor(part, x_ps[of][:].rearrange("p (t h w) -> p t h w", h=HEADS, w=W),
                                                    onehot[:, t, :].unsqueeze(2).to_broadcast([P, G, HEADS, W]), ALU.mult))
                            v.sem_inc(x_free, 1)
                            ch.add(v.tensor_reduce(logit[:, t, :], part, AX.X, ALU.add))
                        ch.wait()
                        ch.step(v.tensor_tensor(logit[:], logit[:], over(member[:], [P, C, HEADS]), ALU.add))
                        ch.step(v.tensor_reduce(col_max[:], logit[:].rearrange("p t h -> p h t"), AX.X, ALU.max))
                        ch.close(LOGITS - 2 - wide)
                        v.sem_inc(col_ready, 1)

                    def maximum(at):
                        ch = Chain(v, s.chain, at.n * SHIFTS)
                        v.wait_ge(col_turned, at.n + 1)
                        ch.step(v.tensor_reduce(new_max[:], max_ps[0:HEADS, 0:P], AX.X, ALU.max))
                        ch.step(v.tensor_tensor(top[:], top[:], new_max[:], ALU.max))
                        ch.step(v.tensor_scalar(diag[:], m.ident[0:HEADS, 0:HEADS], top[:], None, ALU.mult))
                        v.sem_inc(diag_ready, 1)

                    def shift(at):
                        ch = Chain(v, s.chain, at.n * SHIFTS + 3)
                        if wide:
                            span = shift_row[:, ds(at.w * W_WIDE, W_WIDE)]
                        else:
                            base = v.value_load(m.base_i[0:1, ds(at.chunk * C, 1)], min_val=0, max_val=k.N - 1)
                            span = shift_row[:, ds(base, CW)]
                        size = W_WIDE if wide else CW
                        ch.add(v.tensor_scalar(span, m.ones[0:HEADS, 0:1].to_broadcast([HEADS, size]), top[:], None, ALU.mult))
                        v.wait_ge(top_ready, at.n + 1)
                        ch.step(v.tensor_copy(top_all[at.b][:], max_ps[:, P:P + HEADS]))
                        ch.add(v.tensor_tensor(p[:], logit[:], top_all[at.b][:].unsqueeze(1).to_broadcast([P, C, HEADS]), ALU.subtract))
                        v.tensor_tensor(fade[at.b][:], top_all[1 - at.b][:], top_all[at.b][:], ALU.subtract).then_inc(shifted, 1)
                        ch.wait()

                    def build(at, g):
                        onehot = s.onehot[at.b][:, 0:C * W].rearrange("p (t w) -> p t w", w=W)
                        out = weights[(at.b * per + g) % 2][:].rearrange("p (t h w) -> p t h w", h=HEADS, w=W)
                        t = slice(g * G, (g + 1) * G)
                        v.tensor_tensor(out, onehot[:, t, :].unsqueeze(2).to_broadcast([P, G, HEADS, W]),
                                        p[:, t, :].unsqueeze(3).to_broadcast([P, G, HEADS, W]), ALU.mult).then_inc(weights_ready, 1)

                    def total(at):
                        ch = Chain(v, s.chain, at.n * SHIFTS + 6)
                        ch.add(v.tensor_reduce(p_sum[:], p[:].rearrange("p t h -> p h t"), AX.X, ALU.add))
                        ch.step(v.tensor_tensor(den[:], den[:], fade[at.b][:], ALU.mult))
                        ch.step(v.tensor_tensor(den[:], den[:], p_sum[:], ALU.add))
                        ch.close(SHIFTS - 6)

                    def add(at):
                        bases = bases_of(v, nc, k, m.base_i, at.chunk, at.w)
                        window = acc[:, :, ds(bases[0], W)]
                        v.tensor_tensor(window, window, over(fade[at.b][:], [P, HEADS, W]), ALU.mult).then_inc(s.added, 1)
                        v.wait_ge(s.added, at.n * (C + 1) + 1)
                        for g in range(per):
                            if wide:
                                build(at, g)
                            v.wait_ge(s.agg_ready, at.n * per + g + 1)
                            for q in range(G):
                                t = g * G + q
                                window = acc[:, :, ds(bases[t], W)]
                                got = agg[(at.b * per + g) % 2][:, q * HEADS * W:(q + 1) * HEADS * W]
                                v.tensor_tensor(window, window, got.rearrange("p (h w) -> p h w", w=W), ALU.add).then_inc(s.added, 1)
                                v.wait_ge(s.added, at.n * (C + 1) + t + 2)
                            v.sem_inc(s.agg_free, 1)
                        v.sem_inc(s.rows_free[at.r], 1)

                    def work(now, last, following):
                        logits(now)
                        if last:
                            add(last)
                        maximum(now)
                        if following:
                            make(following)
                        shift(now)
                        v.wait_ge(p_ready, 2 * now.n + 2)
                        if not wide:
                            build(now, 0)
                        total(now)

                    def one(at):
                        make(at)
                        work(at, None, None)
                        add(at)

                    if wide:
                        with v.Fori(0, k.NW) as w:
                            steps(v, k, w, k.NC, lambda at: one(at(0)))
                            next_window(v, m, windows, w)
                    else:
                        assert per == 1
                        walk(v, make, work, add)
                both_paths(v, m, path)
class Node:

    def __init__(self, nc, ctx, k, m, name):
        self.nc, self.ctx, self.k, self.m, self.name = nc, ctx, k, m, name

    def sb(self, n, shape, dt=F32):
        return self.ctx.enter_context(self.nc.sbuf_tensor(self.name + n, shape, dt))

    def ps(self, n):
        return self.ctx.enter_context(self.nc.psum_tensor(self.name + n, [P, 512], F32))

    def sem(self, n):
        return new_semaphore(self.nc, self.m, self.name + n)


def load_nodes(nc, k, m, name, x_from, hT_from=None):
    with ExitStack() as ctx:
        loaded = new_semaphore(nc, m, name + "loaded")
        with nc.Block() as block:
            @block.sync
            def _(sp):
                sp.dma_start(m.x[:], x_from.rearrange("(n p) d -> p n d", p=P)).then_inc(loaded, 16)
                if hT_from is not None:
                    sp.dma_start(m.hT[:], hT_from).then_inc(loaded, 16)
                sp.wait_ge(loaded, 32 if hT_from is not None else 16)


def keep_nodes(nc, k, m, name, x_to, hT_to=None):
    with ExitStack() as ctx:
        kept = new_semaphore(nc, m, name + "kept")
        with nc.Block() as block:
            @block.sync
            def _(sp):
                sp.dma_start(x_to.rearrange("(n p) d -> p n d", p=P), m.x[:]).then_inc(kept, 16)
                if hT_to is not None:
                    sp.dma_start(hT_to, m.hT[:]).then_inc(kept, 16)
                sp.wait_ge(kept, 32 if hT_to is not None else 16)


def add_to_x(v, m, g, y, bias, ch):
    x = m.x[:, ds(g * G4, G4), :]
    ch.step(v.tensor_tensor(x, x, y[:].rearrange("p (b d) -> p b d", b=G4), ALU.add))
    ch.step(v.tensor_tensor(x, x, bias[:].unsqueeze(1).to_broadcast([P, G4, P]), ALU.add))


def attention_output(nc, k, m, acc, ad):
    STEPS = 16
    with ExitStack() as ctx:
        a = Node(nc, ctx, k, m, "o0_")
        w, bias = a.sb("w", [P, P]), a.sb("bias", [P, P])
        e = a.sb("e", [P, 2, GN])
        top, whole, mixed = a.sb("top", [P, GN]), a.sb("whole", [P, GN]), a.sb("mixed", [P, GN])
        own_ps, y_ps = a.ps("own"), a.ps("y")
        loaded, own_ready, own_free, chain = a.sem("loaded"), a.sem("own_ready"), a.sem("own_free"), a.sem("chain")
        shifted, factors, mixed_ready, y_ready = a.sem("shifted"), a.sem("factors"), a.sem("mixed_ready"), a.sem("y_ready")
        with nc.Block() as block:
            @block.sync
            def _(sp):
                sp.dma_start(w[:], k.dram["W0"]).then_inc(loaded, 16)
                sp.dma_start(bias[:], k.dram["bias0"].partition_broadcast(P)).then_inc(loaded, 16)
                sp.wait_ge(loaded, 32)

            @block.tensor
            def _(pe):
                pe.wait_ge(loaded, 32)
                with pe.Fori(0, k.NG) as g:
                    pe.wait_ge(own_free, g + 1)
                    pe.matmul(own_ps[:], m.ws_rep[:], m.hT[:, ds(g * GN, GN)], start=True, stop=True).then_inc(own_ready, 1)
                    pe.wait_ge(mixed_ready, g + 1)
                    for b in range(G4):
                        ins = pe.matmul(y_ps[:, b * P:(b + 1) * P], mixed[:, b * P:(b + 1) * P], w[:], start=True, stop=True)
                    ins.then_inc(y_ready, 1)

            @block.scalar
            def _(act):
                with act.Fori(0, k.NG) as g:
                    act.wait_ge(shifted, g + 1)
                    act.activation(e[:], e[:], ACT.Exp).then_inc(factors, 1)

            @block.vector
            def _(v):
                v.wait_ge(loaded, 32)
                v.sem_inc(own_free, 1)
                with v.Fori(0, k.NG) as g:
                    ch = Chain(v, chain, g * STEPS)
                    at = ds(g * GN, GN)
                    v.wait_ge(own_ready, g + 1)
                    ch.add(v.tensor_tensor(e[:, 1, :], own_ps[:], ad[:, at], ALU.add))
                    ch.step(v.tensor_scalar(e[:, 0, :], acc[:, 1, at], 0.0, -BIG, ALU.is_equal, ALU.mult))
                    v.sem_inc(own_free, 1)
                    ch.step(v.tensor_tensor(e[:, 0, :], e[:, 0, :], acc[:, 2, at], ALU.add))
                    ch.step(v.tensor_tensor(e[:, 0, :], e[:, 0, :], ad[:, at], ALU.add))
                    ch.step(v.scalar_tensor_tensor(e[:], e[:], SLOPE, e[:], ALU.mult, ALU.max))
                    ch.step(v.tensor_tensor(top[:], e[:, 0, :], e[:, 1, :], ALU.max))
                    ch.step(v.tensor_tensor(e[:], e[:], top[:].unsqueeze(1).to_broadcast([P, 2, GN]), ALU.subtract))
                    v.sem_inc(shifted, 1)
                    v.wait_ge(factors, g + 1)
                    ch.add(v.tensor_tensor(mixed[:], acc[:, 0, at], e[:, 0, :], ALU.mult))
                    ch.add(v.tensor_tensor(top[:], m.hT[:, at], e[:, 1, :], ALU.mult))
                    ch.step(v.tensor_tensor(whole[:], acc[:, 1, at], e[:, 0, :], ALU.mult))
                    ch.add(v.tensor_tensor(mixed[:], mixed[:], top[:], ALU.add))
                    ch.step(v.tensor_tensor(whole[:], whole[:], e[:, 1, :], ALU.add))
                    ch.step(v.reciprocal(whole[:], whole[:]))
                    ch.step(v.tensor_tensor(mixed[:], mixed[:], whole[:], ALU.mult))
                    v.sem_inc(mixed_ready, 1)
                    v.wait_ge(y_ready, g + 1)
                    add_to_x(v, m, g, y_ps, bias, ch)
                    ch.close(STEPS)


def key_phase(nc, k, m):
    SCALE = float(P) ** -0.5
    with ExitStack() as ctx:
        a = Node(nc, ctx, k, m, "key_")
        wq, wk, pair = a.sb("wq", [P, HEADS, P]), a.sb("wk", [P, HEADS, P]), a.sb("pair", [P, HEADS, P])
        out = a.sb("out", [P, HEADS, GN])
        pair_ps = a.ps("pair_ps")
        key_ps = [a.ps(f"key_ps{h}") for h in range(HEADS)]
        loaded, pair_ready, pair_kept = a.sem("loaded"), a.sem("pair_ready"), a.sem("pair_kept")
        key_ready, taken, stored = a.sem("key_ready"), a.sem("taken"), a.sem("stored")
        with nc.Block() as block:
            @block.sync
            def _(sp):
                sp.dma_start(wq[:], k.dram["Wq"]).then_inc(loaded, 16)
                sp.dma_start(wk[:], k.dram["Wk"]).then_inc(loaded, 16)
                sp.sem_inc(stored, 16)
                with sp.Fori(0, k.NG) as g:
                    sp.wait_ge(taken, HEADS * (g + 1) + HEADS)
                    sp.dma_start(k.dram["key_dram"][:, :, ds(g * GN, GN)], out[:]).then_inc(stored, 16)
                sp.wait_ge(stored, 16 * (k.NG + 1))

            @block.tensor
            def _(pe):
                pe.wait_ge(loaded, 32)
                for h in range(HEADS):
                    ins = pe.matmul(pair_ps[:, h * P:(h + 1) * P], wk[:, h, :], wq[:, h, :], start=True, stop=True)
                ins.then_inc(pair_ready, 1)
                pe.wait_ge(pair_kept, 1)
                pe.sem_inc(taken, HEADS)
                with pe.Fori(0, k.NG) as g:
                    pe.wait_ge(taken, HEADS * (g + 1))
                    for h in range(HEADS):
                        pe.matmul(key_ps[h][:], pair[:, h, :], m.hT[:, ds(g * GN, GN)], start=True, stop=True
                                  ).then_inc(key_ready, 1)

            @block.vector
            def _(v):
                v.wait_ge(pair_ready, 1)
                v.tensor_scalar(pair[:].rearrange("p h d -> p (h d)"), pair_ps[:], SCALE, None, ALU.mult).then_inc(pair_kept, 1)
                with v.Fori(0, k.NG) as g:
                    v.wait_ge(stored, 16 * (g + 1))
                    for h in range(2):
                        v.wait_ge(key_ready, HEADS * g + h + 1)
                        v.tensor_copy(out[:, h, :], key_ps[h][:]).then_inc(taken, 1)

            @block.scalar
            def _(act):
                with act.Fori(0, k.NG) as g:
                    act.wait_ge(stored, 16 * (g + 1))
                    for h in range(2, 4):
                        act.wait_ge(key_ready, HEADS * g + h + 1)
                        act.activation(out[:, h, :], key_ps[h][:], ACT.Copy).then_inc(taken, 1)


def factor_phase(nc, k, m, shift_row, top, den, factor):
    with ExitStack() as ctx:
        a = Node(nc, ctx, k, m, "fa_")
        negative, inverse = a.sb("negative", [HEADS, 1]), a.sb("inverse", [P, HEADS])
        f_ps, den_ps = a.ps("f_ps"), a.ps("den_ps")
        den_ready, top_ready, row_ready, cols_ready, taken, chain = (
            a.sem(n) for n in ("den_ready", "top_ready", "row_ready", "cols_ready", "taken", "chain"))
        static = a.sb("static", [HEADS, GN])
        with nc.Block() as block:
            @block.tensor
            def _(pe):
                pe.matmul(den_ps[:, 0:HEADS], m.ones[:], den[:], start=True, stop=True).then_inc(den_ready, 1)
                with pe.Fori(0, k.NG) as g:
                    pe.wait_ge(row_ready, g + 1)
                    for b in range(G4):
                        ins = pe.matmul(f_ps[:, b * HEADS:(b + 1) * HEADS], static[:, b * P:(b + 1) * P],
                                        m.ident[0:HEADS, 0:HEADS], start=True, stop=True)
                    ins.then_inc(cols_ready, 1)

            @block.scalar
            def _(act):
                act.wait_ge(top_ready, 1)
                act.sem_inc(taken, 1)
                with act.Fori(0, k.NG) as g:
                    act.wait_ge(taken, g + 1)
                    act.activation(static[:], shift_row[:, ds(g * GN, GN)], ACT.Exp, bias=negative[:]).then_inc(row_ready, 1)

            @block.vector
            def _(v):
                v.tensor_scalar(negative[:], top[:], -1.0, None, ALU.mult).then_inc(top_ready, 1)
                v.wait_ge(den_ready, 1)
                v.reciprocal(inverse[:], den_ps[:, 0:HEADS]).then_inc(chain, 1)
                v.wait_ge(chain, 1)
                with v.Fori(0, k.NG) as g:
                    v.wait_ge(cols_ready, g + 1)
                    v.tensor_tensor(factor[:, ds(g * G4, G4), :], f_ps[:, 0:G4 * HEADS].rearrange("p (b h) -> p b h", h=HEADS),
                                    inverse[:].unsqueeze(1).to_broadcast([P, G4, HEADS]), ALU.mult).then_inc(taken, 1)


def softmax_output(nc, k, m, acc, factor):
    F = HEADS * P
    STEPS = 21
    with ExitStack() as ctx:
        a = Node(nc, ctx, k, m, "o1_")
        wq, wr, wo = a.sb("wq", [P, HEADS, P]), a.sb("wr", [P, F]), a.sb("wo", [P, HEADS, P])
        bo, gamma, beta, br = a.sb("bo", [P, P]), a.sb("gamma", [P, F]), a.sb("beta", [P, F]), a.sb("br", [P, F])
        sums, h_T, h_rows = a.sb("sums", [P, HEADS, P]), a.sb("h_T", [P, P]), a.sb("h_rows", [P, P])
        heads, gate, joined_T = a.sb("heads", [P, F]), a.sb("gate", [P, F]), a.sb("joined_T", [P, F])
        fac = a.sb("fac", [P, HEADS])
        stats, mv, rstd = a.sb("stats", [P, 1, 6]), a.sb("mv", [P, 1, 2]), a.sb("rstd", [P, 1])
        heads_ps, h_ps, res_ps, t_ps, y_ps = (a.ps(n) for n in ("heads_ps", "h_ps", "res_ps", "t_ps", "y_ps"))
        loaded, copied, sums_ready, chain, act_chain = (a.sem(n) for n in ("loaded", "copied", "sums_ready", "chain", "act_chain"))
        var_ready, shift_ready, gate_ready, affine, joined_ready, turned, joined_T_ready, y_ready, done = (
            a.sem(n) for n in ("var_ready", "shift_ready", "gate_ready", "affine", "joined_ready", "turned", "joined_T_ready",
                               "y_ready", "done"))
        parts = ((wq, k.dram["WqT"]), (wr, k.dram["WrT"]), (wo, k.dram["WoT"]), (bo, k.dram["bo"].partition_broadcast(P)), (gamma, k.dram["gamma"].partition_broadcast(P)),
                 (beta, k.dram["beta"].partition_broadcast(P)), (br, k.dram["br"].partition_broadcast(P)))
        with nc.Block() as block:
            @block.sync
            def _(sp):
                for t, d in parts:
                    sp.dma_start(t[:], d).then_inc(loaded, 16)
                sp.wait_ge(loaded, 16 * len(parts))

            @block.scalar
            def _(act):
                act.preload_act_table_set("natural_log_exp_and_others")
                act.wait_ge(loaded, 16 * len(parts))
                with act.Fori(0, k.NB) as n:
                    act.wait_ge(done, n + 1)
                    act.activation(sums[:], acc[:, :, ds(n * P, P)], ACT.Copy).then_inc(copied, 1)
                    act.activation(h_T[:], m.hT[:, ds(n * P, P)], ACT.Copy).then_inc(copied, 1)
                    act.wait_ge(sums_ready, n + 1)
                    act.activation(h_rows[:], h_ps[:, 0:P], ACT.Copy).then_inc(copied, 1)
                    ch = Chain(act, act_chain, n * 4)
                    act.wait_ge(var_ready, n + 1)
                    ch.step(act.activation(rstd[:], mv[:, :, 1], ACT.Ln, bias=m.eps[:]))
                    ch.step(act.activation(rstd[:], rstd[:], ACT.Exp, scale=-0.5))
                    act.sem_inc(shift_ready, 1)
                    act.wait_ge(affine, n + 1)
                    ch.step(act.activation(gate[:], heads[:], ACT.Exp, scale=-1.0))
                    ch.step(act.activation(gate[:], gate[:], ACT.Ln, bias=1.0))
                    act.activation(gate[:], gate[:], ACT.Exp, scale=-1.0).then_inc(gate_ready, 1)
                    act.wait_ge(turned, n + 1)
                    act.activation(joined_T[:], t_ps[:], ACT.Copy).then_inc(joined_T_ready, 1)

            @block.tensor
            def _(pe):
                pe.wait_ge(loaded, 16 * len(parts))
                with pe.Fori(0, k.NB) as n:
                    pe.wait_ge(copied, 3 * n + 2)
                    pe.wait_ge(done, n + 1)
                    for h in range(HEADS):
                        pe.matmul(heads_ps[:, h * P:(h + 1) * P], sums[:, h, :], wq[:, h, :], start=True, stop=True)
                    pe.transpose(h_ps[:, 0:P], h_T[:], m.ident[:])
                    pe.matmul(res_ps[:], h_T[:], wr[:], start=True, stop=True).then_inc(sums_ready, 1)
                    pe.wait_ge(joined_ready, n + 1)
                    for h in range(HEADS):
                        ins = pe.transpose(t_ps[:, h * P:(h + 1) * P], gate[:, h * P:(h + 1) * P], m.ident[:])
                    ins.then_inc(turned, 1)
                    pe.wait_ge(joined_T_ready, n + 1)
                    for h in range(HEADS):
                        ins = pe.matmul(y_ps[:, 0:P], joined_T[:, h * P:(h + 1) * P], wo[:, h, :],
                                        start=(h == 0), stop=(h == HEADS - 1))
                    ins.then_inc(y_ready, 1)

            @block.vector
            def _(v):
                v.wait_ge(loaded, 16 * len(parts))
                v.sem_inc(done, 1)
                with v.Fori(0, k.NB) as n:
                    ch = Chain(v, chain, n * STEPS)
                    ch.step(v.tensor_copy(fac[:], factor[:, ds(n, 1), :].rearrange("p a h -> p (a h)")))
                    v.wait_ge(sums_ready, n + 1)
                    v.wait_ge(copied, 3 * n + 3)
                    for h in range(HEADS):
                        ch.add(v.scalar_tensor_tensor(heads[:, h * P:(h + 1) * P], heads_ps[:, h * P:(h + 1) * P], fac[:, h:h + 1],
                                                      h_rows[:], ALU.mult, ALU.add))
                    ch.wait()
                    ch.step(v.bn_stats(stats[:, 0, :], heads[:]))
                    mean_and_var(v, ch, stats[:], mv[:], F)
                    v.sem_inc(var_ready, 1)
                    v.wait_ge(shift_ready, n + 1)
                    ch.step(v.tensor_scalar(heads[:], heads[:], mv[:, 0, 0:1], rstd[:], ALU.subtract, ALU.mult))
                    ch.step(v.tensor_tensor(heads[:], heads[:], gamma[:], ALU.mult))
                    ch.step(v.tensor_tensor(heads[:], heads[:], beta[:], ALU.add))
                    v.sem_inc(affine, 1)
                    v.wait_ge(gate_ready, n + 1)
                    ch.step(v.tensor_tensor(gate[:], gate[:], heads[:], ALU.mult))
                    ch.step(v.tensor_tensor(gate[:], gate[:], res_ps[:], ALU.add))
                    ch.step(v.tensor_tensor(gate[:], gate[:], br[:], ALU.add))
                    v.sem_inc(joined_ready, 1)
                    v.wait_ge(y_ready, n + 1)
                    x = m.x[:, ds(n, 1), :].rearrange("p a d -> p (a d)")
                    ch.step(v.tensor_tensor(x, x, y_ps[:, 0:P], ALU.add))
                    ch.step(v.tensor_tensor(x, x, bo[:], ALU.add))
                    ch.close(STEPS)
                    v.sem_inc(done, 1)


def product_phase(nc, k, m):
    with ExitStack() as ctx:
        a = Node(nc, ctx, k, m, "pr_")
        w, bias = a.sb("w", [P, P]), a.sb("bias", [P, P])
        h_T, out, y_ps = a.sb("h_T", [P, GN]), a.sb("out", [P, G4, P]), a.ps("y")
        loaded, copied, y_ready, y_free, out_ready, stored = (
            a.sem(n) for n in ("loaded", "copied", "y_ready", "y_free", "out_ready", "stored"))
        with nc.Block() as block:
            @block.sync
            def _(sp):
                sp.dma_start(w[:], k.dram["WnT"]).then_inc(loaded, 16)
                sp.dma_start(bias[:], k.dram["b_node"].partition_broadcast(P)).then_inc(loaded, 16)
                sp.sem_inc(stored, 16)
                with sp.Fori(0, k.NG) as g:
                    sp.wait_ge(out_ready, g + 1)
                    sp.dma_start(k.table[2].rearrange("(n p) d -> p n d", p=P)[:, ds(g * G4, G4), :], out[:]).then_inc(stored, 16)
                sp.wait_ge(stored, 16 * (k.NG + 1))

            @block.scalar
            def _(act):
                act.sem_inc(y_ready, 1)
                with act.Fori(0, k.NG) as g:
                    act.wait_ge(y_ready, g + 1)
                    act.activation(h_T[:], m.hT[:, ds(g * GN, GN)], ACT.Copy).then_inc(copied, 1)

            @block.tensor
            def _(pe):
                pe.wait_ge(loaded, 32)
                pe.sem_inc(y_free, 1)
                with pe.Fori(0, k.NG) as g:
                    pe.wait_ge(copied, g + 1)
                    pe.wait_ge(y_free, g + 1)
                    for b in range(G4):
                        ins = pe.matmul(y_ps[:, b * P:(b + 1) * P], h_T[:, b * P:(b + 1) * P], w[:], start=True, stop=True)
                    ins.then_inc(y_ready, 1)

            @block.vector
            def _(v):
                v.wait_ge(loaded, 32)
                with v.Fori(0, k.NG) as g:
                    v.wait_ge(y_ready, g + 2)
                    v.wait_ge(stored, 16 * (g + 1))
                    v.tensor_tensor(out[:], y_ps[:].rearrange("p (b d) -> p b d", b=G4),
                                    bias[:].unsqueeze(1).to_broadcast([P, G4, P]), ALU.add).then_inc(out_ready, 1)
                    v.wait_ge(out_ready, g + 1)
                    v.sem_inc(y_free, 1)


def filter_output(nc, k, m, acc):
    STEPS = 5
    with ExitStack() as ctx:
        a = Node(nc, ctx, k, m, "o2_")
        w1, w2, b1, bias = a.sb("w1", [P, P]), a.sb("w2", [P, P]), a.sb("b1", [P, 1]), a.sb("bias", [P, P])
        low, top = a.sb("low", [P, GN]), a.sb("top", [P, GN])
        z_ps, y_ps = a.ps("z"), a.ps("y")
        loaded, z_ready, z_free, low_ready, chain, act_chain, mid_ready, y_ready = (
            a.sem(n) for n in ("loaded", "z_ready", "z_free", "low_ready", "chain", "act_chain", "mid_ready", "y_ready"))
        with nc.Block() as block:
            @block.sync
            def _(sp):
                for t, d in ((w1, k.dram["Wf1T"]), (w2, k.dram["Wf2T"]), (b1, k.dram["b_fc1"].unsqueeze(1)), (bias, k.dram["b_fc2"].partition_broadcast(P))):
                    sp.dma_start(t[:], d).then_inc(loaded, 16)
                sp.wait_ge(loaded, 64)

            @block.tensor
            def _(pe):
                pe.wait_ge(loaded, 64)
                with pe.Fori(0, k.NG) as g:
                    pe.wait_ge(z_free, g + 1)
                    pe.matmul(z_ps[:], w1[:], acc[:, ds(g * GN, GN)], start=True, stop=True).then_inc(z_ready, 1)
                    pe.wait_ge(mid_ready, g + 1)
                    for b in range(G4):
                        ins = pe.matmul(y_ps[:, b * P:(b + 1) * P], low[:, b * P:(b + 1) * P], w2[:], start=True, stop=True)
                    ins.then_inc(y_ready, 1)

            @block.scalar
            def _(act):
                act.preload_act_table_set("natural_log_exp_and_others")
                act.wait_ge(loaded, 64)
                act.sem_inc(y_ready, 1)
                with act.Fori(0, k.NG) as g:
                    ch = Chain(act, act_chain, g * 2)
                    act.wait_ge(z_ready, g + 1)
                    act.wait_ge(y_ready, g + 1)
                    ch.step(act.activation(low[:], z_ps[:], ACT.Abs, bias=b1[:]))
                    ch.step(act.activation(low[:], low[:], ACT.Exp, scale=-1.0))
                    act.activation(low[:], low[:], ACT.Ln, bias=1.0).then_inc(low_ready, 1)

            @block.vector
            def _(v):
                v.wait_ge(loaded, 64)
                v.sem_inc(z_free, 1)
                with v.Fori(0, k.NG) as g:
                    ch = Chain(v, chain, g * 4)
                    v.wait_ge(act_chain, 2 * g + 1)
                    ch.add(v.tensor_scalar(top[:], z_ps[:], b1[:], 0.0, ALU.add, ALU.max))
                    v.wait_ge(low_ready, g + 1)
                    ch.wait()
                    v.sem_inc(z_free, 1)
                    ch.step(v.scalar_tensor_tensor(low[:], low[:], -LOG2, top[:], ALU.add, ALU.add))
                    v.sem_inc(mid_ready, 1)
                    v.wait_ge(y_ready, g + 2)
                    add_to_x(v, m, g, y_ps, bias, ch)
                    ch.close(4)


def perceptron_output(nc, k, m, acc):
    with ExitStack() as ctx:
        a = Node(nc, ctx, k, m, "o3_")
        w1, w2, b1, bias = a.sb("w1", [P, 2 * P]), a.sb("w2", [P, 2, P]), a.sb("b1", [P, 2]), a.sb("bias", [P, P])
        mid = a.sb("mid", [P, 2, GN])
        z_ps, y_ps = [a.ps(f"z{n}") for n in range(2)], a.ps("y")
        loaded, sum_ready, z_ready, mid_ready, chain, y_ready = (
            a.sem(n) for n in ("loaded", "sum_ready", "z_ready", "mid_ready", "chain", "y_ready"))
        with nc.Block() as block:
            @block.sync
            def _(sp):
                for t, d in ((w1, k.dram["W1"]), (w2, k.dram["W2"]), (b1, k.dram["b1"]), (bias, k.dram["b2"].partition_broadcast(P))):
                    sp.dma_start(t[:], d).then_inc(loaded, 16)
                sp.wait_ge(loaded, 64)

            @block.tensor
            def _(pe):
                pe.wait_ge(loaded, 64)
                pe.sem_inc(mid_ready, 2)
                with pe.Fori(0, k.NG) as g:
                    pe.wait_ge(sum_ready, g + 1)
                    pe.wait_ge(mid_ready, 2 * g + 2)
                    for n in range(2):
                        pe.matmul(z_ps[n][:], w1[:, n * P:(n + 1) * P], acc[:, ds(g * GN, GN)], start=True, stop=True
                                  ).then_inc(z_ready, 1)
                    pe.wait_ge(mid_ready, 2 * g + 4)
                    for b in range(G4):
                        for n in range(2):
                            ins = pe.matmul(y_ps[:, b * P:(b + 1) * P], mid[:, n, b * P:(b + 1) * P], w2[:, n, :],
                                            start=(n == 0), stop=(n == 1))
                    ins.then_inc(y_ready, 1)

            @block.scalar
            def _(act):
                act.wait_ge(loaded, 64)
                act.sem_inc(y_ready, 1)
                with act.Fori(0, k.NG) as g:
                    act.wait_ge(y_ready, g + 1)
                    for n in range(2):
                        act.wait_ge(z_ready, 2 * g + n + 1)
                        act.activation(mid[:, n, :], z_ps[n][:], ACT.Relu, bias=b1[:, n:n + 1]).then_inc(mid_ready, 1)

            @block.vector
            def _(v):
                v.wait_ge(loaded, 64)
                with v.Fori(0, k.NG) as g:
                    ch = Chain(v, chain, g * 2)
                    at = ds(g * GN, GN)
                    v.tensor_tensor(acc[:, at], acc[:, at], m.hT[:, at], ALU.add).then_inc(sum_ready, 1)
                    v.wait_ge(y_ready, g + 2)
                    add_to_x(v, m, g, y_ps, bias, ch)
                    ch.close(2)
def build(nc, k):
    k.NC, k.NB, k.NG, k.NW = k.T // C, k.NP // P, k.NP // GN, k.NP // W_WIDE
    m = Names()
    m.semaphores = []

    def sbuf(ctx, name, shape, dt=F32):
        return ctx.enter_context(nc.sbuf_tensor("m_" + name, shape, dt))

    def nodes(ctx, layer):
        m.x = sbuf(ctx, f"x_{layer}", [P, k.NB, P])
        m.hT = sbuf(ctx, f"hT_{layer}", [P, k.NP])

    with ExitStack() as whole:
        m.src_idx = sbuf(whole, "src_idx", [P, k.T], I32)
        m.dst_f = sbuf(whole, "dst_f", [P, k.T])
        m.loc_f = sbuf(whole, "loc_f", [P, k.T])
        m.base_i = sbuf(whole, "base_i", [1, k.T], I32)
        m.rel_i = sbuf(whole, "rel_i", [1, k.T], I32)
        m.narrow_i = sbuf(whole, "narrow_i", [1, 1], I32)
        m.iota_i = sbuf(whole, "iota_i", [P, P], I32)
        m.iota_f = sbuf(whole, "iota_f", [P, P])
        m.iota_w = sbuf(whole, "iota_w", [P, P])
        m.part_i = sbuf(whole, "part_i", [P, 1], I32)
        m.part_f = sbuf(whole, "part_f", [P, 1])
        m.ident = sbuf(whole, "ident", [P, P])
        m.ones = sbuf(whole, "ones", [P, P])
        m.eps = sbuf(whole, "eps", [P, 1])
        with ExitStack() as layer:
            m.tl = sbuf(layer, "tl", [P, 3, k.T])
            m.ws_rep, m.wd_rep = sbuf(layer, "ws_rep", [P, P]), sbuf(layer, "wd_rep", [P, P])
            ad = sbuf(layer, "ad", [P, k.NP])
            with ExitStack() as first:
                m.src_lo, m.as_part = sbuf(first, "src_lo", [P, k.T]), sbuf(first, "as_part", [k.NB, 3, P], BF16)
                with ExitStack() as su:
                    m.base_f = sbuf(su, "base_f", [P, k.T])
                    setup_phase(nc, k, m)
                with ExitStack() as ctx:
                    nodes(ctx, 0)
                    load_nodes(nc, k, m, "l0_", k.dram["x_in"])
                    norm_phase(nc, k, m, "n0_", k.table[0])
                    attention_tables_phase(nc, k, m, ad)
                    keep_nodes(nc, k, m, "k0_", k.dram["x_dram"], k.dram["hT_dram"])
                s_el = sbuf(first, "s_el", [P, k.T])
                lookup_phase(nc, k, m, s_el)
                segment_max_phase(nc, k, m, s_el)
            clear_semaphores(nc, m)
            acc = sbuf(layer, "acc0", [P, 3, k.NP])
            attention_edges(nc, k, m, acc, ad)
            with ExitStack() as ctx:
                nodes(ctx, 1)
                load_nodes(nc, k, m, "l1_", k.dram["x_dram"], k.dram["hT_dram"])
                attention_output(nc, k, m, acc, ad)
                norm_phase(nc, k, m, "n1_", k.table[1])
                key_phase(nc, k, m)
                keep_nodes(nc, k, m, "k1_", k.dram["x_dram"], k.dram["hT_dram"])
        clear_semaphores(nc, m)
        with ExitStack() as layer:
            acc = sbuf(layer, "acc1", [P, HEADS, k.NP])
            factor = sbuf(layer, "factor", [P, k.NB, HEADS])
            with ExitStack() as ctx:
                top = sbuf(ctx, "top", [HEADS, 1])
                den = sbuf(ctx, "den", [P, HEADS])
                shift_row = sbuf(ctx, "shift_row", [HEADS, k.NP])
                softmax_edges(nc, k, m, acc, shift_row, top, den)
                factor_phase(nc, k, m, shift_row, top, den, factor)
            with ExitStack() as ctx:
                nodes(ctx, 2)
                load_nodes(nc, k, m, "l2_", k.dram["x_dram"], k.dram["hT_dram"])
                softmax_output(nc, k, m, acc, factor)
                norm_phase(nc, k, m, "n2_")
                product_phase(nc, k, m)
                keep_nodes(nc, k, m, "k2_", k.dram["x_dram"])
        clear_semaphores(nc, m)
        with ExitStack() as layer:
            acc = sbuf(layer, "acc2", [P, k.NP])
            filter_edges(nc, k, m, acc)
            with ExitStack() as ctx:
                nodes(ctx, 3)
                load_nodes(nc, k, m, "l3_", k.dram["x_dram"])
                filter_output(nc, k, m, acc)
                norm_phase(nc, k, m, "n3_", k.table[3])
                keep_nodes(nc, k, m, "k3_", k.dram["x_dram"], k.dram["hT_dram"])
        clear_semaphores(nc, m)
        with ExitStack() as layer:
            acc = sbuf(layer, "acc3", [P, k.NP])
            sum_edges(nc, k, m, "e3_", acc, k.table[3])
            with ExitStack() as ctx:
                nodes(ctx, 4)
                load_nodes(nc, k, m, "l4_", k.dram["x_dram"], k.dram["hT_dram"])
                perceptron_output(nc, k, m, acc)
                keep_nodes(nc, k, m, "k4_", k.dram["out"])
        clear_semaphores(nc, m)


def kernel(**inputs):
    from concourse import bacc
    from concourse.bass_utils import run_bass_kernel_spmd

    a = {name: np.asarray(value) for name, value in inputs.items()}
    N, E = a["x"].shape[0], a["src"].shape[0]
    NP, T = padded(N, E)
    EP = T * P
    x = np.zeros((NP, P), np.float32)
    x[:N] = a["x"]
    src = np.zeros(EP, np.int32)
    src[:E] = a["src"]
    dst = np.full(EP, NP, np.int32)
    dst[:E] = a["dst"]
    edge = np.zeros((P, EP), np.float32)
    edge[:, :E] = a["edge_attr_128"].T
    heads = lambda w: w.reshape(HEADS, P, P)
    arrays = {
        "x_in": x, "src_tl": src.reshape(T, P).T, "dst_tl": dst.reshape(T, P).T,
        "dst_first": dst.reshape(T, P)[:, 0], "dst_last": dst.reshape(T, P)[:, -1],
        "src_el": src.reshape(P, T), "src_el_t": src.reshape(P, T).T.reshape(P, T), "dst_el": dst.reshape(P, T),
        "dst_before": np.concatenate([np.full(1, -1, np.int32), dst[:-1]]).reshape(P, T),
        "dst_after": np.concatenate([dst[1:], np.full(1, NP + 1, np.int32)]).reshape(P, T),
        "edge_T": edge,
        "W0": a["L0_gnn_W"], "W0T": a["L0_gnn_W"].T, "att_src": a["L0_gnn_att_src"], "att_dst": a["L0_gnn_att_dst"],
        "bias0": a["L0_gnn_bias"],
        "Wq": a["L1_gnn_Wq"].transpose(1, 0, 2), "Wk": a["L1_gnn_Wk"].transpose(1, 0, 2),
        "WqT": a["L1_gnn_Wq"].transpose(2, 0, 1), "gamma": a["L1_gnn_gamma"], "beta": a["L1_gnn_beta"],
        "WrT": a["L1_gnn_Wr"].T, "br": a["L1_gnn_br"],
        "WoT": a["L1_gnn_Wo"].T.reshape(HEADS, P, P).transpose(1, 0, 2), "bo": a["L1_gnn_bo"],
        "WnT": a["L2_gnn_W_node"].T, "b_node": a["L2_gnn_b_node"], "We1T": a["L2_gnn_W_e1"].T, "b_e1": a["L2_gnn_b_e1"],
        "We2T": a["L2_gnn_W_e2"].T, "b_e2": a["L2_gnn_b_e2"], "Wf1T": a["L2_gnn_W_fc1"].T, "b_fc1": a["L2_gnn_b_fc1"],
        "Wf2T": a["L2_gnn_W_fc2"].T, "b_fc2": a["L2_gnn_b_fc2"],
        "W1": a["L3_gnn_W1"], "b1": a["L3_gnn_b1"].reshape(2, P).T, "W2": a["L3_gnn_W2"].reshape(2, P, P).transpose(1, 0, 2),
        "b2": a["L3_gnn_b2"],
    }
    arrays = {name: np.ascontiguousarray(value) for name, value in arrays.items()}
    nc = bacc.Bacc("TRN2", target_bir_lowering=False, num_devices=1)
    k = Names()
    k.N, k.NP, k.T = N, NP, T
    k.dram = {name: nc.dram_tensor(name, value.shape, mybir.dt.from_np(value.dtype), kind="ExternalInput").ap()
              for name, value in arrays.items()}
    k.dram["out"] = nc.dram_tensor("out", (NP, P), F32, kind="ExternalOutput").ap()
    scratch = {"x_dram": ((NP, P), F32), "hT_dram": ((P, NP), F32), "key_dram": ((P, HEADS, NP), F32), "as_dram": ((NP,), F32),
               "el_dram": ((3, EP), F32), "hi_dram": ((EP,), BF16)}
    for name, (shape, dt) in scratch.items():
        k.dram[name] = nc.dram_tensor(name, shape, dt).ap()
    k.table = [nc.dram_tensor(f"table{n}", (NP, P), F32).ap() for n in range(4)]
    build(nc, k)
    result = run_bass_kernel_spmd(nc, [arrays], core_ids=[0])
    return result.results[0]["out"][:N]
```

```python
from contextlib import ExitStack

import numpy as np

import concourse.bass as bass
from concourse import mybir

P = 128
C = 8
RING = 4
W_NARROW = 16
CW = 128
G4 = 4
GN = G4 * P
HEADS = 4
BIG = 1.0e30
START = -1.0e29
EPS = 1e-5
SLOPE = 0.2
LOG2 = float(np.log(2.0))

F32 = mybir.dt.float32
BF16 = mybir.dt.bfloat16
I32 = mybir.dt.int32
ALU = mybir.AluOpType
ACT = mybir.ActivationFunctionType
AX = mybir.AxisListType
ENG = mybir.EngineType
ds = bass.ds


def padded(n_nodes, n_edges):
    nodes = -(-(n_nodes + CW) // GN) * GN
    tiles = -(-n_edges // (P * 2 * C)) * 2 * C
    return nodes, tiles


class Names:
    pass


class Chain:

    def __init__(self, eng, sem, before=0):
        self.eng, self.sem, self.before, self.n = eng, sem, before, 0

    def add(self, ins):
        ins.then_inc(self.sem, 1)
        self.n += 1
        return ins

    def wait(self):
        self.eng.wait_ge(self.sem, self.before + self.n)

    def step(self, ins):
        self.add(ins)
        self.wait()

    def close(self, count):
        self.wait()
        assert self.n == count, (self.n, count)


def over(ap, shape):
    return ap.unsqueeze(2).to_broadcast(shape)


def new_semaphore(nc, m, name):
    semaphore = nc.alloc_semaphore(name)
    m.semaphores.append(semaphore)
    return semaphore


def clear_semaphores(nc, m):
    nc.clear_and_free_semaphores(m.semaphores)
    nc.all_engine_barrier()
    m.semaphores = []


def setup_phase(nc, k, m):
    T, NP, N = k.T, k.NP, k.N
    with ExitStack() as ctx:
        sb = lambda n, s, d: ctx.enter_context(nc.sbuf_tensor(n, s, d))
        sem = lambda n: new_semaphore(nc, m, n)
        dst_i = sb("su_dst", [P, T], I32)
        first_i = sb("su_first", [P, T], I32)
        last_i = sb("su_last", [1, T], I32)
        lo_i = sb("su_lo", [P, T], I32)
        lo_b = sb("su_lob", [P, T], BF16)
        hi_i = sb("su_hi", [P, T], I32)
        span = sb("su_span", [1, 2, T], F32)
        most = sb("su_most", [1, 4], F32)
        loaded = sem("su_loaded")
        lo_ready = sem("su_lo_ready")
        iotas = sem("su_iotas")
        chain = sem("su_chain")
        stored = sem("su_stored")
        pool_chain = sem("su_pool")
        with nc.Block() as block:
            @block.sync
            def _(sp):
                sp.dma_start(dst_i[:], k.dram["dst_tl"]).then_inc(loaded, 16)
                sp.dma_start(first_i[:], k.dram["dst_first"].partition_broadcast(P)).then_inc(loaded, 16)
                sp.dma_start(last_i[:], k.dram["dst_last"].unsqueeze(0)).then_inc(loaded, 16)
                sp.dma_start(lo_i[:], k.dram["src_el_t"]).then_inc(loaded, 16)
                sp.dma_start(hi_i[:], k.dram["src_el"]).then_inc(loaded, 16)
                sp.dma_start(m.src_idx[:], k.dram["src_tl"]).then_inc(loaded, 16)
                sp.wait_ge(lo_ready, 1)
                sp.dma_start(k.dram["lo_dram"].rearrange("(p t) -> p t", p=P), lo_b[:]).then_inc(stored, 16)
                sp.wait_ge(stored, 16)
                sp.wait_ge(loaded, 96)

            @block.gpsimd
            def _(pool):
                ch = Chain(pool, pool_chain)
                ch.add(pool.iota(m.iota_i[:], [[1, P]], base=0, channel_multiplier=0))
                ch.add(pool.iota(m.part_i[:], [[0, 1]], base=0, channel_multiplier=1))
                ch.step(pool.memset(m.ident[:], 0.0))
                ch.step(pool.affine_select(out=m.ident[:], in_=m.ident[:], compare_op=ALU.not_equal, fill=1.0,
                                           base=0, pattern=[[-1, P]], channel_multiplier=1))
                ch.step(pool.memset(m.eps[:], EPS))
                ch.step(pool.memset(m.zeros[:], 0.0))
                pool.memset(m.ones[:], 1.0).then_inc(iotas, 1)

            @block.vector
            def _(v):
                ch = Chain(v, chain)
                v.wait_ge(loaded, 96)
                ch.step(v.tensor_scalar(lo_i[:], lo_i[:], P - 1, None, ALU.bitwise_and))
                v.tensor_copy(lo_b[:], lo_i[:]).then_inc(lo_ready, 1)
                ch.step(v.tensor_scalar(hi_i[:], hi_i[:], 7, None, ALU.logical_shift_right))
                ch.add(v.tensor_copy(m.src_hi[:], hi_i[:]))
                ch.add(v.tensor_copy(m.dst_f[:], dst_i[:]))
                ch.step(v.tensor_copy(m.base_f[:], first_i[:]))
                ch.step(v.tensor_scalar(m.base_f[:], m.base_f[:], float(N - 1), None, ALU.min))
                ch.add(v.tensor_tensor(m.loc_f[:], m.dst_f[:], m.base_f[:], ALU.subtract))
                ch.add(v.tensor_copy(m.base_i[:], m.base_f[0:1, :]))
                ch.step(v.tensor_copy(span[:, 0, :], last_i[:]))
                ch.step(v.tensor_scalar(span[:, 0, :], span[:, 0, :], float(N - 1), None, ALU.min))
                ch.step(v.tensor_tensor(span[:, 0, :], span[:, 0, :], m.base_f[0:1, :], ALU.subtract))
                ch.step(v.tensor_reduce(most[:, 0:1], span[:, 0, :], AX.X, ALU.max))
                first_of = m.base_f[0:1, :].rearrange("p (c t) -> p c t", t=C)
                ch.step(v.tensor_tensor(span[:, 1, :].rearrange("p (c t) -> p c t", t=C), first_of,
                                        first_of[:, :, 0:1].to_broadcast([1, T // C, C]), ALU.subtract))
                ch.add(v.tensor_copy(m.rel_i[:], span[:, 1, :]))
                ch.step(v.tensor_reduce(most[:, 1:2], span[:, 1, :], AX.X, ALU.max))
                ch.add(v.tensor_scalar(most[:, 2:3], most[:, 0:1], float(W_NARROW - 1), None, ALU.is_le))
                ch.step(v.tensor_scalar(most[:, 3:4], most[:, 1:2], float(CW - W_NARROW), None, ALU.is_le))
                ch.step(v.tensor_tensor(most[:, 0:1], most[:, 2:3], most[:, 3:4], ALU.mult))
                ch.step(v.tensor_copy(m.narrow_i[:], most[:, 0:1]))
                v.wait_ge(pool_chain, 2)
                ch.add(v.tensor_copy(m.iota_f[:], m.iota_i[:]))
                ch.add(v.tensor_copy(m.iota_w[:], m.iota_i[:]))
                ch.add(v.tensor_copy(m.part_f[:], m.part_i[:]))
                ch.wait()
                v.wait_ge(iotas, 1)


def mean_and_var(v, ch, stats, mv, count):
    mean, var = mv[:, :, 0], mv[:, :, 1]
    ch.step(v.tensor_tensor(var, stats[:, :, 1], stats[:, :, 4], ALU.subtract))
    ch.step(v.scalar_tensor_tensor(var, var, count / 4.0, var, ALU.mult, ALU.mult))
    ch.step(v.tensor_tensor(var, var, stats[:, :, 2], ALU.add))
    ch.step(v.tensor_tensor(var, var, stats[:, :, 5], ALU.add))
    ch.add(v.tensor_tensor(mean, stats[:, :, 1], stats[:, :, 4], ALU.add))
    ch.wait()
    ch.add(v.tensor_scalar(mean, mean, 0.5, None, ALU.mult))
    ch.step(v.tensor_scalar(var, var, 1.0 / count, None, ALU.mult))


def norm_phase(nc, k, m, name, table=None):
    NB, NG = k.NB, k.NG
    with ExitStack() as ctx:
        sb = lambda n, s, d: ctx.enter_context(nc.sbuf_tensor(name + n, s, d))
        sem = lambda n: new_semaphore(nc, m, name + n)
        stats = sb("stats", [P, NB, 6], F32)
        mv = sb("mv", [P, NB, 2], F32)
        rstd = sb("rstd", [P, NB], F32)
        shift = sb("shift", [P, NB], F32)
        h = [sb(f"h{r}", [P, G4, P], F32) for r in range(4)]
        t_ps = [ctx.enter_context(nc.psum_tensor(f"{name}t_ps{b}", [P, 512], F32)) for b in range(2)]
        chain, var_ready, std_ready, shift_ready = sem("chain"), sem("var_ready"), sem("std_ready"), sem("shift_ready")
        h_ready, h_free, t_ready, t_free = sem("h_ready"), sem("h_free"), sem("t_ready"), sem("t_free")
        stored = [sem(f"stored{r}") for r in range(4)]
        with nc.Block() as block:
            @block.vector
            def _(v):
                with v.Fori(0, NG) as g:
                    for b in range(G4):
                        v.bn_stats(stats[:, ds(g * G4 + b, 1), :], m.x[:, ds(g * G4 + b, 1), :]).then_inc(chain, 1)
                ch = Chain(v, chain, NG * G4)
                ch.wait()
                mean_and_var(v, ch, stats[:], mv[:], P)
                v.sem_inc(var_ready, 1)
                v.wait_ge(std_ready, 1)
                ch.step(v.reciprocal(rstd[:], rstd[:]))
                v.scalar_tensor_tensor(shift[:], mv[:, :, 0], -1.0, rstd[:], ALU.mult, ALU.mult).then_inc(shift_ready, 1)
                v.sem_inc(h_free, 4)

                def take(at):
                    v.wait_ge(t_ready, at.n + 1)
                    v.sem_inc(h_free, 1)
                    v.tensor_copy(m.hT[:, ds(at.n * GN, GN)], t_ps[at.b][:]).then_inc(t_free, 1)
                skewed(v, NG, Item, [(0, take)])

            @block.scalar
            def _(act):
                act.wait_ge(var_ready, 1)
                act.activation(rstd[:], mv[:, :, 1], ACT.Sqrt, bias=m.eps[:]).then_inc(std_ready, 1)
                act.wait_ge(shift_ready, 1)
                if table is not None:
                    for r in range(4):
                        act.sem_inc(stored[r], 16)

                def rows(at):
                    act.wait_ge(h_free, at.n + 1)
                    if table is not None:
                        act.wait_ge(stored[at.r], 16 * (at.turn + 1))
                    for q in range(G4):
                        block_no = at.n * G4 + q
                        act.activation(h[at.r][:, q, :], m.x[:, ds(block_no, 1), :].rearrange("p a d -> p (a d)"),
                                       ACT.Relu, bias=shift[:, ds(block_no, 1)],
                                       scale=rstd[:, ds(block_no, 1)]).then_inc(h_ready, 1)
                skewed(act, NG, Item, [(0, rows)])

            @block.tensor
            def _(pe):
                pe.sem_inc(t_free, 2)

                def turn(at):
                    pe.wait_ge(h_ready, G4 * (at.n + 1))
                    pe.wait_ge(t_free, at.n + 1)
                    for q in range(G4):
                        ins = pe.transpose(t_ps[at.b][:, q * P:(q + 1) * P], h[at.r][:, q, :], m.ident[:])
                    ins.then_inc(t_ready, 1)
                skewed(pe, NG, Item, [(0, turn)])

            @block.sync
            def _(sp):
                if table is None:
                    return

                def store(at):
                    sp.wait_ge(h_ready, G4 * (at.n + 1))
                    sp.dma_start(table.rearrange("(n p) d -> p n d", p=P)[:, ds(at.n * G4, G4), :],
                                 h[at.r][:]).then_inc(stored[at.r], 16)
                skewed(sp, NG, Item, [(0, store)])
                for r in range(4):
                    sp.wait_ge(stored[r], 16 * ((NG - r + 3) // 4 + 1))


def attention_tables_phase(nc, k, m, ad):
    NG, NB = k.NG, k.NB
    with ExitStack() as ctx:
        sb = lambda n, s, d: ctx.enter_context(nc.sbuf_tensor("at_" + n, s, d))
        sem = lambda n: new_semaphore(nc, m, "at_" + n)
        ps = lambda n: ctx.enter_context(nc.psum_tensor("at_" + n, [P, 512], F32))
        wT = sb("wT", [P, P], F32)
        att = sb("att", [P, 2], F32)
        row = sb("row", [1, k.NP], F32)
        a = sb("a", [NB, P], F32)
        turned = sb("turned", [P, NB], F32)
        w_ps, s_ps, d_ps = ps("w_ps"), [ps(f"s_ps{b}") for b in range(1)], ps("d_ps")
        loaded, w_ready, rep_ready, rows_ready = sem("loaded"), sem("w_ready"), sem("rep_ready"), sem("rows_ready")
        copied, moved, chain, turned_ready = sem("copied"), sem("moved"), sem("chain"), sem("turned_ready")
        with nc.Block() as block:
            @block.sync
            def _(sp):
                sp.dma_start(wT[:], k.dram["W0T"]).then_inc(loaded, 16)
                sp.dma_start(att[:, 0:1], k.dram["att_src"].unsqueeze(1)).then_inc(loaded, 16)
                sp.dma_start(att[:, 1:2], k.dram["att_dst"].unsqueeze(1)).then_inc(loaded, 16)
                sp.wait_ge(copied, 2 * NG + 2)
                sp.dma_start(k.dram["as_dram"].unsqueeze(0), row[:]).then_inc(moved, 16)
                sp.wait_ge(moved, 16)
                sp.dma_start(a[:], k.dram["as_dram"].rearrange("(b n) -> b n", n=P)).then_inc(moved, 16)
                sp.wait_ge(moved, 32)

            @block.tensor
            def _(pe):
                pe.wait_ge(loaded, 48)
                pe.matmul(w_ps[:, 0:2], wT[:], att[:], start=True, stop=True).then_inc(w_ready, 1)
                pe.wait_ge(rep_ready, 2)
                pe.sem_inc(copied, 2)
                with pe.Fori(0, NG) as g:
                    pe.wait_ge(copied, 2 * g + 2)
                    pe.matmul(s_ps[0][:], m.ws_rep[:], m.hT[:, ds(g * GN, GN)], start=True, stop=True)
                    pe.matmul(d_ps[:], m.wd_rep[:], m.hT[:, ds(g * GN, GN)], start=True,
                              stop=True).then_inc(rows_ready, 1)
                pe.wait_ge(moved, 32)
                pe.transpose(w_ps[:, 0:NB], a[:], m.ident[0:NB, 0:NB]).then_inc(turned_ready, 1)

            @block.vector
            def _(v):
                v.wait_ge(w_ready, 1)
                v.tensor_scalar(m.ws_rep[:], m.ones[:], w_ps[:, 0:1], None, ALU.mult).then_inc(rep_ready, 1)
                v.tensor_scalar(m.wd_rep[:], m.ones[:], w_ps[:, 1:2], None, ALU.mult).then_inc(rep_ready, 1)
                with v.Fori(0, NG) as g:
                    v.wait_ge(rows_ready, g + 1)
                    v.tensor_copy(row[:, ds(g * GN, GN)], s_ps[0][0:1, :]).then_inc(copied, 1)
                    v.tensor_copy(ad[:, ds(g * GN, GN)], d_ps[:]).then_inc(copied, 1)
                v.wait_ge(turned_ready, 1)
                ch = Chain(v, chain)
                ch.step(v.tensor_copy(turned[:], w_ps[:, 0:NB]))
                ch.step(v.tensor_copy(m.as_part[:, 0, :], turned[:]))
                ch.step(v.tensor_tensor(turned[:], turned[:], m.as_part[:, 0, :], ALU.subtract))
                ch.step(v.tensor_copy(m.as_part[:, 1, :], turned[:]))
                ch.step(v.tensor_tensor(turned[:], turned[:], m.as_part[:, 1, :], ALU.subtract))
                ch.step(v.tensor_copy(m.as_part[:, 2, :], turned[:]))


def lookup_phase(nc, k, m, s_el):
    NB, T = k.NB, k.T
    L = 8
    with ExitStack() as ctx:
        sb = lambda n, s, d: ctx.enter_context(nc.sbuf_tensor("lu_" + n, s, d))
        sem = lambda n: new_semaphore(nc, m, "lu_" + n)
        place = [sb(f"place{r}", [P, L * P], BF16) for r in range(4)]
        onehot = [sb(f"onehot{b}", [P, L * P], BF16) for b in range(2)]
        picked = [sb(f"picked{b}", [P, L], F32) for b in range(2)]
        masked = sb("masked", [P, L, NB], F32)
        hi = [sb(f"hi{b}", [P, L], F32) for b in range(2)]
        block_ps = [ctx.enter_context(nc.psum_tensor(f"lu_ps{b}", [P, L, 512 // L], F32)) for b in range(2)]
        place_ready, place_free = [sem(f"place_ready{r}") for r in range(4)], sem("place_free")
        onehot_ready, onehot_free, block_ready, block_free = (sem(n) for n in ("oh_ready", "oh_free", "b_ready", "b_free"))
        picks, kept, hi_ready = sem("picks"), sem("kept"), sem("hi_ready")
        place_rows = k.dram["lo_dram"].partition_broadcast(P)
        assert NB <= 512 // L
        steps = T // L
        with nc.Block() as block:
            @block.sync
            def _(sp):
                def load(at):
                    sp.wait_ge(place_free, at.n + 1)
                    sp.dma_start(place[at.r][:], place_rows[:, ds(at.n * (L * P), L * P)]).then_inc(place_ready[at.r], 16)
                skewed(sp, steps, Item, [(0, load)])

            @block.vector
            def _(v):
                v.sem_inc(place_free, 4)
                v.sem_inc(onehot_free, 2)

                def make(at):
                    v.wait_ge(place_ready[at.r], 16 * (at.turn + 1))
                    v.wait_ge(onehot_free, at.n + 1)
                    v.tensor_scalar(onehot[at.b][:], place[at.r][:], m.part_f[:], None, ALU.is_equal).then_inc(onehot_ready, 1)
                    v.wait_ge(onehot_ready, at.n + 1)
                    v.sem_inc(place_free, 1)
                    v.tensor_copy(hi[at.b][:], m.src_hi[:, ds(at.n * L, L)]).then_inc(hi_ready, 1)

                def pick(at):
                    v.wait_ge(block_ready, at.n + 1)
                    v.sem_inc(onehot_free, 1)
                    v.wait_ge(hi_ready, at.n + 1)
                    for q in range(L):
                        v.scalar_tensor_tensor(masked[:, q, :], m.iota_f[:, 0:NB], hi[at.b][:, q:q + 1],
                                               block_ps[at.b][:, q, 0:NB], ALU.is_equal, ALU.mult,
                                               accum_out=picked[at.b][:, q:q + 1]).then_inc(picks, 1)

                def keep(at):
                    v.wait_ge(picks, L * at.n + L)
                    v.tensor_copy(s_el[:, ds(at.n * L, L)], picked[at.b][:]).then_inc(kept, 1)
                    v.wait_ge(kept, at.n + 1)
                    v.sem_inc(block_free, 1)

                skewed(v, steps, Item, [(0, make), (-1, pick), (-1, keep)])

            @block.tensor
            def _(pe):
                pe.sem_inc(block_free, 2)

                def product(at):
                    pe.wait_ge(onehot_ready, at.n + 1)
                    pe.wait_ge(block_free, at.n + 1)
                    for q in range(L):
                        for part in range(3):
                            ins = pe.matmul(block_ps[at.b][:, q, 0:NB], onehot[at.b][:, q * P:(q + 1) * P],
                                            m.as_part[:, part, :], start=(part == 0), stop=(part == 2))
                    ins.then_inc(block_ready, 1)
                skewed(pe, steps, Item, [(0, product)])


def segment_max_phase(nc, k, m, s_el):
    T = k.T
    TB = -(-T // P)
    with ExitStack() as ctx:
        sb = lambda n, s, d: ctx.enter_context(nc.sbuf_tensor("sg_" + n, s, d))
        sem = lambda n: new_semaphore(nc, m, "sg_" + n)
        here_i = sb("here_i", [P, T], I32)
        other_i = sb("other_i", [P, 2, T], I32)
        here = sb("here", [P, T], F32)
        other = sb("other", [P, 2, T], F32)
        bars = sb("bars", [P, 2, T], F32)
        run = sb("run", [P, T], F32)
        ends = sb("ends", [P, T], F32)
        most = sb("most", [P, T], F32)
        col = sb("col", [P, 2], F32)
        line = sb("line", [1, 3, P + 1], F32)
        carry = sb("carry", [P, 1], F32)
        rows = [sb(f"rows{n}", [P, P], F32) for n in range(2)]
        line_ps = ctx.enter_context(nc.psum_tensor("sg_line_ps", [P, 512], F32))
        t_ps = [ctx.enter_context(nc.psum_tensor(f"sg_t_ps{b}", [P, 512], F32)) for b in range(2)]
        loaded, chain, cols_ready, lines_ready = sem("loaded"), sem("chain"), sem("cols_ready"), sem("lines_ready")
        carry_out, carry_in, scanned, stored = sem("carry_out"), sem("carry_in"), sem("scanned"), sem("stored")
        row_loaded = [sem(f"row_loaded{b}") for b in range(2)]
        turned, taken = sem("turned"), sem("taken")
        moves = [(n, tb) for n in range(3) for tb in range(TB)]
        with nc.Block() as block:
            @block.sync
            def _(sp):
                sp.dma_start(here_i[:], k.dram["dst_el"]).then_inc(loaded, 16)
                sp.dma_start(other_i[:, 0, :], k.dram["dst_before"]).then_inc(loaded, 16)
                sp.dma_start(other_i[:, 1, :], k.dram["dst_after"]).then_inc(loaded, 16)
                sp.wait_ge(scanned, 1)
                for n, t in enumerate((s_el, most, ends)):
                    sp.dma_start(k.dram["el_dram"][n].rearrange("(p t) -> p t", p=P), t[:]).then_inc(stored, 16)
                sp.wait_ge(stored, 48)
                for i, (n, tb) in enumerate(moves):
                    nt = min(P, T - tb * P)
                    if i >= 2:
                        sp.wait_ge(turned, i - 1)
                    sp.dma_start(rows[i % 2][0:nt, :], k.dram["el_dram"][n].rearrange("(t p) -> t p", p=P)[tb * P:tb * P + nt, :]
                                 ).then_inc(row_loaded[i % 2], 16)

            @block.tensor
            def _(pe):
                for n in range(2):
                    pe.wait_ge(cols_ready, n + 1)
                    pe.matmul(line_ps[0:1, 0:P], col[:, 0:1], m.ident[:], start=True, stop=True)
                    pe.matmul(line_ps[0:1, P:2 * P], col[:, 1:2], m.ident[:], start=True, stop=True
                              ).then_inc(lines_ready, 1)
                    pe.wait_ge(carry_out, n + 1)
                    c0 = 0 if n == 0 else 1
                    pe.matmul(line_ps[:, 2 * P:2 * P + 1], line[:, 2, c0:c0 + P], m.ones[0:1, 0:1], start=True, stop=True
                              ).then_inc(carry_in, 1)
                for i, (n, tb) in enumerate(moves):
                    nt = min(P, T - tb * P)
                    pe.wait_ge(row_loaded[i % 2], 16 * (i // 2 + 1))
                    if i >= 2:
                        pe.wait_ge(taken, i - 1)
                    pe.transpose(t_ps[i % 2][:, 0:nt], rows[i % 2][0:nt, :], m.ident[0:nt, 0:nt]).then_inc(turned, 1)

            @block.vector
            def _(v):
                ch = Chain(v, chain)
                v.wait_ge(loaded, 48)
                ch.add(v.tensor_copy(here[:], here_i[:]))
                ch.step(v.tensor_copy(other[:], other_i[:]))
                for n in range(2):
                    ch.step(v.tensor_tensor(other[:, n, :], other[:, n, :], here[:], ALU.not_equal))
                    ch.step(v.tensor_scalar(bars[:, n, :], other[:, n, :], -BIG, None, ALU.mult))
                for n in range(2):
                    back = slice(None, None, -1) if n else slice(None)
                    data = (s_el, run)[n]
                    out = (run, most)[n]
                    ch.step(v.tensor_tensor_scan(out[:, back], bars[:, n, back], data[:, back], -BIG, ALU.add, ALU.max))
                    edge = 0 if n else T - 1
                    ch.add(v.tensor_copy(col[:, 0:1], out[:, edge:edge + 1]))
                    ch.add(v.tensor_reduce(col[:, 1:2], bars[:, n, :], AX.X, ALU.min))
                    ch.wait()
                    v.sem_inc(cols_ready, 1)
                    v.wait_ge(lines_ready, n + 1)
                    ch.add(v.memset(line[:, 2, :], -BIG))
                    ch.step(v.tensor_copy(line[:, 0:2, 0:P], line_ps[0:1, 0:2 * P].rearrange("p (a b) -> p a b", a=2)))
                    to = line[:, 2, P - 1::-1] if n else line[:, 2, 1:P + 1]
                    ch.step(v.tensor_tensor_scan(to, line[:, 1, P - 1::-1] if n else line[:, 1, 0:P],
                                                 line[:, 0, P - 1::-1] if n else line[:, 0, 0:P], -BIG, ALU.add, ALU.max))
                    v.sem_inc(carry_out, 1)
                    v.wait_ge(carry_in, n + 1)
                    ch.step(v.tensor_copy(carry[:], line_ps[:, 2 * P:2 * P + 1]))
                    ch.step(v.tensor_tensor_scan(out[:, back], bars[:, n, back], data[:, back], carry[:], ALU.add, ALU.max))
                ch.step(v.tensor_tensor(ends[:], most[:], other[:, 1, :], ALU.mult))
                v.sem_inc(scanned, 1)
                for i, (n, tb) in enumerate(moves):
                    nt = min(P, T - tb * P)
                    v.wait_ge(turned, i + 1)
                    v.tensor_copy(m.tl[:, n, tb * P:tb * P + nt], t_ps[i % 2][:, 0:nt]).then_inc(taken, 1)
                v.wait_ge(taken, len(moves))
class At:

    def __init__(self, k, w, i, j):
        turn = i + j // RING
        self.w, self.r, self.b = w, j % RING, j % 2
        self.chunk = turn * RING + self.r
        self.n, self.turn, self.pair = self.chunk, turn, turn * (RING // 2) + self.r // 2
        if w is not None:
            self.n = w * k.NC + self.chunk
            self.turn = w * ((k.NC - self.r + RING - 1) // RING) + turn
            self.pair = w * (k.NC // 2) + self.pair


def steps(eng, k, w, count, body):
    full = count // RING
    with eng.Fori(0, full) as i:
        for j in range(RING):
            body(lambda d, i=i, j=j: At(k, w, i, j + d))
    for j in range(count % RING):
        body(lambda d, j=j: At(k, w, full, j + d))


class Item:

    def __init__(self, turn, j):
        self.turn = turn + j // 4
        self.n, self.r, self.b = turn * 4 + j, j % 4, j % 2


def skewed(eng, count, place, slots):
    full = max(0, (count - 4) // 4)

    def ends(first, last):
        for i in range(first, last):
            for offset, body in slots:
                if 0 <= i + offset < count:
                    body(place(0, i + offset))

    ends(-2, 2)
    if full:
        with eng.Fori(0, full) as turn:
            for i in range(2, 6):
                for offset, body in slots:
                    body(place(turn, i + offset))
    ends(2 + 4 * full, count + 2)


def over_chunks(eng, k, wide, body):
    if not wide:
        steps(eng, k, None, k.NC, lambda at: body(at(0)))
    else:
        with eng.Fori(0, k.NW) as w:
            steps(eng, k, w, k.NC, lambda at: body(at(0)))


def over_chunks_lagged(eng, k, wide, first, second, per_window=None):
    def both(at):
        first(at(1))
        second(at(0))

    def run(w):
        first(At(k, w, 0, 0))
        steps(eng, k, w, k.NC - 1, both)
        second(At(k, w, 0, k.NC - 1))

    if not wide:
        run(None)
    else:
        with eng.Fori(0, k.NW) as w:
            run(w)
            per_window(w)


def both_paths(eng, m, path):
    narrow = eng.value_load(m.narrow_i[:], min_val=0, max_val=1)
    with eng.If(narrow != 0):
        path(False)
    with eng.Else():
        path(True)


def bases_of(eng, nc, k, table, chunk, w, most=None):
    if w is not None:
        return [w * CW] * C
    _, values = nc.values_load_multi_w_load_instructions(
        table[0:1, ds(chunk * C, C)], engines=(eng.engine,), min_val=0, max_val=k.N - 1 if most is None else most,
        skip_runtime_bounds_check_because="setup_phase bounds the bases, and takes this path only where the others fit")
    return values


def chunk_window(eng, k, m, at):
    if at.w is not None:
        return at.w * CW
    return eng.value_load(m.base_i[0:1, ds(at.chunk * C, 1)], min_val=0, max_val=k.N - 1)


def tile_windows(eng, nc, k, m, at):
    return [0] * C if at.w is not None else bases_of(eng, nc, k, m.rel_i, at.chunk, None, CW - W_NARROW)


def clear_bank(pe, m, bank, cols):
    pe.matmul(bank[:, 0:cols], m.zeros[:], m.zeros[:].unsqueeze(1).to_broadcast([1, cols // P, P]), start=True, stop=False)


def gather_program(pool, k, m, s, table, wide):
    def chunk_rows(at):
        n, chunk, w, b = at.n, at.chunk, at.w, at.b
        pool.wait_ge(s.rows_free[at.r], at.turn + 1)
        pool.sem_inc(s.idx_seen, 1)
        pool.tensor_copy(s.idx[at.r][:], m.src_idx[:, ds(chunk * C, C)]).then_inc(s.idx_ready, 1)
        pool.wait_ge(s.idx_ready, n + 1)
        pool.sem_inc(s.idx_seen, 1)
        for t in range(C):
            pool.indirect_dma_start(s.rows[at.r][:, t, :], None, table,
                                    bass.IndirectOffsetOnAxis(ap=s.idx[at.r][:, t:t + 1], axis=0)
                                    ).then_inc(s.gathered[at.r], 16)
    over_chunks(pool, k, wide, chunk_rows)


def edge_resources(nc, m, ctx, name):
    sb = lambda n, s, d: ctx.enter_context(nc.sbuf_tensor(name + n, s, d))
    sem = lambda n: new_semaphore(nc, m, name + n)
    s = Names()
    s.idx = [sb(f"idx{b}", [P, C], I32) for b in range(RING)]
    s.rows = [sb(f"rows{b}", [P, C, P], F32) for b in range(RING)]
    s.onehot = [sb(f"onehot{b}", [P, C * CW], F32) for b in range(2)]
    s.rows_free = [sem(f"rows_free{b}") for b in range(RING)]
    s.gathered = [sem(f"gathered{b}") for b in range(RING)]
    s.idx_ready, s.idx_seen = sem("idx_ready"), sem("idx_seen")
    s.agg_ready, s.agg_free, s.added = sem("agg_ready"), sem("agg_free"), sem("added")
    s.chain = sem("chain")
    return s, sb, sem


def onehot_of(v, m, s, chunk, w, b):
    W = W_NARROW if w is None else CW
    view = s.onehot[b][:, 0:C * W].rearrange("p (t w) -> p t w", w=W)
    nodes = (m.iota_f if w is None else m.iota_w)[:, 0:W]
    where = (m.loc_f if w is None else m.dst_f)[:, ds(chunk * C, C)]
    return view, v.tensor_tensor(view, nodes.unsqueeze(1).to_broadcast([P, C, W]),
                                 where.unsqueeze(2).to_broadcast([P, C, W]), ALU.is_equal)


def next_window(v, m, chain, w):
    v.tensor_scalar(m.iota_w[:], m.iota_w[:], float(CW), None, ALU.add).then_inc(chain, 1)
    v.wait_ge(chain, w + 1)


def attention_edges(nc, k, m, acc, ad):
    STEPS = C + 7
    with ExitStack() as ctx:
        s, sb, sem = edge_resources(nc, m, ctx, "e0_")
        masked_all = sb("masked", [P, C * CW], F32)
        ade = sb("ade", [P, C], F32)
        uv = sb("uv", [P, 2, C], F32)
        diff = sb("diff", [P, C], F32)
        pl = [sb(f"pl{b}", [P, C, 2], F32) for b in range(2)]
        weights = [sb(f"weights{b}", [P, C * 2 * CW], F32) for b in range(2)]
        agg = [ctx.enter_context(nc.psum_tensor(f"e0_agg{n}", [P, 512], F32)) for n in range(2)]
        diff_ready, p_ready, weights_ready, start = sem("diff_ready"), sem("p_ready"), sem("weights_ready"), sem("start")
        windows = sem("windows")

        with nc.Block() as block:
            @block.gpsimd
            def _(pool):
                both_paths(pool, m, lambda wide: gather_program(pool, k, m, s, k.table[0], wide))

            @block.scalar
            def _(act):
                def p_of(at):
                    n, chunk, w, b = at.n, at.chunk, at.w, at.b
                    act.wait_ge(diff_ready, n + 1)
                    act.activation(pl[b][:, :, 0], diff[:], ACT.Exp).then_inc(p_ready, 1)
                both_paths(act, m, lambda wide: over_chunks(act, k, wide, p_of))

            @block.vector
            def _(v):
                v.memset(acc[:], 0.0).then_inc(start, 1)
                v.wait_ge(start, 1)
                v.sem_inc(s.agg_free, 2)
                for free in s.rows_free:
                    v.sem_inc(free, 1)

                def path(wide):
                    W = CW if wide else W_NARROW

                    def weigh(at):
                        n, chunk, w, b = at.n, at.chunk, at.w, at.b
                        ch = Chain(v, s.chain, n * STEPS)
                        onehot, ins = onehot_of(v, m, s, chunk, w, b)
                        ch.step(ins)
                        masked = masked_all[:, 0:C * W].rearrange("p (t w) -> p t w", w=W)
                        for t, base in enumerate(bases_of(v, nc, k, m.base_i, chunk, w)):
                            ch.add(v.tensor_tensor(masked[:, t, :], onehot[:, t, :], ad[:, ds(base, W)], ALU.mult))
                        ch.wait()
                        ch.step(v.tensor_reduce(ade[:], masked, AX.X, ALU.add))
                        ch.step(v.tensor_tensor(uv[:], m.tl[:, 0:2, ds(chunk * C, C)],
                                                ade[:].unsqueeze(1).to_broadcast([P, 2, C]), ALU.add))
                        ch.step(v.scalar_tensor_tensor(uv[:], uv[:], SLOPE, uv[:], ALU.mult, ALU.max))
                        v.tensor_tensor(diff[:], uv[:, 0, :], uv[:, 1, :], ALU.subtract).then_inc(diff_ready, 1)
                        ch.add(v.tensor_copy(pl[b][:, :, 1], m.tl[:, 2, ds(chunk * C, C)]))
                        v.wait_ge(p_ready, n + 1)
                        ch.wait()
                        both = weights[b][:, 0:C * 2 * W].rearrange("p (t kw) -> p t kw", kw=2 * W)
                        for kind in range(2):
                            ch.add(v.tensor_tensor(both[:, :, kind * W:(kind + 1) * W], onehot,
                                                   pl[b][:, :, kind:kind + 1].to_broadcast([P, C, W]), ALU.mult))
                        ch.close(STEPS)
                        v.sem_inc(weights_ready, 1)

                    def add(at):
                        window = acc[:, :, ds(chunk_window(v, k, m, at), CW)]
                        v.wait_ge(s.agg_ready, at.n + 1)
                        v.tensor_tensor(window, window, agg[at.b][:, 0:3 * CW].rearrange("p (a w) -> p a w", w=CW),
                                        ALU.add).then_inc(s.added, 1)
                        v.wait_ge(s.added, at.n + 1)
                        v.sem_inc(s.agg_free, 1)
                        v.sem_inc(s.rows_free[at.r], 1)

                    over_chunks_lagged(v, k, wide, weigh, add, lambda w: next_window(v, m, windows, w))
                both_paths(v, m, path)

            @block.tensor
            def _(pe):
                def path(wide):
                    W = CW if wide else W_NARROW

                    def sums(at):
                        rel = tile_windows(pe, nc, k, m, at)
                        pe.wait_ge(s.agg_free, at.n + 1)
                        clear_bank(pe, m, agg[at.b], 3 * CW)
                        pe.wait_ge(s.gathered[at.r], (at.turn + 1) * 16 * C)
                        pe.wait_ge(weights_ready, at.n + 1)
                        to = agg[at.b][:, 0:3 * CW].rearrange("p (a w) -> p a w", w=CW)
                        both = weights[at.b][:, 0:C * 2 * W].rearrange("p (t a w) -> p t a w", a=2, w=W)
                        for t in range(C):
                            cols = ds(rel[t], W)
                            pe.matmul(to[:, 0, cols], s.rows[at.r][:, t, :], both[:, t, 0, :], start=False, stop=False)
                            ins = pe.matmul(to[:, 1:3, cols], m.ones[:], both[:, t, :, :], start=False, stop=(t == C - 1))
                        ins.then_inc(s.agg_ready, 1)
                    over_chunks(pe, k, wide, sums)
                both_paths(pe, m, path)


def reset_windows(v, m, chain):
    v.tensor_copy(m.iota_w[:], m.iota_f[:]).then_inc(chain, 1)
    v.wait_ge(chain, 1)


def sum_edges(nc, k, m, name, acc, table):
    with ExitStack() as ctx:
        s, sb, sem = edge_resources(nc, m, ctx, name)
        agg = [ctx.enter_context(nc.psum_tensor(f"{name}agg{n}", [P, 512], F32)) for n in range(2)]
        onehot_ready, start, windows = sem("onehot_ready"), sem("start"), sem("windows")

        with nc.Block() as block:
            @block.gpsimd
            def _(pool):
                both_paths(pool, m, lambda wide: gather_program(pool, k, m, s, table, wide))

            @block.vector
            def _(v):
                reset_windows(v, m, start)
                v.memset(acc[:], 0.0).then_inc(start, 1)
                v.wait_ge(start, 2)
                v.sem_inc(s.agg_free, 2)
                for free in s.rows_free:
                    v.sem_inc(free, 1)

                def path(wide):
                    def make(at):
                        onehot_of(v, m, s, at.chunk, at.w, at.b)[1].then_inc(onehot_ready, 1)

                    def add(at):
                        window = acc[:, ds(chunk_window(v, k, m, at), CW)]
                        v.wait_ge(s.agg_ready, at.n + 1)
                        v.tensor_tensor(window, window, agg[at.b][:, 0:CW], ALU.add).then_inc(s.added, 1)
                        v.wait_ge(s.added, at.n + 1)
                        v.sem_inc(s.agg_free, 1)
                        v.sem_inc(s.rows_free[at.r], 1)

                    over_chunks_lagged(v, k, wide, make, add, lambda w: next_window(v, m, windows, w))
                both_paths(v, m, path)

            @block.tensor
            def _(pe):
                def path(wide):
                    W = CW if wide else W_NARROW

                    def sums(at):
                        rel = tile_windows(pe, nc, k, m, at)
                        pe.wait_ge(s.agg_free, at.n + 1)
                        clear_bank(pe, m, agg[at.b], CW)
                        pe.wait_ge(s.gathered[at.r], (at.turn + 1) * 16 * C)
                        pe.wait_ge(onehot_ready, at.n + 1)
                        for t in range(C):
                            ins = pe.matmul(agg[at.b][:, ds(rel[t], W)], s.rows[at.r][:, t, :],
                                            s.onehot[at.b][:, t * W:(t + 1) * W], start=False, stop=(t == C - 1))
                        ins.then_inc(s.agg_ready, 1)
                    over_chunks(pe, k, wide, sums)
                both_paths(pe, m, path)


def filter_edges(nc, k, m, acc):
    E = C * P
    SETUP = 14
    with ExitStack() as ctx:
        s, sb, sem = edge_resources(nc, m, ctx, "e2_")
        two = lambda n: [sb(f"{n}{b}", [P, E], F32) for b in range(2)]
        w1, w2, b1 = sb("w1", [P, P], F32), sb("w2", [P, P], F32), sb("b1", [P, 1], F32)
        b2, b2_part, b2_sum = sb("b2", [3, P], F32), sb("b2_part", [3, P], BF16), sb("b2_sum", [3, P], F32)
        b2_parts, ones_b = sb("b2_parts", [3, G4, P], BF16), sb("ones_b", [3, P], BF16)
        edge, low1, low2, filt1, message = two("edge"), two("low1_"), two("low2_"), two("filt1_"), two("message")
        top1, top2 = sb("top1", [P, E], F32), sb("top2", [P, E], F32)
        z1 = ctx.enter_context(nc.psum_tensor("e2_z1", [P, E], F32))
        z2 = ctx.enter_context(nc.psum_tensor("e2_z2", [P, E], F32))
        agg = [ctx.enter_context(nc.psum_tensor(f"e2_agg{n}", [P, 512], F32)) for n in range(2)]
        consts, start, windows = sem("consts"), sem("start"), sem("windows")
        edge_ready = [sem(f"edge_ready{b}") for b in range(2)]
        z1_ready, z2_ready, z1_free, z2_free = sem("z1_ready"), sem("z2_ready"), sem("z1_free"), sem("z2_free")
        low1_ready, low2_ready, low1_free, low2_free = (sem(n) for n in ("low1_ready", "low2_ready", "low1_free", "low2_free"))
        low1_chain, low2_chain, top1_ready, top2_ready = (sem(n) for n in ("low1_chain", "low2_chain", "top1_ready", "top2_ready"))
        filt1_ready, soft_ready, message_ready, onehot_ready = (sem(n) for n in ("filt1_ready", "soft_ready", "message_ready", "onehot_ready"))

        def walk(eng, wide, slots, per_window=None):
            if not wide:
                skewed(eng, k.NC, lambda turn, j: At(k, None, turn, j), slots)
            else:
                with eng.Fori(0, k.NW) as w:
                    skewed(eng, k.NC, lambda turn, j: At(k, w, turn, j), slots)
                    if per_window:
                        per_window(w)

        with nc.Block() as block:
            @block.sync
            def _(sp):
                for t, d in ((w1, k.dram["We1T"]), (w2, k.dram["We2T"]), (b1, k.dram["b_e1"].unsqueeze(1)),
                             (b2, k.dram["b_e2"].partition_broadcast(3))):
                    sp.dma_start(t[:], d).then_inc(consts, 16)

                def load(at):
                    sp.wait_ge(z1_ready, at.n + 1)
                    sp.dma_start(edge[at.b][:], k.dram["edge_T"][:, ds(at.chunk * E, E)]).then_inc(edge_ready[at.b], 16)
                both_paths(sp, m, lambda wide: over_chunks(sp, k, wide, load))
                sp.wait_ge(consts, 64)

            @block.gpsimd
            def _(pool):
                both_paths(pool, m, lambda wide: gather_program(pool, k, m, s, k.table[2], wide))

            @block.tensor
            def _(pe):
                pe.wait_ge(start, SETUP)
                pe.sem_inc(z1_ready, 2)

                def path(wide):
                    W = CW if wide else W_NARROW

                    def first_product(at):
                        pe.wait_ge(edge_ready[at.b], 16 * (at.pair + 1))
                        pe.wait_ge(z1_free, at.n + 1)
                        for half in range(2):
                            cols = slice(half * 512, (half + 1) * 512)
                            ins = pe.matmul(z1[:, cols], w1[:], edge[at.b][:, cols], start=True, stop=True)
                        ins.then_inc(z1_ready, 1)

                    def second_product(at):
                        pe.wait_ge(z2_free, at.n + 1)
                        for half in range(2):
                            pe.matmul(z2[:, half * 512:(half + 1) * 512], ones_b[:], b2_parts[:].rearrange("p g d -> p (g d)"),
                                      start=True, stop=False)
                        pe.wait_ge(filt1_ready, at.n + 1)
                        for t in range(C):
                            cols = slice(t * P, (t + 1) * P)
                            ins = pe.matmul(z2[:, cols], filt1[at.b][:, cols], w2[:], start=False, stop=(t % G4 == G4 - 1))
                        ins.then_inc(z2_ready, 1)

                    def sums(at):
                        rel = tile_windows(pe, nc, k, m, at)
                        pe.wait_ge(s.agg_free, at.n + 1)
                        clear_bank(pe, m, agg[at.b], CW)
                        pe.wait_ge(onehot_ready, at.n + 1)
                        pe.wait_ge(message_ready, at.n + 1)
                        for t in range(C):
                            ins = pe.matmul(agg[at.b][:, ds(rel[t], W)], message[at.b][:, t * P:(t + 1) * P],
                                            s.onehot[at.b][:, t * W:(t + 1) * W], start=False, stop=(t == C - 1))
                        ins.then_inc(s.agg_ready, 1)
                    walk(pe, wide, [(0, second_product), (2, first_product), (-1, sums)])
                both_paths(pe, m, path)

            @block.scalar
            def _(act):
                act.preload_act_table_set("natural_log_exp_and_others")
                act.wait_ge(consts, 64)

                def low_part(at, z, low, bias, chain, ready):
                    act.activation(low[:], z[:], ACT.Abs, bias=bias).then_inc(chain, 1)
                    act.wait_ge(chain, 2 * at.n + 1)
                    act.activation(low[:], low[:], ACT.Exp, scale=-1.0).then_inc(chain, 1)
                    act.wait_ge(chain, 2 * at.n + 2)
                    act.activation(low[:], low[:], ACT.Ln, bias=1.0).then_inc(ready, 1)

                def first_low(at):
                    act.wait_ge(z1_ready, at.n + 3)
                    act.wait_ge(low1_free, at.n + 1)
                    low_part(at, z1, low1[at.b], b1[:], low1_chain, low1_ready)

                def second_low(at):
                    act.wait_ge(z2_ready, at.n + 1)
                    act.wait_ge(low2_free, at.n + 1)
                    low_part(at, z2, low2[at.b], 0.0, low2_chain, low2_ready)
                both_paths(act, m, lambda wide: walk(act, wide, [(1, first_low), (0, second_low)]))

            @block.vector
            def _(v):
                v.wait_ge(consts, 64)
                reset_windows(v, m, start)
                ch = Chain(v, start, 1)
                ch.add(v.memset(acc[:], 0.0))
                ch.step(v.memset(b2_sum[:], 0.0))
                ch.add(v.memset(ones_b[:], 1.0))
                for n in range(3):
                    ch.step(v.tensor_copy(b2_part[:], b2[:]))
                    ch.add(v.scalar_tensor_tensor(b2_sum[:], b2_part[:], m.ident[0:3, n:n + 1], b2_sum[:], ALU.mult, ALU.add))
                    ch.step(v.tensor_tensor(b2[:], b2[:], b2_part[:], ALU.subtract))
                ch.step(v.tensor_copy(b2_parts[:], b2_sum[:].unsqueeze(1).to_broadcast([3, G4, P])))
                ch.close(SETUP - 1)
                for free, count in ((s.agg_free, 2), (z1_free, 1), (z2_free, 1), (low1_free, 2), (low2_free, 2)):
                    v.sem_inc(free, count)
                for free in s.rows_free:
                    v.sem_inc(free, 1)

                def path(wide):
                    def first_filter(at):
                        v.wait_ge(low1_chain, 2 * at.n + 1)
                        v.tensor_scalar(top1[:], z1[:], b1[:], 0.0, ALU.add, ALU.max).then_inc(top1_ready, 1)
                        v.wait_ge(top1_ready, at.n + 1)
                        v.sem_inc(z1_free, 1)
                        v.wait_ge(low1_ready, at.n + 1)
                        v.scalar_tensor_tensor(filt1[at.b][:], low1[at.b][:], -LOG2, top1[:], ALU.add, ALU.add).then_inc(filt1_ready, 1)
                        v.wait_ge(filt1_ready, at.n + 1)
                        v.sem_inc(low1_free, 1)

                    def second_top(at):
                        v.wait_ge(low2_chain, 2 * at.n + 1)
                        v.tensor_scalar(top2[:], z2[:], 0.0, None, ALU.max).then_inc(top2_ready, 1)
                        v.wait_ge(top2_ready, at.n + 1)
                        v.sem_inc(z2_free, 1)

                    def to_messages(at):
                        v.wait_ge(low2_ready, at.n + 1)
                        v.tensor_tensor(top2[:], low2[at.b][:], top2[:], ALU.add).then_inc(soft_ready, 1)
                        v.wait_ge(soft_ready, at.n + 1)
                        v.sem_inc(low2_free, 1)
                        v.wait_ge(s.gathered[at.r], (at.turn + 1) * 16 * C)
                        v.scalar_tensor_tensor(message[at.b][:], top2[:], -LOG2, s.rows[at.r][:].rearrange("p t d -> p (t d)"),
                                               ALU.add, ALU.mult).then_inc(message_ready, 1)
                        v.wait_ge(message_ready, at.n + 1)
                        v.sem_inc(s.rows_free[at.r], 1)

                    def make(at):
                        onehot_of(v, m, s, at.chunk, at.w, at.b)[1].then_inc(onehot_ready, 1)

                    def add(at):
                        window = acc[:, ds(chunk_window(v, k, m, at), CW)]
                        v.wait_ge(s.agg_ready, at.n + 1)
                        v.tensor_tensor(window, window, agg[at.b][:, 0:CW], ALU.add).then_inc(s.added, 1)
                        v.wait_ge(s.added, at.n + 1)
                        v.sem_inc(s.agg_free, 1)
                    walk(v, wide, [(-1, to_messages), (1, first_filter), (0, second_top), (-2, add), (0, make)],
                         lambda w: next_window(v, m, windows, w))
                both_paths(v, m, path)


def softmax_edges(nc, k, m, acc, shift_row, top, den):
    SHIFTS = 10
    with ExitStack() as ctx:
        s, sb, sem = edge_resources(nc, m, ctx, "e1_")
        ps = lambda n: ctx.enter_context(nc.psum_tensor("e1_" + n, [P, 512], F32))
        key = [sb(f"key{b}", [P, HEADS, CW], F32) for b in range(2)]
        rows_T = sb("rows_T", [P, C, P], F32)
        masked = [sb(f"masked{b}", [P, 512], F32) for b in range(2)]
        weights = [sb(f"weights{b}", [P, 512], F32) for b in range(2)]
        logit = sb("logit", [P, C, HEADS], F32)
        member = sb("member", [P, C], F32)
        p = sb("p", [P, C, HEADS], F32)
        p_sum = sb("p_sum", [P, HEADS], F32)
        col_max = sb("col_max", [P, HEADS], F32)
        new_max = sb("new_max", [HEADS, 1], F32)
        diag = sb("diag", [HEADS, HEADS], F32)
        top_all = [sb(f"top_all{b}", [P, HEADS], F32) for b in range(2)]
        fade = [sb(f"fade{b}", [P, HEADS], F32) for b in range(2)]
        t_ps = [ps(f"t{n}") for n in range(2)]
        x_ps = [ps(f"x{n}") for n in range(2)]
        agg = [ps(f"agg{n}") for n in range(2)]
        max_ps = ps("max")
        key_ready, key_free = [sem(f"key_ready{b}") for b in range(2)], sem("key_free")
        turned, rows_T_ready, rows_T_free = sem("turned"), sem("rows_T_ready"), sem("rows_T_free")
        x_ready, x_free, logits_chain = sem("x_ready"), sem("x_free"), sem("logits_chain")
        col_ready, col_turned, diag_ready, top_ready = sem("col_ready"), sem("col_turned"), sem("diag_ready"), sem("top_ready")
        shifted, p_ready, weights_ready, weights_read = sem("shifted"), sem("p_ready"), sem("weights_ready"), sem("weights_read")
        start, windows = sem("start"), sem("windows")

        def shape(wide):
            W = CW if wide else W_NARROW
            return W, 512 // (HEADS * W), C * HEADS * W // 512

        def walk(eng, begin, work, finish):
            begin(At(k, None, 0, 0))
            work(At(k, None, 0, 0), None, At(k, None, 0, 1))
            steps(eng, k, None, k.NC - 2, lambda at: work(at(1), at(0), at(2)))
            work(At(k, None, 0, k.NC - 1), At(k, None, 0, k.NC - 2), None)
            finish(At(k, None, 0, k.NC - 1))

        with nc.Block() as block:
            @block.sync
            def _(sp):
                def load(at):
                    n, chunk, w, b = at.n, at.chunk, at.w, at.b
                    sp.wait_ge(key_free, n + 1)
                    sp.dma_start(key[b][:], k.dram["key_dram"][:, :, ds(chunk_window(sp, k, m, at), CW)]).then_inc(key_ready[b], 16)
                both_paths(sp, m, lambda wide: over_chunks(sp, k, wide, load))

            @block.gpsimd
            def _(pool):
                both_paths(pool, m, lambda wide: gather_program(pool, k, m, s, k.table[1], wide))

            @block.scalar
            def _(act):
                def take_rows(at):
                    act.wait_ge(rows_T_free, at.n + 1)
                    for half in range(2):
                        act.wait_ge(turned, 2 * at.n + half + 1)
                        act.activation(rows_T[:, half * 4:half * 4 + 4, :].rearrange("p t d -> p (t d)"), t_ps[half][:],
                                       ACT.Copy).then_inc(rows_T_ready, 1)

                def exponents(at):
                    act.wait_ge(shifted, at.n + 1)
                    act.activation(p[:], p[:], ACT.Exp).then_inc(p_ready, 1)
                    act.activation(fade[at.b][:], fade[at.b][:], ACT.Exp).then_inc(p_ready, 1)

                def work(now, last, following):
                    if following:
                        take_rows(following)
                    exponents(now)

                def both(at):
                    take_rows(at)
                    exponents(at)
                both_paths(act, m, lambda wide: over_chunks(act, k, wide, both) if wide
                           else walk(act, take_rows, work, lambda at: None))

            @block.tensor
            def _(pe):
                def path(wide):
                    W, G, per = shape(wide)
                    windows_of = lambda at: tile_windows(pe, nc, k, m, at)

                    def turn_rows(at):
                        pe.wait_ge(s.gathered[at.r], (at.turn + 1) * 16 * C)
                        for half in range(2):
                            for q in range(4):
                                ins = pe.transpose(t_ps[half][:, q * P:(q + 1) * P], s.rows[at.r][:, half * 4 + q, :], m.ident[:])
                            ins.then_inc(turned, 1)

                    def products(at, rel):
                        pe.wait_ge(key_ready[at.b], 16 * (at.pair + 1))
                        for g in range(per):
                            pe.wait_ge(x_free, at.n * per + g + 1)
                            to = x_ps[(at.b * per + g) % 2]
                            for q in range(G):
                                t = g * G + q
                                if t % 4 == 0 or q == 0:
                                    pe.wait_ge(rows_T_ready, 2 * at.n + t // 4 + 1)
                                ins = pe.matmul(to[:, q * HEADS * W:(q + 1) * HEADS * W], rows_T[:, t, :],
                                                key[at.b][:, :, ds(rel[t], W)], start=True, stop=True)
                            ins.then_inc(x_ready, 1)

                    def turn_maximum(at):
                        pe.wait_ge(col_ready, at.n + 1)
                        pe.transpose(max_ps[0:HEADS, 0:P], col_max[:], m.ident[:]).then_inc(col_turned, 1)

                    def spread_maximum(at):
                        pe.wait_ge(diag_ready, at.n + 1)
                        pe.matmul(max_ps[:, P:P + HEADS], m.ones[0:HEADS, :], diag[:], start=True, stop=True).then_inc(top_ready, 1)

                    def open_sums(at):
                        pe.wait_ge(s.agg_free, at.n + 1)
                        clear_bank(pe, m, agg[at.b], HEADS * CW)

                    def sums(at, rel):
                        to = agg[at.b][:].rearrange("p (h w) -> p h w", w=CW)
                        for g in range(per):
                            pe.wait_ge(weights_ready, at.n * per + g + 1)
                            part = weights[(at.b * per + g) % 2]
                            for q in range(G):
                                t = g * G + q
                                ins = pe.matmul(to[:, :, ds(rel[t], W)], s.rows[at.r][:, t, :],
                                                part[:, q * HEADS * W:(q + 1) * HEADS * W], start=False, stop=(t == C - 1))
                            if g < per - 1:
                                ins.then_inc(weights_read, 1)
                        ins.then_inc(s.agg_ready, 1)

                    def begin(at):
                        turn_rows(at)
                        products(at, windows_of(at))

                    def work(now, last, following):
                        if following:
                            turn_rows(following)
                            rel = windows_of(following)
                        if last:
                            last_rel = windows_of(last)
                            open_sums(last)
                        turn_maximum(now)
                        if last:
                            sums(last, last_rel)
                        spread_maximum(now)
                        if following:
                            products(following, rel)

                    def finish(at):
                        open_sums(at)
                        sums(at, windows_of(at))

                    def one(at):
                        begin(at)
                        work(at, None, None)
                        finish(at)

                    if wide:
                        over_chunks(pe, k, wide, one)
                    else:
                        walk(pe, begin, work, finish)
                both_paths(pe, m, path)

            @block.vector
            def _(v):
                reset_windows(v, m, start)
                for t, value in ((acc, 0.0), (shift_row, START), (top, START), (den, 0.0), (top_all[1], START)):
                    v.memset(t[:], value).then_inc(start, 1)
                v.wait_ge(start, 6)
                for free in s.rows_free:
                    v.sem_inc(free, 1)
                for free, count in ((key_free, 2), (rows_T_free, 1), (x_free, 2), (s.agg_free, 2), (weights_read, 2)):
                    v.sem_inc(free, count)

                def path(wide):
                    W, G, per = shape(wide)
                    LOGITS = 2 + 2 * per + 2 + wide

                    def make(at):
                        ch = Chain(v, logits_chain, at.n * LOGITS)
                        onehot, ins = onehot_of(v, m, s, at.chunk, at.w, at.b)
                        if wide:
                            ch.step(ins)
                            ch.step(v.tensor_reduce(member[:], onehot, AX.X, ALU.add))
                            ch.step(v.tensor_scalar(member[:], member[:], -1.0, BIG, ALU.add, ALU.mult))
                        else:
                            ch.add(ins)
                            ch.step(v.tensor_scalar(member[:], m.loc_f[:, ds(at.chunk * C, C)], float(W), -BIG, ALU.is_ge, ALU.mult))

                    def logits(at):
                        ch = Chain(v, logits_chain, at.n * LOGITS + 2 + wide)
                        onehot = s.onehot[at.b][:, 0:C * W].rearrange("p (t w) -> p t w", w=W)
                        for g in range(per):
                            v.wait_ge(x_ready, at.n * per + g + 1)
                            if g == per - 1:
                                v.sem_inc(rows_T_free, 1)
                                v.sem_inc(key_free, 1)
                            t, of = slice(g * G, (g + 1) * G), (at.b * per + g) % 2
                            part = masked[of][:].rearrange("p (t h w) -> p t h w", h=HEADS, w=W)
                            ch.step(v.tensor_tensor(part, x_ps[of][:].rearrange("p (t h w) -> p t h w", h=HEADS, w=W),
                                                    onehot[:, t, :].unsqueeze(2).to_broadcast([P, G, HEADS, W]), ALU.mult))
                            v.sem_inc(x_free, 1)
                            ch.add(v.tensor_reduce(logit[:, t, :], part, AX.X, ALU.add))
                        ch.wait()
                        ch.step(v.tensor_tensor(logit[:], logit[:], over(member[:], [P, C, HEADS]), ALU.add))
                        ch.step(v.tensor_reduce(col_max[:], logit[:].rearrange("p t h -> p h t"), AX.X, ALU.max))
                        ch.close(LOGITS - 2 - wide)
                        v.sem_inc(col_ready, 1)

                    def maximum(at):
                        ch = Chain(v, s.chain, at.n * SHIFTS)
                        v.wait_ge(col_turned, at.n + 1)
                        ch.step(v.tensor_reduce(new_max[:], max_ps[0:HEADS, 0:P], AX.X, ALU.max))
                        ch.step(v.tensor_tensor(top[:], top[:], new_max[:], ALU.max))
                        ch.step(v.tensor_scalar(diag[:], m.ident[0:HEADS, 0:HEADS], top[:], None, ALU.mult))
                        v.sem_inc(diag_ready, 1)

                    def shift(at):
                        ch = Chain(v, s.chain, at.n * SHIFTS + 3)
                        span = shift_row[:, ds(chunk_window(v, k, m, at), CW)]
                        ch.add(v.tensor_scalar(span, m.ones[0:HEADS, 0:1].to_broadcast([HEADS, CW]), top[:], None, ALU.mult))
                        v.wait_ge(top_ready, at.n + 1)
                        ch.step(v.tensor_copy(top_all[at.b][:], max_ps[:, P:P + HEADS]))
                        ch.add(v.tensor_tensor(p[:], logit[:], top_all[at.b][:].unsqueeze(1).to_broadcast([P, C, HEADS]), ALU.subtract))
                        ch.step(v.tensor_tensor(fade[at.b][:], top_all[1 - at.b][:], top_all[at.b][:], ALU.subtract))
                        v.sem_inc(shifted, 1)

                    def build(at, g):
                        v.wait_ge(weights_read, at.n * per + g + 1)
                        onehot = s.onehot[at.b][:, 0:C * W].rearrange("p (t w) -> p t w", w=W)
                        out = weights[(at.b * per + g) % 2][:].rearrange("p (t h w) -> p t h w", h=HEADS, w=W)
                        t = slice(g * G, (g + 1) * G)
                        v.tensor_tensor(out, onehot[:, t, :].unsqueeze(2).to_broadcast([P, G, HEADS, W]),
                                        p[:, t, :].unsqueeze(3).to_broadcast([P, G, HEADS, W]), ALU.mult).then_inc(weights_ready, 1)

                    def total(at):
                        ch = Chain(v, s.chain, at.n * SHIFTS + 7)
                        ch.add(v.tensor_reduce(p_sum[:], p[:].rearrange("p t h -> p h t"), AX.X, ALU.add))
                        ch.step(v.tensor_tensor(den[:], den[:], fade[at.b][:], ALU.mult))
                        ch.step(v.tensor_tensor(den[:], den[:], p_sum[:], ALU.add))
                        ch.close(SHIFTS - 7)

                    def add(at):
                        base = chunk_window(v, k, m, at)
                        window, faded = acc[:, :, ds(base, CW)], acc[:, :, ds(base, W)]
                        v.tensor_tensor(faded, faded, over(fade[at.b][:], [P, HEADS, W]), ALU.mult).then_inc(s.added, 1)
                        v.wait_ge(s.agg_ready, at.n + 1)
                        v.wait_ge(s.added, 2 * at.n + 1)
                        v.tensor_tensor(window, window, agg[at.b][:].rearrange("p (h w) -> p h w", w=CW), ALU.add).then_inc(s.added, 1)
                        v.wait_ge(s.added, 2 * at.n + 2)
                        v.sem_inc(s.agg_free, 1)
                        v.sem_inc(weights_read, 1)
                        v.sem_inc(s.rows_free[at.r], 1)

                    def work(now, last, following):
                        logits(now)
                        maximum(now)
                        if following:
                            make(following)
                        shift(now)
                        if last:
                            add(last)
                        v.wait_ge(p_ready, 2 * now.n + 2)
                        for g in range(per):
                            build(now, g)
                        total(now)

                    def one(at):
                        make(at)
                        work(at, None, None)
                        add(at)

                    if wide:
                        with v.Fori(0, k.NW) as w:
                            steps(v, k, w, k.NC, lambda at: one(at(0)))
                            next_window(v, m, windows, w)
                    else:
                        assert per == 1
                        walk(v, make, work, add)
                both_paths(v, m, path)
class Node:

    def __init__(self, nc, ctx, k, m, name):
        self.nc, self.ctx, self.k, self.m, self.name = nc, ctx, k, m, name

    def sb(self, n, shape, dt=F32):
        return self.ctx.enter_context(self.nc.sbuf_tensor(self.name + n, shape, dt))

    def ps(self, n):
        return self.ctx.enter_context(self.nc.psum_tensor(self.name + n, [P, 512], F32))

    def sem(self, n):
        return new_semaphore(self.nc, self.m, self.name + n)


def load_nodes(nc, k, m, name, x_from, hT_from=None):
    with ExitStack() as ctx:
        loaded = new_semaphore(nc, m, name + "loaded")
        with nc.Block() as block:
            @block.sync
            def _(sp):
                sp.dma_start(m.x[:], x_from.rearrange("(n p) d -> p n d", p=P)).then_inc(loaded, 16)
                if hT_from is not None:
                    sp.dma_start(m.hT[:], hT_from).then_inc(loaded, 16)
                sp.wait_ge(loaded, 32 if hT_from is not None else 16)


def keep_nodes(nc, k, m, name, x_to, hT_to=None):
    with ExitStack() as ctx:
        kept = new_semaphore(nc, m, name + "kept")
        with nc.Block() as block:
            @block.sync
            def _(sp):
                sp.dma_start(x_to.rearrange("(n p) d -> p n d", p=P), m.x[:]).then_inc(kept, 16)
                if hT_to is not None:
                    sp.dma_start(hT_to, m.hT[:]).then_inc(kept, 16)
                sp.wait_ge(kept, 32 if hT_to is not None else 16)


def add_to_x(v, m, g, y, bias, ch):
    x = m.x[:, ds(g * G4, G4), :]
    ch.step(v.tensor_tensor(x, x, y[:].rearrange("p (b d) -> p b d", b=G4), ALU.add))
    ch.step(v.tensor_tensor(x, x, bias[:].unsqueeze(1).to_broadcast([P, G4, P]), ALU.add))


def attention_output(nc, k, m, acc, ad):
    STEPS = 16
    with ExitStack() as ctx:
        a = Node(nc, ctx, k, m, "o0_")
        w, bias = a.sb("w", [P, P]), a.sb("bias", [P, P])
        e = a.sb("e", [P, 2, GN])
        top, whole, mixed = a.sb("top", [P, GN]), a.sb("whole", [P, GN]), a.sb("mixed", [P, GN])
        own_ps, y_ps = a.ps("own"), a.ps("y")
        loaded, own_ready, own_free, chain = a.sem("loaded"), a.sem("own_ready"), a.sem("own_free"), a.sem("chain")
        shifted, factors, mixed_ready, y_ready = a.sem("shifted"), a.sem("factors"), a.sem("mixed_ready"), a.sem("y_ready")
        with nc.Block() as block:
            @block.sync
            def _(sp):
                sp.dma_start(w[:], k.dram["W0"]).then_inc(loaded, 16)
                sp.dma_start(bias[:], k.dram["bias0"].partition_broadcast(P)).then_inc(loaded, 16)
                sp.wait_ge(loaded, 32)

            @block.tensor
            def _(pe):
                pe.wait_ge(loaded, 32)
                with pe.Fori(0, k.NG) as g:
                    pe.wait_ge(own_free, g + 1)
                    pe.matmul(own_ps[:], m.ws_rep[:], m.hT[:, ds(g * GN, GN)], start=True, stop=True).then_inc(own_ready, 1)
                    pe.wait_ge(mixed_ready, g + 1)
                    for b in range(G4):
                        ins = pe.matmul(y_ps[:, b * P:(b + 1) * P], mixed[:, b * P:(b + 1) * P], w[:], start=True, stop=True)
                    ins.then_inc(y_ready, 1)

            @block.scalar
            def _(act):
                with act.Fori(0, k.NG) as g:
                    act.wait_ge(shifted, g + 1)
                    act.activation(e[:], e[:], ACT.Exp).then_inc(factors, 1)

            @block.vector
            def _(v):
                v.wait_ge(loaded, 32)
                v.sem_inc(own_free, 1)
                with v.Fori(0, k.NG) as g:
                    ch = Chain(v, chain, g * STEPS)
                    at = ds(g * GN, GN)
                    v.wait_ge(own_ready, g + 1)
                    ch.add(v.tensor_tensor(e[:, 1, :], own_ps[:], ad[:, at], ALU.add))
                    ch.step(v.tensor_scalar(e[:, 0, :], acc[:, 1, at], 0.0, -BIG, ALU.is_equal, ALU.mult))
                    v.sem_inc(own_free, 1)
                    ch.step(v.tensor_tensor(e[:, 0, :], e[:, 0, :], acc[:, 2, at], ALU.add))
                    ch.step(v.tensor_tensor(e[:, 0, :], e[:, 0, :], ad[:, at], ALU.add))
                    ch.step(v.scalar_tensor_tensor(e[:], e[:], SLOPE, e[:], ALU.mult, ALU.max))
                    ch.step(v.tensor_tensor(top[:], e[:, 0, :], e[:, 1, :], ALU.max))
                    ch.step(v.tensor_tensor(e[:], e[:], top[:].unsqueeze(1).to_broadcast([P, 2, GN]), ALU.subtract))
                    v.sem_inc(shifted, 1)
                    v.wait_ge(factors, g + 1)
                    ch.add(v.tensor_tensor(mixed[:], acc[:, 0, at], e[:, 0, :], ALU.mult))
                    ch.add(v.tensor_tensor(top[:], m.hT[:, at], e[:, 1, :], ALU.mult))
                    ch.step(v.tensor_tensor(whole[:], acc[:, 1, at], e[:, 0, :], ALU.mult))
                    ch.add(v.tensor_tensor(mixed[:], mixed[:], top[:], ALU.add))
                    ch.step(v.tensor_tensor(whole[:], whole[:], e[:, 1, :], ALU.add))
                    ch.step(v.reciprocal(whole[:], whole[:]))
                    ch.step(v.tensor_tensor(mixed[:], mixed[:], whole[:], ALU.mult))
                    v.sem_inc(mixed_ready, 1)
                    v.wait_ge(y_ready, g + 1)
                    add_to_x(v, m, g, y_ps, bias, ch)
                    ch.close(STEPS)


def key_phase(nc, k, m):
    SCALE = float(P) ** -0.5
    with ExitStack() as ctx:
        a = Node(nc, ctx, k, m, "key_")
        wq, wk, pair = a.sb("wq", [P, HEADS, P]), a.sb("wk", [P, HEADS, P]), a.sb("pair", [P, HEADS, P])
        out = [a.sb(f"out{b}", [P, HEADS, GN]) for b in range(2)]
        pair_ps = a.ps("pair_ps")
        key_ps = [a.ps(f"key_ps{h}") for h in range(HEADS)]
        loaded, pair_ready, pair_kept = a.sem("loaded"), a.sem("pair_ready"), a.sem("pair_kept")
        key_ready, taken, stored = a.sem("key_ready"), a.sem("taken"), [a.sem(f"stored{b}") for b in range(2)]
        with nc.Block() as block:
            @block.sync
            def _(sp):
                sp.dma_start(wq[:], k.dram["Wq"]).then_inc(loaded, 16)
                sp.dma_start(wk[:], k.dram["Wk"]).then_inc(loaded, 16)
                for b in range(2):
                    sp.sem_inc(stored[b], 16)

                def store(at):
                    sp.wait_ge(taken, HEADS * at.n + 2 * HEADS)
                    sp.dma_start(k.dram["key_dram"][:, :, ds(at.n * GN, GN)], out[at.b][:]).then_inc(stored[at.b], 16)
                skewed(sp, k.NG, Item, [(0, store)])
                for b in range(2):
                    sp.wait_ge(stored[b], 16 * ((k.NG - b + 1) // 2 + 1))

            @block.tensor
            def _(pe):
                pe.wait_ge(loaded, 32)
                for h in range(HEADS):
                    ins = pe.matmul(pair_ps[:, h * P:(h + 1) * P], wk[:, h, :], wq[:, h, :], start=True, stop=True)
                ins.then_inc(pair_ready, 1)
                pe.wait_ge(pair_kept, 1)
                pe.sem_inc(taken, HEADS)
                with pe.Fori(0, k.NG) as g:
                    pe.wait_ge(taken, HEADS * (g + 1))
                    for h in range(HEADS):
                        pe.matmul(key_ps[h][:], pair[:, h, :], m.hT[:, ds(g * GN, GN)], start=True, stop=True
                                  ).then_inc(key_ready, 1)

            @block.vector
            def _(v):
                v.wait_ge(pair_ready, 1)
                v.tensor_scalar(pair[:].rearrange("p h d -> p (h d)"), pair_ps[:], SCALE, None, ALU.mult).then_inc(pair_kept, 1)

                def take(at):
                    v.wait_ge(stored[at.b], 16 * (at.turn * 2 + at.r // 2 + 1))
                    for h in range(2):
                        v.wait_ge(key_ready, HEADS * at.n + h + 1)
                        v.tensor_copy(out[at.b][:, h, :], key_ps[h][:]).then_inc(taken, 1)
                skewed(v, k.NG, Item, [(0, take)])

            @block.scalar
            def _(act):
                def take(at):
                    act.wait_ge(stored[at.b], 16 * (at.turn * 2 + at.r // 2 + 1))
                    for h in range(2, 4):
                        act.wait_ge(key_ready, HEADS * at.n + h + 1)
                        act.activation(out[at.b][:, h, :], key_ps[h][:], ACT.Copy).then_inc(taken, 1)
                skewed(act, k.NG, Item, [(0, take)])


def factor_phase(nc, k, m, shift_row, top, den, factor):
    with ExitStack() as ctx:
        a = Node(nc, ctx, k, m, "fa_")
        negative, inverse = a.sb("negative", [HEADS, 1]), a.sb("inverse", [P, HEADS])
        f_ps, den_ps = a.ps("f_ps"), a.ps("den_ps")
        den_ready, top_ready, row_ready, cols_ready, taken, chain = (
            a.sem(n) for n in ("den_ready", "top_ready", "row_ready", "cols_ready", "taken", "chain"))
        static = a.sb("static", [HEADS, GN])
        with nc.Block() as block:
            @block.tensor
            def _(pe):
                pe.matmul(den_ps[:, 0:HEADS], m.ones[:], den[:], start=True, stop=True).then_inc(den_ready, 1)
                with pe.Fori(0, k.NG) as g:
                    pe.wait_ge(row_ready, g + 1)
                    for b in range(G4):
                        ins = pe.matmul(f_ps[:, b * HEADS:(b + 1) * HEADS], static[:, b * P:(b + 1) * P],
                                        m.ident[0:HEADS, 0:HEADS], start=True, stop=True)
                    ins.then_inc(cols_ready, 1)

            @block.scalar
            def _(act):
                act.wait_ge(top_ready, 1)
                act.sem_inc(taken, 1)
                with act.Fori(0, k.NG) as g:
                    act.wait_ge(taken, g + 1)
                    act.activation(static[:], shift_row[:, ds(g * GN, GN)], ACT.Exp, bias=negative[:]).then_inc(row_ready, 1)

            @block.vector
            def _(v):
                v.tensor_scalar(negative[:], top[:], -1.0, None, ALU.mult).then_inc(top_ready, 1)
                v.wait_ge(den_ready, 1)
                v.reciprocal(inverse[:], den_ps[:, 0:HEADS]).then_inc(chain, 1)
                v.wait_ge(chain, 1)
                with v.Fori(0, k.NG) as g:
                    v.wait_ge(cols_ready, g + 1)
                    v.tensor_tensor(factor[:, ds(g * G4, G4), :], f_ps[:, 0:G4 * HEADS].rearrange("p (b h) -> p b h", h=HEADS),
                                    inverse[:].unsqueeze(1).to_broadcast([P, G4, HEADS]), ALU.mult).then_inc(taken, 1)


def softmax_output(nc, k, m, acc, factor):
    F = HEADS * P
    STATS, AFFINE, OUT = 14, 2, 2
    with ExitStack() as ctx:
        a = Node(nc, ctx, k, m, "o1_")
        wq, wr, wo = a.sb("wq", [P, HEADS, P]), a.sb("wr", [P, HEADS, P]), a.sb("wo", [P, HEADS, P])
        bo, gamma, beta, br = a.sb("bo", [P, P]), a.sb("gamma", [P, F]), a.sb("beta", [P, F]), a.sb("br", [P, HEADS])
        br_rep, wro = a.sb("br_rep", [P, HEADS, P]), a.sb("wro", [P, P])
        two = lambda n, shape: [a.sb(f"{n}{b}", shape) for b in range(2)]
        sums, heads, gate, joined_T = two("sums", [P, HEADS, P]), two("heads", [P, F]), two("gate", [P, F]), two("joined_T", [P, F])
        h_T = [a.sb(f"h_T{r}", [P, P]) for r in range(4)]
        h_rows, fac, rstd = two("h_rows", [P, P]), two("fac", [P, HEADS]), two("rstd", [P, 1])
        stats, mv = two("stats", [P, 1, 6]), two("mv", [P, 1, 2])
        heads_ps, h_ps, t_ps, y_ps = ([a.ps(f"{n}{b}") for b in range(2)] for n in ("heads_ps", "h_ps", "t_ps", "y_ps"))
        loaded, setup, setup_ps = a.sem("loaded"), a.sem("setup"), a.sem("setup_ps")
        copied, sums_ready, sums_read, h_rows_ready = (a.sem(n) for n in ("copied", "sums_ready", "sums_read", "h_rows_ready"))
        stats_chain, affine_chain, mult_chain, out_chain, rstd_chain, gate_chain = (
            a.sem(n) for n in ("stats_chain", "affine_chain", "mult_chain", "out_chain", "rstd_chain", "gate_chain"))
        rstd_ready, gate_ready, turned, joined_T_ready, y_ready, y_free = (
            a.sem(n) for n in ("rstd_ready", "gate_ready", "turned", "joined_T_ready", "y_ready", "y_free"))
        parts = ((wq, k.dram["WqT"]), (wr, k.dram["Wr"]), (wo, k.dram["WoT"]), (br, k.dram["br"]),
                 (bo, k.dram["bo"].partition_broadcast(P)), (gamma, k.dram["gamma"].partition_broadcast(P)),
                 (beta, k.dram["beta"].partition_broadcast(P)))
        with nc.Block() as block:
            @block.sync
            def _(sp):
                for t, d in parts:
                    sp.dma_start(t[:], d).then_inc(loaded, 16)
                sp.wait_ge(loaded, 16 * len(parts))

            @block.scalar
            def _(act):
                act.preload_act_table_set("natural_log_exp_and_others")

                def take_in(at):
                    n, r, b = at.n, at.r, at.b
                    act.wait_ge(sums_ready, n + 1)
                    act.wait_ge(y_ready, n + 1)
                    act.activation(sums[b][:], acc[:, :, ds(n * P, P)], ACT.Copy).then_inc(copied, 1)
                    act.activation(h_T[r][:], m.hT[:, ds(n * P, P)], ACT.Copy).then_inc(copied, 1)

                def spread(at):
                    n, r, b = at.n, at.r, at.b
                    act.wait_ge(stats_chain, STATS * n + STATS)
                    act.activation(rstd[b][:], mv[b][:, :, 1], ACT.Ln, bias=m.eps[:]).then_inc(rstd_chain, 1)
                    act.wait_ge(rstd_chain, n + 1)
                    act.activation(rstd[b][:], rstd[b][:], ACT.Exp, scale=-0.5).then_inc(rstd_ready, 1)

                def sigmoid(at):
                    n, r, b = at.n, at.r, at.b
                    act.wait_ge(affine_chain, AFFINE * n + AFFINE)
                    g = gate[b]
                    act.activation(g[:], heads[b][:], ACT.Exp, scale=-1.0).then_inc(gate_chain, 1)
                    act.wait_ge(gate_chain, 2 * n + 1)
                    act.activation(g[:], g[:], ACT.Ln, bias=1.0).then_inc(gate_chain, 1)
                    act.wait_ge(gate_chain, 2 * n + 2)
                    act.activation(g[:], g[:], ACT.Exp, scale=-1.0).then_inc(gate_ready, 1)

                def take_turned(at):
                    n, r, b = at.n, at.r, at.b
                    act.wait_ge(turned, n + 1)
                    act.wait_ge(y_ready, n + 3)
                    act.activation(joined_T[b][:], t_ps[b][:], ACT.Copy).then_inc(joined_T_ready, 1)

                skewed(act, k.NB, Item, [(-1, take_turned), (2, take_in), (1, spread), (0, sigmoid)])

            @block.tensor
            def _(pe):
                pe.wait_ge(setup, 1)
                for h in range(HEADS):
                    pe.matmul(y_ps[0][:, 0:P], wr[:, h, :], wo[:, h, :], start=(h == 0), stop=(h == HEADS - 1))
                for h in range(HEADS):
                    ins = pe.matmul(y_ps[1][:, 0:P], br_rep[:, h, :], wo[:, h, :], start=(h == 0), stop=(h == HEADS - 1))
                ins.then_inc(setup_ps, 1)
                pe.wait_ge(setup, 3)
                pe.sem_inc(sums_ready, 2)
                pe.sem_inc(y_ready, 4)

                def products(at):
                    n, r, b = at.n, at.r, at.b
                    pe.wait_ge(copied, 2 * n + 2)
                    pe.wait_ge(sums_read, n + 1)
                    pe.transpose(h_ps[b][:, 0:P], h_T[r][:], m.ident[:])
                    for h in range(HEADS):
                        ins = pe.matmul(heads_ps[b][:, h * P:(h + 1) * P], sums[b][:, h, :], wq[:, h, :],
                                        start=True, stop=True)
                    ins.then_inc(sums_ready, 1)

                def turn(at):
                    n, r, b = at.n, at.r, at.b
                    pe.wait_ge(mult_chain, n + 1)
                    for h in range(HEADS):
                        ins = pe.transpose(t_ps[b][:, h * P:(h + 1) * P], gate[b][:, h * P:(h + 1) * P], m.ident[:])
                    ins.then_inc(turned, 1)

                def output(at):
                    n, r, b = at.n, at.r, at.b
                    pe.wait_ge(y_free, n + 1)
                    pe.matmul(y_ps[b][:, 0:P], h_T[r][:], wro[:], start=True, stop=False)
                    pe.wait_ge(joined_T_ready, n + 1)
                    for h in range(HEADS):
                        ins = pe.matmul(y_ps[b][:, 0:P], joined_T[b][:, h * P:(h + 1) * P], wo[:, h, :],
                                        start=False, stop=(h == HEADS - 1))
                    ins.then_inc(y_ready, 1)

                skewed(pe, k.NB, Item, [(-1, output), (2, products), (0, turn)])

            @block.vector
            def _(v):
                v.wait_ge(loaded, 16 * len(parts))
                v.tensor_copy(br_rep[:], over(br[:], [P, HEADS, P])).then_inc(setup, 1)
                v.wait_ge(setup_ps, 1)
                v.tensor_copy(wro[:], y_ps[0][:, 0:P]).then_inc(setup, 1)
                v.tensor_tensor(bo[:], bo[:], y_ps[1][:, 0:P], ALU.add).then_inc(setup, 1)
                v.wait_ge(setup, 3)
                v.sem_inc(sums_read, 2)
                v.sem_inc(y_free, 2)

                def join(at):
                    n, r, b = at.n, at.r, at.b
                    ch = Chain(v, stats_chain, n * STATS)
                    ch.add(v.tensor_copy(fac[b][:], factor[:, ds(n, 1), :].rearrange("p a h -> p (a h)")))
                    v.wait_ge(sums_ready, n + 3)
                    ch.step(v.tensor_copy(h_rows[b][:], h_ps[b][:, 0:P]))
                    for h in range(HEADS):
                        cols = slice(h * P, (h + 1) * P)
                        ch.add(v.scalar_tensor_tensor(heads[b][:, cols], heads_ps[b][:, cols], fac[b][:, h:h + 1], h_rows[b][:],
                                                      ALU.mult, ALU.add))
                    ch.wait()
                    v.sem_inc(sums_read, 1)
                    ch.step(v.bn_stats(stats[b][:, 0, :], heads[b][:]))
                    mean_and_var(v, ch, stats[b][:], mv[b][:], F)
                    ch.close(STATS)

                def affine(at):
                    n, r, b = at.n, at.r, at.b
                    ch = Chain(v, affine_chain, n * AFFINE)
                    ch.step(v.scalar_tensor_tensor(heads[b][:], heads[b][:], mv[b][:, 0, 0:1], gamma[:], ALU.subtract, ALU.mult))
                    v.wait_ge(rstd_ready, n + 1)
                    ch.step(v.scalar_tensor_tensor(heads[b][:], heads[b][:], rstd[b][:], beta[:], ALU.mult, ALU.add))
                    ch.close(AFFINE)

                def gated(at):
                    n, r, b = at.n, at.r, at.b
                    v.wait_ge(gate_ready, n + 1)
                    v.tensor_tensor(gate[b][:], gate[b][:], heads[b][:], ALU.mult).then_inc(mult_chain, 1)
                    v.wait_ge(mult_chain, n + 1)

                def to_x(at):
                    n, r, b = at.n, at.r, at.b
                    ch = Chain(v, out_chain, n * OUT)
                    x = m.x[:, ds(n, 1), :].rearrange("p a d -> p (a d)")
                    ch.step(v.tensor_tensor(x, x, bo[:], ALU.add))
                    v.wait_ge(y_ready, n + 5)
                    ch.step(v.tensor_tensor(x, x, y_ps[b][:, 0:P], ALU.add))
                    ch.close(OUT)
                    v.sem_inc(y_free, 1)

                skewed(v, k.NB, Item, [(1, join), (1, affine), (-1, to_x), (0, gated)])


def product_phase(nc, k, m):
    with ExitStack() as ctx:
        a = Node(nc, ctx, k, m, "pr_")
        w, bias = a.sb("w", [P, P]), a.sb("bias", [P, P])
        h_T, out, y_ps = a.sb("h_T", [P, GN]), a.sb("out", [P, G4, P]), a.ps("y")
        loaded, copied, y_ready, y_free, out_ready, stored = (
            a.sem(n) for n in ("loaded", "copied", "y_ready", "y_free", "out_ready", "stored"))
        with nc.Block() as block:
            @block.sync
            def _(sp):
                sp.dma_start(w[:], k.dram["WnT"]).then_inc(loaded, 16)
                sp.dma_start(bias[:], k.dram["b_node"].partition_broadcast(P)).then_inc(loaded, 16)
                sp.sem_inc(stored, 16)
                with sp.Fori(0, k.NG) as g:
                    sp.wait_ge(out_ready, g + 1)
                    sp.dma_start(k.table[2].rearrange("(n p) d -> p n d", p=P)[:, ds(g * G4, G4), :], out[:]).then_inc(stored, 16)
                sp.wait_ge(stored, 16 * (k.NG + 1))

            @block.scalar
            def _(act):
                act.sem_inc(y_ready, 1)
                with act.Fori(0, k.NG) as g:
                    act.wait_ge(y_ready, g + 1)
                    act.activation(h_T[:], m.hT[:, ds(g * GN, GN)], ACT.Copy).then_inc(copied, 1)

            @block.tensor
            def _(pe):
                pe.wait_ge(loaded, 32)
                pe.sem_inc(y_free, 1)
                with pe.Fori(0, k.NG) as g:
                    pe.wait_ge(copied, g + 1)
                    pe.wait_ge(y_free, g + 1)
                    for b in range(G4):
                        ins = pe.matmul(y_ps[:, b * P:(b + 1) * P], h_T[:, b * P:(b + 1) * P], w[:], start=True, stop=True)
                    ins.then_inc(y_ready, 1)

            @block.vector
            def _(v):
                v.wait_ge(loaded, 32)
                with v.Fori(0, k.NG) as g:
                    v.wait_ge(y_ready, g + 2)
                    v.wait_ge(stored, 16 * (g + 1))
                    v.tensor_tensor(out[:], y_ps[:].rearrange("p (b d) -> p b d", b=G4),
                                    bias[:].unsqueeze(1).to_broadcast([P, G4, P]), ALU.add).then_inc(out_ready, 1)
                    v.wait_ge(out_ready, g + 1)
                    v.sem_inc(y_free, 1)


def filter_output(nc, k, m, acc):
    STEPS = 5
    with ExitStack() as ctx:
        a = Node(nc, ctx, k, m, "o2_")
        w1, w2, b1, bias = a.sb("w1", [P, P]), a.sb("w2", [P, P]), a.sb("b1", [P, 1]), a.sb("bias", [P, P])
        low, top = a.sb("low", [P, GN]), a.sb("top", [P, GN])
        z_ps, y_ps = a.ps("z"), a.ps("y")
        loaded, z_ready, z_free, low_ready, chain, act_chain, mid_ready, y_ready = (
            a.sem(n) for n in ("loaded", "z_ready", "z_free", "low_ready", "chain", "act_chain", "mid_ready", "y_ready"))
        with nc.Block() as block:
            @block.sync
            def _(sp):
                for t, d in ((w1, k.dram["Wf1T"]), (w2, k.dram["Wf2T"]), (b1, k.dram["b_fc1"].unsqueeze(1)), (bias, k.dram["b_fc2"].partition_broadcast(P))):
                    sp.dma_start(t[:], d).then_inc(loaded, 16)
                sp.wait_ge(loaded, 64)

            @block.tensor
            def _(pe):
                pe.wait_ge(loaded, 64)
                with pe.Fori(0, k.NG) as g:
                    pe.wait_ge(z_free, g + 1)
                    pe.matmul(z_ps[:], w1[:], acc[:, ds(g * GN, GN)], start=True, stop=True).then_inc(z_ready, 1)
                    pe.wait_ge(mid_ready, g + 1)
                    for b in range(G4):
                        ins = pe.matmul(y_ps[:, b * P:(b + 1) * P], low[:, b * P:(b + 1) * P], w2[:], start=True, stop=True)
                    ins.then_inc(y_ready, 1)

            @block.scalar
            def _(act):
                act.preload_act_table_set("natural_log_exp_and_others")
                act.wait_ge(loaded, 64)
                act.sem_inc(y_ready, 1)
                with act.Fori(0, k.NG) as g:
                    ch = Chain(act, act_chain, g * 2)
                    act.wait_ge(z_ready, g + 1)
                    act.wait_ge(y_ready, g + 1)
                    ch.step(act.activation(low[:], z_ps[:], ACT.Abs, bias=b1[:]))
                    ch.step(act.activation(low[:], low[:], ACT.Exp, scale=-1.0))
                    act.activation(low[:], low[:], ACT.Ln, bias=1.0).then_inc(low_ready, 1)

            @block.vector
            def _(v):
                v.wait_ge(loaded, 64)
                v.sem_inc(z_free, 1)
                with v.Fori(0, k.NG) as g:
                    ch = Chain(v, chain, g * 4)
                    v.wait_ge(act_chain, 2 * g + 1)
                    ch.add(v.tensor_scalar(top[:], z_ps[:], b1[:], 0.0, ALU.add, ALU.max))
                    v.wait_ge(low_ready, g + 1)
                    ch.wait()
                    v.sem_inc(z_free, 1)
                    ch.step(v.scalar_tensor_tensor(low[:], low[:], -LOG2, top[:], ALU.add, ALU.add))
                    v.sem_inc(mid_ready, 1)
                    v.wait_ge(y_ready, g + 2)
                    add_to_x(v, m, g, y_ps, bias, ch)
                    ch.close(4)


def perceptron_output(nc, k, m, acc):
    with ExitStack() as ctx:
        a = Node(nc, ctx, k, m, "o3_")
        w1, w2, b1, bias = a.sb("w1", [P, 2 * P]), a.sb("w2", [P, 2, P]), a.sb("b1", [P, 2]), a.sb("bias", [P, P])
        mid = [a.sb(f"mid{b}", [P, 2, GN]) for b in range(2)]
        z_ps, y_ps = [[a.ps(f"z{b}_{half}") for half in range(2)] for b in range(2)], [a.ps(f"y{b}") for b in range(2)]
        loaded, sum_ready, z_ready, mid_ready, chain, y_ready, y_free = (
            a.sem(n) for n in ("loaded", "sum_ready", "z_ready", "mid_ready", "chain", "y_ready", "y_free"))
        with nc.Block() as block:
            @block.sync
            def _(sp):
                for t, d in ((w1, k.dram["W1"]), (w2, k.dram["W2"]), (b1, k.dram["b1"]), (bias, k.dram["b2"].partition_broadcast(P))):
                    sp.dma_start(t[:], d).then_inc(loaded, 16)
                sp.wait_ge(loaded, 64)

            @block.tensor
            def _(pe):
                pe.wait_ge(loaded, 64)
                pe.sem_inc(mid_ready, 4)

                def first(at):
                    pe.wait_ge(sum_ready, at.n + 1)
                    pe.wait_ge(mid_ready, 2 * at.n + 2)
                    for half in range(2):
                        pe.matmul(z_ps[at.b][half][:], w1[:, half * P:(half + 1) * P], acc[:, ds(at.n * GN, GN)],
                                  start=True, stop=True).then_inc(z_ready, 1)

                def second(at):
                    pe.wait_ge(y_free, at.n + 1)
                    pe.wait_ge(mid_ready, 2 * at.n + 6)
                    for q in range(G4):
                        cols = slice(q * P, (q + 1) * P)
                        for half in range(2):
                            ins = pe.matmul(y_ps[at.b][:, cols], mid[at.b][:, half, cols], w2[:, half, :],
                                            start=(half == 0), stop=(half == 1))
                    ins.then_inc(y_ready, 1)
                skewed(pe, k.NG, Item, [(1, first), (0, second)])

            @block.scalar
            def _(act):
                act.wait_ge(loaded, 64)
                act.sem_inc(y_ready, 2)

                def relu(at):
                    act.wait_ge(y_ready, at.n + 1)
                    for half in range(2):
                        act.wait_ge(z_ready, 2 * at.n + half + 1)
                        act.activation(mid[at.b][:, half, :], z_ps[at.b][half][:], ACT.Relu, bias=b1[:, half:half + 1]
                                       ).then_inc(mid_ready, 1)
                skewed(act, k.NG, Item, [(0, relu)])

            @block.vector
            def _(v):
                v.wait_ge(loaded, 64)
                v.sem_inc(y_free, 2)

                def join(at):
                    cols = ds(at.n * GN, GN)
                    v.tensor_tensor(acc[:, cols], acc[:, cols], m.hT[:, cols], ALU.add).then_inc(sum_ready, 1)

                def to_x(at):
                    ch = Chain(v, chain, at.n * 2)
                    v.wait_ge(y_ready, at.n + 3)
                    add_to_x(v, m, at.n, y_ps[at.b], bias, ch)
                    ch.close(2)
                    v.sem_inc(y_free, 1)
                skewed(v, k.NG, Item, [(1, join), (-1, to_x)])
def build(nc, k):
    k.NC, k.NB, k.NG, k.NW = k.T // C, k.NP // P, k.NP // GN, k.NP // CW
    m = Names()
    m.semaphores = []

    def sbuf(ctx, name, shape, dt=F32):
        return ctx.enter_context(nc.sbuf_tensor("m_" + name, shape, dt))

    def nodes(ctx, layer):
        m.x = sbuf(ctx, f"x_{layer}", [P, k.NB, P])
        m.hT = sbuf(ctx, f"hT_{layer}", [P, k.NP])

    with ExitStack() as whole:
        m.src_idx = sbuf(whole, "src_idx", [P, k.T], I32)
        m.dst_f = sbuf(whole, "dst_f", [P, k.T])
        m.loc_f = sbuf(whole, "loc_f", [P, k.T])
        m.base_i = sbuf(whole, "base_i", [1, k.T], I32)
        m.rel_i = sbuf(whole, "rel_i", [1, k.T], I32)
        m.narrow_i = sbuf(whole, "narrow_i", [1, 1], I32)
        m.iota_i = sbuf(whole, "iota_i", [P, P], I32)
        m.iota_f = sbuf(whole, "iota_f", [P, P])
        m.iota_w = sbuf(whole, "iota_w", [P, P])
        m.part_i = sbuf(whole, "part_i", [P, 1], I32)
        m.part_f = sbuf(whole, "part_f", [P, 1])
        m.ident = sbuf(whole, "ident", [P, P])
        m.ones = sbuf(whole, "ones", [P, P])
        m.eps = sbuf(whole, "eps", [P, 1])
        m.zeros = sbuf(whole, "zeros", [1, P], BF16)
        with ExitStack() as layer:
            m.tl = sbuf(layer, "tl", [P, 3, k.T])
            m.ws_rep, m.wd_rep = sbuf(layer, "ws_rep", [P, P]), sbuf(layer, "wd_rep", [P, P])
            ad = sbuf(layer, "ad", [P, k.NP])
            with ExitStack() as first:
                m.src_hi, m.as_part = sbuf(first, "src_hi", [P, k.T]), sbuf(first, "as_part", [P, 3, k.NB], BF16)
                with ExitStack() as su:
                    m.base_f = sbuf(su, "base_f", [P, k.T])
                    setup_phase(nc, k, m)
                with ExitStack() as ctx:
                    nodes(ctx, 0)
                    load_nodes(nc, k, m, "l0_", k.dram["x_in"])
                    norm_phase(nc, k, m, "n0_", k.table[0])
                    attention_tables_phase(nc, k, m, ad)
                    keep_nodes(nc, k, m, "k0_", k.dram["x_dram"], k.dram["hT_dram"])
                s_el = sbuf(first, "s_el", [P, k.T])
                lookup_phase(nc, k, m, s_el)
                segment_max_phase(nc, k, m, s_el)
            clear_semaphores(nc, m)
            acc = sbuf(layer, "acc0", [P, 3, k.NP])
            attention_edges(nc, k, m, acc, ad)
            with ExitStack() as ctx:
                nodes(ctx, 1)
                load_nodes(nc, k, m, "l1_", k.dram["x_dram"], k.dram["hT_dram"])
                attention_output(nc, k, m, acc, ad)
                norm_phase(nc, k, m, "n1_", k.table[1])
                key_phase(nc, k, m)
                keep_nodes(nc, k, m, "k1_", k.dram["x_dram"], k.dram["hT_dram"])
        clear_semaphores(nc, m)
        with ExitStack() as layer:
            acc = sbuf(layer, "acc1", [P, HEADS, k.NP])
            factor = sbuf(layer, "factor", [P, k.NB, HEADS])
            with ExitStack() as ctx:
                top = sbuf(ctx, "top", [HEADS, 1])
                den = sbuf(ctx, "den", [P, HEADS])
                shift_row = sbuf(ctx, "shift_row", [HEADS, k.NP])
                softmax_edges(nc, k, m, acc, shift_row, top, den)
                factor_phase(nc, k, m, shift_row, top, den, factor)
            with ExitStack() as ctx:
                nodes(ctx, 2)
                load_nodes(nc, k, m, "l2_", k.dram["x_dram"], k.dram["hT_dram"])
                softmax_output(nc, k, m, acc, factor)
                norm_phase(nc, k, m, "n2_")
                product_phase(nc, k, m)
                keep_nodes(nc, k, m, "k2_", k.dram["x_dram"])
        clear_semaphores(nc, m)
        nodes(whole, 3)
        with ExitStack() as layer:
            acc = sbuf(layer, "acc2", [P, k.NP])
            filter_edges(nc, k, m, acc)
            load_nodes(nc, k, m, "l3_", k.dram["x_dram"])
            filter_output(nc, k, m, acc)
            norm_phase(nc, k, m, "n3_", k.table[3])
        clear_semaphores(nc, m)
        with ExitStack() as layer:
            acc = sbuf(layer, "acc3", [P, k.NP])
            sum_edges(nc, k, m, "e3_", acc, k.table[3])
            perceptron_output(nc, k, m, acc)
            keep_nodes(nc, k, m, "k4_", k.dram["out"])
        clear_semaphores(nc, m)


def kernel(**inputs):
    from concourse import bacc
    from concourse.bass_utils import run_bass_kernel_spmd

    a = {name: np.asarray(value) for name, value in inputs.items()}
    N, E = a["x"].shape[0], a["src"].shape[0]
    NP, T = padded(N, E)
    EP = T * P
    x = np.zeros((NP, P), np.float32)
    x[:N] = a["x"]
    src = np.zeros(EP, np.int32)
    src[:E] = a["src"]
    dst = np.full(EP, NP, np.int32)
    dst[:E] = a["dst"]
    edge = np.zeros((P, EP), np.float32)
    edge[:, :E] = a["edge_attr_128"].T
    heads = lambda w: w.reshape(HEADS, P, P)
    arrays = {
        "x_in": x, "src_tl": src.reshape(T, P).T, "dst_tl": dst.reshape(T, P).T,
        "dst_first": dst.reshape(T, P)[:, 0], "dst_last": dst.reshape(T, P)[:, -1],
        "src_el": src.reshape(P, T), "src_el_t": src.reshape(P, T).T.reshape(P, T), "dst_el": dst.reshape(P, T),
        "dst_before": np.concatenate([np.full(1, -1, np.int32), dst[:-1]]).reshape(P, T),
        "dst_after": np.concatenate([dst[1:], np.full(1, NP + 1, np.int32)]).reshape(P, T),
        "edge_T": edge,
        "W0": a["L0_gnn_W"], "W0T": a["L0_gnn_W"].T, "att_src": a["L0_gnn_att_src"], "att_dst": a["L0_gnn_att_dst"],
        "bias0": a["L0_gnn_bias"],
        "Wq": a["L1_gnn_Wq"].transpose(1, 0, 2), "Wk": a["L1_gnn_Wk"].transpose(1, 0, 2),
        "WqT": a["L1_gnn_Wq"].transpose(2, 0, 1), "gamma": a["L1_gnn_gamma"], "beta": a["L1_gnn_beta"],
        "Wr": a["L1_gnn_Wr"].reshape(HEADS, P, P).transpose(1, 0, 2), "br": a["L1_gnn_br"].reshape(HEADS, P).T,
        "WoT": a["L1_gnn_Wo"].T.reshape(HEADS, P, P).transpose(1, 0, 2), "bo": a["L1_gnn_bo"],
        "WnT": a["L2_gnn_W_node"].T, "b_node": a["L2_gnn_b_node"], "We1T": a["L2_gnn_W_e1"].T, "b_e1": a["L2_gnn_b_e1"],
        "We2T": a["L2_gnn_W_e2"].T, "b_e2": a["L2_gnn_b_e2"], "Wf1T": a["L2_gnn_W_fc1"].T, "b_fc1": a["L2_gnn_b_fc1"],
        "Wf2T": a["L2_gnn_W_fc2"].T, "b_fc2": a["L2_gnn_b_fc2"],
        "W1": a["L3_gnn_W1"], "b1": a["L3_gnn_b1"].reshape(2, P).T, "W2": a["L3_gnn_W2"].reshape(2, P, P).transpose(1, 0, 2),
        "b2": a["L3_gnn_b2"],
    }
    arrays = {name: np.ascontiguousarray(value) for name, value in arrays.items()}
    nc = bacc.Bacc("TRN2", target_bir_lowering=False, num_devices=1)
    k = Names()
    k.N, k.NP, k.T = N, NP, T
    k.dram = {name: nc.dram_tensor(name, value.shape, mybir.dt.from_np(value.dtype), kind="ExternalInput").ap()
              for name, value in arrays.items()}
    k.dram["out"] = nc.dram_tensor("out", (NP, P), F32, kind="ExternalOutput").ap()
    scratch = {"x_dram": ((NP, P), F32), "hT_dram": ((P, NP), F32), "key_dram": ((P, HEADS, NP), F32), "as_dram": ((NP,), F32),
               "el_dram": ((3, EP), F32), "lo_dram": ((EP,), BF16)}
    for name, (shape, dt) in scratch.items():
        k.dram[name] = nc.dram_tensor(name, shape, dt).ap()
    k.table = [nc.dram_tensor(f"table{n}", (NP, P), F32).ap() for n in range(4)]
    build(nc, k)
    result = run_bass_kernel_spmd(nc, [arrays], core_ids=[0])
    return result.results[0]["out"][:N]
```
